# Optimizing a Trainium2 kernel written in Bass

```python
import numpy as np
import jax
import jax.numpy as jnp

def _softmax(x, axis=-1):
    return jax.nn.softmax(x, axis=axis)

def _gelu(x):
    return jax.nn.gelu(x, approximate=True)

def _silu(x):
    return jax.nn.silu(x)

def _sigmoid(x):
    return jax.nn.sigmoid(x)

def _layernorm(x, axis=-1, eps=1e-05):
    m = jnp.mean(x, axis=axis, keepdims=True)
    v = jnp.var(x, axis=axis, keepdims=True)
    return (x - m) / jnp.sqrt(v + eps)

def _scatter_add(tgt, idx, src, axis=0):
    return tgt.at[idx].add(src)

def _segment_sum(src, seg, n):
    return jax.ops.segment_sum(src, seg, n)
kernel_name = 'mk_decoder_preln_d1_seqx_r4_fce3a7'

def setup_inputs(seed: int=0):
    np.random.seed(seed)
    _w = jnp.asarray

    def _rec_inputs():
        import jax
        import jax.numpy as jnp
        _rk = jax.random.key(seed)
        x = 4.136e-05 + 0.9999 * jax.random.normal(jax.random.fold_in(_rk, 1), (4, 512, 512), jnp.float32)
        _lenS = 512 - jax.random.randint(jax.random.fold_in(_rk, 7), (4,), 0, max(1, 512 // 4) + 1, jnp.int32)
        _lenS2 = 512 - jax.random.randint(jax.random.fold_in(_rk, 8), (4,), 0, max(1, 512 // 4) + 1, jnp.int32)
        _ctx_1024P = jax.random.normal(jax.random.fold_in(_rk, 11), (4, 16, 256), jnp.float32)
        _ctx_1024c = jax.random.dirichlet(jax.random.fold_in(_rk, 511), 0.3 * jnp.ones((16,), jnp.float32), (4, 512))
        _ctx_1024t = jnp.einsum('bsk,bkd->bsd', _ctx_1024c, _ctx_1024P)
        _ctx_1024t = _ctx_1024t * jax.lax.rsqrt(jnp.mean(jnp.square(_ctx_1024t)) + 1e-12) * 0.953939
        ctx_1024 = -0.000292821 + 1.00034 * (_ctx_1024t + 0.3 * jax.random.normal(jax.random.fold_in(_rk, 611), (4, 512, 256), jnp.float32))
        return (x, ctx_1024)
    x, ctx_1024 = _rec_inputs()

    def _L0_attn_setup():
        import jax, jax.numpy as jnp
        import numpy as np
        HEADS = 16
        DIM_HEAD = 128
        SCALE = 16.0
        EPS = 1e-05

        def _layernorm(x, g):
            mu = jnp.mean(x, axis=-1, keepdims=True)
            var = jnp.mean((x - mu) ** 2, axis=-1, keepdims=True)
            return (x - mu) * jax.lax.rsqrt(var + EPS) * g

        def _l2norm(t):
            return t * jax.lax.rsqrt(jnp.sum(t * t, axis=-1, keepdims=True) + 1e-12)
        key = jax.random.key(seed)
        ks = jax.random.split(key, 5)
        B, N, dim = (2, 512, 512)
        hidden = HEADS * DIM_HEAD
        x = jax.random.normal(ks[0], (B, N, dim), dtype=jnp.float32)
        g_norm = jnp.ones((dim,), dtype=jnp.float32)
        Wq = jax.random.normal(ks[1], (dim, hidden), dtype=jnp.float32) * dim ** (-0.5)
        Wkv = jax.random.normal(ks[2], (dim, 2 * DIM_HEAD), dtype=jnp.float32) * dim ** (-0.5)
        Wout = jax.random.normal(ks[3], (hidden, dim), dtype=jnp.float32) * hidden ** (-0.5)
        g_out = jnp.ones((dim,), dtype=jnp.float32)
        return {'x': x, 'g_norm': g_norm, 'Wq': Wq, 'Wkv': Wkv, 'Wout': Wout, 'g_out': g_out}
    _L0_attn_all = _L0_attn_setup()
    _L0_attn_in = {k: v for k, v in _L0_attn_all.items() if k in ('g_norm', 'Wq', 'Wkv', 'Wout', 'g_out')}
    del _L0_attn_all

    def _L0_xattn_setup():
        import jax, jax.numpy as jnp
        import numpy as np
        import math
        B, L, DM = (2, 512, 256)
        DS, DC, EXP = (16, 4, 2)
        DI = EXP * DM
        DR = math.ceil(DM / 16)
        DT_MIN, DT_MAX, DT_FLOOR = (0.001, 0.1, 0.0001)

        def _ssm_forward(hidden_states, z, in_proj_w, conv_w, conv_b, x_proj_w, dt_proj_w, dt_proj_b, A_log, D):
            b = hidden_states.shape[0]
            x = jnp.einsum('ed,bld->bel', in_proj_w, hidden_states)
            xp = jnp.pad(x, ((0, 0), (0, 0), (DC - 1, 0)))
            xc = jax.lax.conv_general_dilated(xp, conv_w[:, None, :], window_strides=(1,), padding='VALID', dimension_numbers=('NCH', 'OIH', 'NCH'), feature_group_count=DI)
            u = jax.nn.silu(xc + conv_b[None, :, None])
            x_dbl = jnp.einsum('ke,bel->bkl', x_proj_w, u)
            dt_lo = x_dbl[:, :DR]
            Bm = x_dbl[:, DR:DR + DS]
            Cm = x_dbl[:, DR + DS:]
            delta = jax.nn.softplus(jnp.einsum('er,brl->bel', dt_proj_w, dt_lo) + dt_proj_b[None, :, None])
            A = -jnp.exp(A_log)

            def step(state, xs):
                d_t, B_t, C_t, u_t = xs
                dA = jnp.exp(d_t[..., None] * A)
                state = state * dA + (d_t * u_t)[..., None] * B_t[:, None, :]
                y_t = jnp.einsum('ben,bn->be', state, C_t)
                return (state, y_t)
            xs = (jnp.moveaxis(delta, -1, 0), jnp.moveaxis(Bm, -1, 0), jnp.moveaxis(Cm, -1, 0), jnp.moveaxis(u, -1, 0))
            state0 = jnp.zeros((b, DI, DS), delta.dtype)
            _, ys = jax.lax.scan(step, state0, xs)
            y = jnp.moveaxis(ys, 0, -1)
            y = y + D[None, :, None] * u
            y = y * jax.nn.silu(z)
            return jnp.swapaxes(y, 1, 2)
        key = jax.random.key(seed)
        ks = jax.random.split(key, 8)
        hidden_states = jax.random.normal(ks[0], (B, L, DM), jnp.float32)
        z = jax.random.normal(ks[1], (B, DI, L), jnp.float32)
        in_proj_w = jax.random.normal(ks[2], (DI, DM), jnp.float32) * DM ** (-0.5)
        conv_w = jax.random.normal(ks[3], (DI, DC), jnp.float32) * DC ** (-0.5)
        conv_b = jnp.zeros((DI,), jnp.float32)
        x_proj_w = jax.random.normal(ks[4], (DR + 2 * DS, DI), jnp.float32) * DI ** (-0.5)
        dt_std = DR ** (-0.5)
        dt_proj_w = jax.random.uniform(ks[5], (DI, DR), jnp.float32, -dt_std, dt_std)
        dt = jnp.exp(jax.random.uniform(ks[6], (DI,), jnp.float32) * (math.log(DT_MAX) - math.log(DT_MIN)) + math.log(DT_MIN))
        dt = jnp.clip(dt, DT_FLOOR)
        dt_proj_b = dt + jnp.log(-jnp.expm1(-dt))
        A_log = jnp.log(jnp.broadcast_to(jnp.arange(1, DS + 1, dtype=jnp.float32), (DI, DS)))
        D = jnp.ones((DI,), jnp.float32)
        return dict(hidden_states=hidden_states, z=z, in_proj_w=in_proj_w, conv_w=conv_w, conv_b=conv_b, x_proj_w=x_proj_w, dt_proj_w=dt_proj_w, dt_proj_b=dt_proj_b, A_log=A_log, D=D)
    _L0_xattn_all = _L0_xattn_setup()
    _L0_xattn_in = {k: v for k, v in _L0_xattn_all.items() if k in ('in_proj_w', 'conv_w', 'conv_b', 'x_proj_w', 'dt_proj_w', 'dt_proj_b', 'A_log', 'D')}
    del _L0_xattn_all

    def _L0_ffn_setup():
        import jax
        import jax.numpy as jnp
        import numpy as np
        NUM_EXPERTS = 32
        HIDDEN = 512
        INTER = 192
        TOP_K = 8
        TAU = 0.05
        BATCH, SEQ = (2, 256)
        key = jax.random.key(seed)
        k1, k2, k3, k4 = jax.random.split(key, 4)
        return {'hidden_states': jax.random.normal(k1, (BATCH, SEQ, HIDDEN), dtype=jnp.float32), 'gate_weight': jax.random.normal(k2, (NUM_EXPERTS, HIDDEN), dtype=jnp.float32) * 0.02, 'gate_up_proj': jax.random.normal(k3, (NUM_EXPERTS, 2 * INTER, HIDDEN), dtype=jnp.float32) * 0.02, 'down_proj': jax.random.normal(k4, (NUM_EXPERTS, HIDDEN, INTER), dtype=jnp.float32) * 0.02, 'layer_alpha': jnp.array(1.0, dtype=jnp.float32)}
    _L0_ffn_all = _L0_ffn_setup()
    _L0_ffn_in = {k: v for k, v in _L0_ffn_all.items() if k in ('gate_weight', 'gate_up_proj', 'down_proj', 'layer_alpha')}
    del _L0_ffn_all
    return {'x': x, 'ctx_1024': ctx_1024, 'L0_attn_g_norm': _L0_attn_in['g_norm'], 'L0_attn_Wq': _L0_attn_in['Wq'], 'L0_attn_Wkv': _L0_attn_in['Wkv'], 'L0_attn_Wout': _L0_attn_in['Wout'], 'L0_attn_g_out': _L0_attn_in['g_out'], 'L0_xattn_in_proj_w': _L0_xattn_in['in_proj_w'], 'L0_xattn_conv_w': _L0_xattn_in['conv_w'], 'L0_xattn_conv_b': _L0_xattn_in['conv_b'], 'L0_xattn_x_proj_w': _L0_xattn_in['x_proj_w'], 'L0_xattn_dt_proj_w': _L0_xattn_in['dt_proj_w'], 'L0_xattn_dt_proj_b': _L0_xattn_in['dt_proj_b'], 'L0_xattn_A_log': _L0_xattn_in['A_log'], 'L0_xattn_D': _L0_xattn_in['D'], 'L0_ffn_gate_weight': _L0_ffn_in['gate_weight'], 'L0_ffn_gate_up_proj': _L0_ffn_in['gate_up_proj'], 'L0_ffn_down_proj': _L0_ffn_in['down_proj'], 'L0_ffn_layer_alpha': _L0_ffn_in['layer_alpha']}

def reference(x, ctx_1024, L0_attn_g_norm, L0_attn_Wq, L0_attn_Wkv, L0_attn_Wout, L0_attn_g_out, L0_xattn_in_proj_w, L0_xattn_conv_w, L0_xattn_conv_b, L0_xattn_x_proj_w, L0_xattn_dt_proj_w, L0_xattn_dt_proj_b, L0_xattn_A_log, L0_xattn_D, L0_ffn_gate_weight, L0_ffn_gate_up_proj, L0_ffn_down_proj, L0_ffn_layer_alpha):
    import jax
    import jax.numpy as jnp

    def _L0_attn_ref(x, g_norm, Wq, Wkv, Wout, g_out):
        import jax, jax.numpy as jnp
        import numpy as np
        HEADS = 16
        DIM_HEAD = 128
        SCALE = 16.0
        EPS = 1e-05

        def _layernorm(x, g):
            mu = jnp.mean(x, axis=-1, keepdims=True)
            var = jnp.mean((x - mu) ** 2, axis=-1, keepdims=True)
            return (x - mu) * jax.lax.rsqrt(var + EPS) * g

        def _l2norm(t):
            return t * jax.lax.rsqrt(jnp.sum(t * t, axis=-1, keepdims=True) + 1e-12)
        B, N, dim = x.shape
        xn = _layernorm(x, g_norm)
        q = xn @ Wq
        kv = xn @ Wkv
        k, v = (kv[..., :DIM_HEAD], kv[..., DIM_HEAD:])
        q = q.reshape(B, N, HEADS, DIM_HEAD).transpose(0, 2, 1, 3)
        q = q * SCALE
        q = _l2norm(q)
        k = _l2norm(k)
        s = jnp.sqrt(SCALE).astype(x.dtype)
        q = q * s
        k = k * s
        sim = jnp.einsum('bhid,bjd->bhij', q, k)
        attn = jax.nn.softmax(sim.astype(jnp.float32), axis=-1).astype(sim.dtype)
        out = jnp.einsum('bhij,bjd->bhid', attn, v)
        out = out.transpose(0, 2, 1, 3).reshape(B, N, HEADS * DIM_HEAD)
        out = out @ Wout
        return _layernorm(out, g_out)

    def _L0_xattn_ref(hidden_states, z, in_proj_w, conv_w, conv_b, x_proj_w, dt_proj_w, dt_proj_b, A_log, D):
        import jax, jax.numpy as jnp
        import numpy as np
        import math
        B, L, DM = (2, 512, 256)
        DS, DC, EXP = (16, 4, 2)
        DI = EXP * DM
        DR = math.ceil(DM / 16)
        DT_MIN, DT_MAX, DT_FLOOR = (0.001, 0.1, 0.0001)

        def _ssm_forward(hidden_states, z, in_proj_w, conv_w, conv_b, x_proj_w, dt_proj_w, dt_proj_b, A_log, D):
            b = hidden_states.shape[0]
            x = jnp.einsum('ed,bld->bel', in_proj_w, hidden_states)
            xp = jnp.pad(x, ((0, 0), (0, 0), (DC - 1, 0)))
            xc = jax.lax.conv_general_dilated(xp, conv_w[:, None, :], window_strides=(1,), padding='VALID', dimension_numbers=('NCH', 'OIH', 'NCH'), feature_group_count=DI)
            u = jax.nn.silu(xc + conv_b[None, :, None])
            x_dbl = jnp.einsum('ke,bel->bkl', x_proj_w, u)
            dt_lo = x_dbl[:, :DR]
            Bm = x_dbl[:, DR:DR + DS]
            Cm = x_dbl[:, DR + DS:]
            delta = jax.nn.softplus(jnp.einsum('er,brl->bel', dt_proj_w, dt_lo) + dt_proj_b[None, :, None])
            A = -jnp.exp(A_log)

            def step(state, xs):
                d_t, B_t, C_t, u_t = xs
                dA = jnp.exp(d_t[..., None] * A)
                state = state * dA + (d_t * u_t)[..., None] * B_t[:, None, :]
                y_t = jnp.einsum('ben,bn->be', state, C_t)
                return (state, y_t)
            xs = (jnp.moveaxis(delta, -1, 0), jnp.moveaxis(Bm, -1, 0), jnp.moveaxis(Cm, -1, 0), jnp.moveaxis(u, -1, 0))
            state0 = jnp.zeros((b, DI, DS), delta.dtype)
            _, ys = jax.lax.scan(step, state0, xs)
            y = jnp.moveaxis(ys, 0, -1)
            y = y + D[None, :, None] * u
            y = y * jax.nn.silu(z)
            return jnp.swapaxes(y, 1, 2)
        return _ssm_forward(hidden_states, z, in_proj_w, conv_w, conv_b, x_proj_w, dt_proj_w, dt_proj_b, A_log, D)

    def _L0_ffn_ref(hidden_states, gate_weight, gate_up_proj, down_proj, layer_alpha):
        import jax
        import jax.numpy as jnp
        import numpy as np
        NUM_EXPERTS = 32
        HIDDEN = 512
        INTER = 192
        TOP_K = 8
        TAU = 0.05
        BATCH, SEQ = (2, 256)
        B, S, H = hidden_states.shape
        x = hidden_states.reshape(-1, H)
        T = x.shape[0]
        logits = x @ gate_weight.T
        probs = jax.nn.softmax(logits.astype(jnp.float32), axis=-1).astype(logits.dtype)
        topv, topi = jax.lax.top_k(probs, TOP_K)
        topv = topv / jnp.clip(topv.sum(axis=-1, keepdims=True), 1e-12)
        scaled = topv * layer_alpha.astype(topv.dtype)
        active = scaled >= TAU
        empty = ~jnp.any(active, axis=-1)
        fallback = jnp.arange(TOP_K)[None, :] == jnp.argmax(scaled, axis=-1)[:, None]
        active = active | empty[:, None] & fallback
        routing_weights = topv * active.astype(topv.dtype)
        routing_weights = routing_weights / jnp.clip(routing_weights.sum(axis=-1, keepdims=True), 1e-12)
        combine = jnp.zeros((T, NUM_EXPERTS), dtype=x.dtype)
        combine = combine.at[jnp.arange(T)[:, None], topi].add(routing_weights)

        def expert_step(acc, xs):
            w_gu, w_d, c_e = xs
            gu = x @ w_gu.T
            g, u = jnp.split(gu, 2, axis=-1)
            h = jax.nn.silu(g) * u
            acc = acc + h @ w_d.T * c_e[:, None]
            return (acc, None)
        out, _ = jax.lax.scan(expert_step, jnp.zeros_like(x), (gate_up_proj, down_proj, combine.T))
        return out.reshape(B, S, H)
    x = x + _L0_attn_ref(_layernorm(x, axis=-1), L0_attn_g_norm, L0_attn_Wq, L0_attn_Wkv, L0_attn_Wout, L0_attn_g_out)
    x = x + _L0_xattn_ref(ctx_1024, _layernorm(x, axis=-1), L0_xattn_in_proj_w, L0_xattn_conv_w, L0_xattn_conv_b, L0_xattn_x_proj_w, L0_xattn_dt_proj_w, L0_xattn_dt_proj_b, L0_xattn_A_log, L0_xattn_D)
    x = x + _L0_ffn_ref(_layernorm(x, axis=-1), L0_ffn_gate_weight, L0_ffn_gate_up_proj, L0_ffn_down_proj, L0_ffn_layer_alpha)
    return x

_drawn_inputs = setup_inputs


def setup_inputs(seed=0):
    import zlib

    import numpy as np

    out = dict(_drawn_inputs(seed))
    spreads = {'L0_attn_g_norm': (1.0, 0.2),
     'L0_attn_g_out': (1.0, 0.2),
     'L0_xattn_conv_b': (0.0, 0.305),
     'L0_xattn_D': (1.0, 0.2)}
    factors = {'L0_xattn_dt_proj_w': 7.427,
     'L0_xattn_dt_proj_b': 3.145,
     'L0_ffn_gate_weight': 8.0,
     'L0_ffn_gate_up_proj': 7.258,
     'L0_ffn_down_proj': 7.26}
    for name, (base, spread) in spreads.items():
        noise = np.random.default_rng([zlib.crc32(name.encode()), seed]).standard_normal(out[name].shape)
        drawn = base * np.exp(spread * noise) if base else spread * noise
        out[name] = jnp.asarray(drawn.astype(out[name].dtype))
    for name, factor in factors.items():
        out[name] = (out[name] * factor).astype(out[name].dtype)
    return out
```

```python
from contextlib import ExitStack

import numpy as np

import concourse.bass as bass
from concourse import mybir

F32 = mybir.dt.float32
F32R = mybir.dt.float32r
I32 = mybir.dt.int32
U32 = mybir.dt.uint32
ALU = mybir.AluOpType
ACT = mybir.ActivationFunctionType
AX = mybir.AxisListType.X

P = 128
NB, T, D = 4, 512, 512
TT, KT = T // P, D // P
H, DH = 16, 128
G = H // 4
DM, DI, DS, DC, DR = 256, 512, 16, 4, 16
ET, MT = DI // P, DM // P
XD = DR + 2 * DS
NE, INTER, TOPK, TAU = 32, 192, 8, 0.05
NTOK = NB * T
CAP = NTOK + 3 * P
MIN_BLK = 2
CHAIN = 62
TRASH = NE * CAP
ROW = 560
W_COL, ID_COL = D, D + NE
EPS_LN, EPS_L2 = 1e-5, 1e-12
SCALE = 16.0
EXP_SET = "natural_log_exp_and_others"

RS_LN1, RS_LN2, RS_K, RS_Q0 = 0, 1, 2, 3
RS_O, RS_Z, RS_F = RS_Q0 + H, RS_Q0 + H + 1, RS_Q0 + H + 2
RS_ALL = RS_F + 1
LN1, LN2, LNO, LNZ, LNF, LN_ALL = 0, 1, 2, 3, 4, 5

C_ID, C_TRI, C_ONE = 0, P, 2 * P
C_BASE, C_REV, C_TRASH, C_TOK = 3 * P, 3 * P + NE, 3 * P + 2 * NE, 3 * P + 2 * NE + 1
EXP_BLK = NTOK // P + 1
MAX_BLK = NTOK * TOPK // P + MIN_BLK * NE
C_PAD = C_TOK + NB * TT
C_ALL = C_PAD + 1


def constants():
    c = np.zeros((P, C_ALL), np.float32)
    p = np.arange(P)
    c[:, C_ID:C_ID + P] = np.eye(P)
    c[:, C_TRI:C_TRI + P] = p[:, None] < p[None, :]
    c[:, C_ONE:C_ONE + P] = 1.0
    c[:, C_BASE:C_BASE + NE] = np.arange(NE)[None, :] * CAP + 1
    c[:, C_REV:C_REV + NE] = NE - np.arange(NE)[None, :]
    c[:, C_TRASH] = TRASH + 1 + p
    c[:, C_TOK:C_PAD] = p[:, None] + P * np.arange(NB * TT)[None, :]
    c[:, C_PAD] = NTOK + p
    return c


def decoder_layer(nc, a):
    ctx = ExitStack()
    with ctx:
        def sb(name, shape, dt=F32):
            return ctx.enter_context(nc.sbuf_tensor(name, shape, dt))

        def sem(name):
            return ctx.enter_context(nc.semaphore(name))

        def dram(name, shape):
            return nc.dram_tensor(name, shape, F32, kind="Internal").ap()

        bank = [ctx.enter_context(nc.psum_tensor(f"bank{i}", [P, 512], F32)) for i in range(8)]
        bank_q, bank_s, bank_o, bank_t = bank[0:2], bank[2:4], bank[4:6], bank[6:8]

        bc_dram = dram("bc_dram", [NB, 2 * DS, T])
        slots = dram("slots", [TRASH + P, ROW])

        out = a["out"]

        x_sb = sb("x_sb", [P, TT, D])
        x_row = sb("x_row", [P, TT, ROW])
        slot = sb("slot", [P, TT, 8], I32)
        cs = sb("cs", [P, TT + 1, NE])
        const = sb("const", [P, C_ALL])
        ident, tri, ones = const[:, C_ID:C_ID + P], const[:, C_TRI:C_TRI + P], const[:, C_ONE:C_ONE + P]

        stage_a = ExitStack()
        def sb(name, shape, dt=F32):
            return stage_a.enter_context(nc.sbuf_tensor(name, shape, dt))

        wq = sb("wq", [P, KT, H * DH])
        wkv = sb("wkv", [P, KT, 2 * DH])
        w_in = sb("w_in", [P, MT, DI])
        w_x = sb("w_x", [P, ET, XD])
        w_dt = sb("w_dt", [DR, DI])
        w_gate = sb("w_gate", [P, KT, NE])
        g_norm = sb("g_norm", [P, KT])
        g_out = sb("g_out", [P, D])
        conv_w = sb("conv_w", [P, ET, DC])
        conv_b = sb("conv_b", [P, ET])
        dt_b = sb("dt_b", [P, ET])
        d_skip = sb("d_skip", [P, ET])
        neg_a = sb("neg_a", [P, DS, ET])
        alpha = sb("alpha", [P, 1])

        ctx_t = sb("ctx_t", [P, MT, T])
        xn_t = sb("xn_t", [P, KT, T])
        k_t = sb("k_t", [P, T])
        v_aug = sb("v_aug", [P, TT, DH + 1])
        q_s = sb("q_s", [P, TT, 4, DH])
        q_t = sb("q_t", [P, 4, T])
        probs = sb("probs", [P, KT, T])
        o_s = sb("o_s", [P, TT, DH])
        k_n = o_s
        o_t = sb("o_t", [P, H, T])
        wout = sb("wout", [P, 4, D])
        delta = sb("delta", [P, ET, T])
        du = sb("du", [P, ET, T])
        y = sb("y", [P, ET, T])
        decay = sb("decay", [P, ET * (T + DC - 1)])
        x_pad = decay[:, :].rearrange("p (e t) -> p e t", e=ET)
        dA = decay[:, 0:ET * T]
        dA3 = dA.rearrange("p (e t) -> p e t", e=ET)
        dbu = sb("dbu", [P, ET, T])
        state = sb("state", [P, ET, T])
        b_bc = sb("b_bc", [P, 2, T])
        c_bc = sb("c_bc", [P, 2, T])
        x_dbl = sb("x_dbl", [XD, T])
        junk = sb("junk", [P, 4, DH], mybir.dt.bfloat16)
        norm = probs
        st = sb("st", [P, TT, 6])
        mv = sb("mv", [P, TT, 2])
        rs_in = sb("rs_in", [P, 4])
        rs_x = sb("rs_x", [P, 4])
        rs_l = sb("rs_l", [P, 4])
        rs_y = sb("rs_y", [P, 4])
        rs_t = sb("rs_t", [P, 4])
        rs_r = sb("rs_r", [P, 4])
        z_bias = sb("z_bias", [P, TT])
        den = sb("den", [P, TT])
        NAMES = ["lg", "pr", "rep", "sel", "tvn", "scl", "act", "cand", "ct", "fb", "wts", "slv"]
        r = {n: dbu[:].rearrange("p e t -> p (e t)")[:, i * TT * NE:(i + 1) * TT * NE].rearrange("p (t e) -> p t e", t=TT)
             for i, n in enumerate(NAMES)}
        p8 = sb("p8", [P, TT, 8])
        s8 = sb("s8", [P, TT, 8])
        t8 = sb("t8", [P, TT, 8])
        r1 = {n: sb("r1_" + n, [P, TT]) for n in ["mx", "sm", "rc", "s8", "r8", "any", "mx2", "m2", "m3", "s2", "rw"]}

        stage_a.close()

        def sb(name, shape, dt=F32):
            return ctx.enter_context(nc.sbuf_tensor(name, shape, dt))

        gu_w = [sb(f"gu_w{i}", [P, KT, 2 * INTER]) for i in range(2)]
        dn_w = [sb(f"dn_w{i}", [P, 2, D]) for i in range(2)]
        gu_hi = [sb(f"gu_hi{i}", [P, KT, 2 * INTER], F32R) for i in range(2)]
        gu_lo = [sb(f"gu_lo{i}", [P, KT, 2 * INTER], F32R) for i in range(2)]
        dn_hi = [sb(f"dn_hi{i}", [P, 2, D], F32R) for i in range(2)]
        dn_lo = [sb(f"dn_lo{i}", [P, 2, D], F32R) for i in range(2)]
        x_blk = sb("x_blk", [P, D])
        meta = sb("meta", [P, MAX_BLK + EXP_BLK, NE + 1])
        ids = [sb(f"ids{i}", [P, 1], I32) for i in range(2)]
        xt_hi, xt_lo = sb("xt_hi", [P, KT, P], F32R), sb("xt_lo", [P, KT, P], F32R)
        silu_g = sb("silu_g", [P, INTER])
        h_sb = sb("h_sb", [P, 2 * P])
        ht_hi = sb("ht_hi", [P, 2 * P], F32R)
        ht_lo = sb("ht_lo", [P, P], F32R)
        y_both = sb("y_both", [P, 2, D])
        pad = sb("pad", [P, ROW])
        n_f, nb_f, cum_f = sb("n_f", [P, NE]), sb("nb_f", [P, NE]), sb("cum_f", [P, NE])
        nb_i = sb("nb_i", [P, NE], I32)
        odd_i, odd_f = sb("odd_i", [P, 1], I32), sb("odd_f", [P, 1])
        tab = sb("tab", [P, 3 * NE + 1], I32)

        S = {n: sem(n) for n in """
            w_in_sb x_in ctx_in bc_written bc_in0 bc_in1 wout_in0 wout_in1 wout_in2 wout_in3 x2_out
            inp_ps xT_ps kv_ps kT_ps qp_ps qT_ps s_ps pv_ps oT_ps xd_ps dt_ps wout_used op_ps yT_ps fT_ps lg_ps rank_ps
            neg_a_ok act_step rs_ln rs_seed xpad_ok xnT_ok ksq_ok v_ok kT_ok u_ok xd_ok dt_ev sp_e sp_ln qss_ok qT_ok
            exp_ok dA_ok oT_ok sz_ok fT_ok rexp_ok
            dve_step bn_ok ag_ok nw ln_a ln_x conv_ok kn_ok q_ok scan_ok bc_free o_ok on_ok x1_ok zr_ok ys_ok x2_ok xf_ok dbu_ok den_ok y_ok chain
            lgs_ok act_ok slot_ok
            sent
            gu_in0 gu_in1 dn_in0 dn_in1 pad_out blk_in
            cnt_ps xt_ps gu_ps ht_ps y_ps
            guhi_ok dnhi_ok xthi_ok silu_ok hthi_ok yb_ok
            pad_ok cnt_step tab_ok gulo_ok dnlo_ok xtlo_ok h_ok htlo_ok
            ids_ok added
            """.split()}

        N_W = 15
        block = ctx.enter_context(nc.Block())

        def wait_apart(eng, semaphore, value):
            count = eng.to_reg(value)
            eng.wait_ge(S["w_in_sb"], 16 * N_W)
            eng.wait_ge(semaphore, count)

        def span(eng, e):
            return (eng.value_load(tab[0:1, bass.ds(e, 1)], min_val=MIN_BLK - 1, max_val=EXP_BLK - 1),
                    eng.value_load(tab[0:1, bass.ds(e + NE, 1)], min_val=0, max_val=MAX_BLK))

        def each_expert(eng, expert):
            with eng.Fori(0, NE // 2 - 1) as pair:
                expert(pair, 0)
                expert(pair, 1)
            expert(NE // 2 - 1, 0, after_next=False)
            expert(NE // 2 - 1, 1, after_next=False, following=False)

        @block.sync
        def _(sp):
            def load(dst, src):
                sp.dma_start(dst, src).then_inc(S["w_in_sb"], 16)

            load(const[:], a["const"])
            load(w_in[:], a["w_in_t"].rearrange("(m p) e -> p m e", p=P))
            load(conv_w[:], a["conv_w"].rearrange("(e p) c -> p e c", p=P))
            load(conv_b[:], a["conv_b"])
            load(dt_b[:], a["dt_b"])
            load(d_skip[:], a["d_skip"])
            load(neg_a[:], a["a_log"])
            load(g_norm[:], a["g_norm"])
            load(w_x[:], a["w_x_t"].rearrange("(e p) k -> p e k", p=P))
            load(w_dt[:], a["w_dt_t"])
            load(wkv[:], a["wkv"].rearrange("(k p) n -> p k n", p=P))
            load(wq[:], a["wq"].rearrange("(k p) n -> p k n", p=P))
            load(w_gate[:], a["w_gate_t"].rearrange("(k p) n -> p k n", p=P))
            load(g_out[:], a["g_out"].partition_broadcast(P))
            sp.dma_start(alpha[:], a["alpha"].partition_broadcast(P)).then_inc(S["w_in_sb"], 16)

            with sp.Fori(0, NB) as b:
                wait_apart(sp, S["x2_out"], b * 16)
                sp.wait_ge(S["xf_ok"], b * TT)
                sp.dma_start(x_sb[:], a["x"][bass.ds(b * T, T), :].rearrange("(t p) d -> p t d", p=P)).then_inc(S["x_in"], 16)
                wait_apart(sp, S["inp_ps"], b * ET)
                sp.dma_start(ctx_t[:], a["ctx_t"][bass.ds(b * DM, DM), :].rearrange("(m p) l -> p m l", p=P)).then_inc(S["ctx_in"], 16)

                def load_wout(h):
                    sp.dma_start(wout[:, h % 4, :], a["wout"][h * DH:(h + 1) * DH, :]).then_inc(S[f"wout_in{h % 4}"], 16)

                sp.wait_ge(S["op_ps"], b * TT)
                for h in range(4):
                    load_wout(h)
                wait_apart(sp, S["xd_ok"], b + 1)
                sp.dma_start(bc_dram[bass.ds(b, 1)].rearrange("o n t -> (o n) t"), x_dbl[DR:XD, :]).then_inc(S["bc_written"], 16)
                wait_apart(sp, S["bc_written"], b * 16 + 16)
                with sp.Fori(0, DS // 2) as pair:
                    n = pair * 2
                    for i in range(2):
                        wait_apart(sp, S["bc_free"], b * DS + n + i)
                        for dst, row in ((b_bc, 0), (c_bc, DS)):
                            src = bc_dram[bass.ds(b, 1), bass.ds(n + (row + i), 1), :].rearrange("o n t -> (o n t)")
                            sp.dma_start(dst[:, i, :], src.partition_broadcast(P)).then_inc(S[f"bc_in{i}"], 16)
                for h in range(4, H):
                    sp.wait_ge(S["wout_used"], b * (H - 1) + (h - 3))
                    load_wout(h)
                wait_apart(sp, S["x2_ok"], b * TT + TT)
                sp.dma_start(out[bass.ds(b * T, T), :].rearrange("(t p) d -> p t d", p=P), x_sb[:]).then_inc(S["x2_out"], 16)

            sp.wait_ge(S["tab_ok"], 1)
            sp.wait_ge(S["sent"], NB * TT * TOPK * 16)
            with sp.Fori(0, NE) as e:
                n = sp.value_load(tab[0:1, bass.ds(e + 2 * NE, 1)], min_val=0, max_val=NTOK)
                dst = slots[bass.ds(e * CAP + n, 3 * P), :].rearrange("(t p) r -> p t r", p=P)
                sp.dma_start(dst, pad[:].unsqueeze(1).to_broadcast([P, 3, ROW])).then_inc(S["pad_out"], 16)
            sp.wait_ge(S["pad_out"], NE * 16)
            sp.wait_ge(S["x2_out"], NB * 16)

            def load_block(row, blk):
                sp.dma_start(x_blk[:], slots[bass.ds(row, P), 0:D]).then_inc(S["blk_in"], 16)
                sp.dma_start(meta[:, bass.ds(blk, 1), :].rearrange("p o c -> p (o c)"), slots[bass.ds(row, P), W_COL:ID_COL + 1]).then_inc(S["blk_in"], 16)

            with sp.Fori(0, NE) as e:
                more, c = span(sp, e)
                with sp.Fori(0, more + 1) as k:
                    blk = c + k
                    wait_apart(sp, S["xt_ps"], blk)
                    load_block(e * CAP + k * P, blk)
            pairs = sp.value_load(tab[0:1, 3 * NE:3 * NE + 1], min_val=NE, max_val=MAX_BLK // 2 + 1)
            wait_apart(sp, S["xt_ps"], pairs * 2)
            load_block(0, pairs * 2)
            sp.wait_ge(S["blk_in"], pairs * 64 + 32)
            wait_apart(sp, S["added"], pairs * 32 + 16)

        @block.tensor
        def _(pe):
            def transpose(out, src):
                return pe.transpose(out, src, ident)

            pe.wait_ge(S["w_in_sb"], 16 * N_W)
            with pe.Fori(0, NB) as b:
                pe.wait_ge(S["ctx_in"], b * 16 + 16)
                pe.wait_ge(S["on_ok"], b * TT)
                for e in range(ET):
                    if e >= 2:
                        pe.wait_ge(S["xpad_ok"], b * ET + e - 1)
                    for m in range(MT):
                        mm = pe.matmul(bank_s[e % 2][:], w_in[:, m, e * P:(e + 1) * P], ctx_t[:, m, :], start=(m == 0), stop=(m == MT - 1))
                    mm.then_inc(S["inp_ps"], 1)
                pe.wait_ge(S["ln_x"], b * TT + TT)
                for k in range(KT):
                    if k >= 2:
                        pe.wait_ge(S["xnT_ok"], b * KT + k - 1)
                    for t in range(TT):
                        mm = transpose(bank_q[k % 2][:, t * P:(t + 1) * P], norm[:, t, k * P:(k + 1) * P])
                    mm.then_inc(S["xT_ps"], 1)
                pe.wait_ge(S["xnT_ok"], b * KT + KT)
                for t in range(TT):
                    for k in range(KT):
                        mm = pe.matmul(bank_o[t // 2][:, (t % 2) * 2 * DH:(t % 2 + 1) * 2 * DH], xn_t[:, k, t * P:(t + 1) * P], wkv[:, k, :],
                                       start=(k == 0), stop=(k == KT - 1))
                    mm.then_inc(S["kv_ps"], 1)

                def q_piece(group, t):
                    for k in range(KT):
                        rhs = wq[:, k, bass.ds(group * 4 * DH, 4 * DH)]
                        mm = pe.matmul(bank_q[t % 2][:], xn_t[:, k, t * P:(t + 1) * P], rhs, start=(k == 0), stop=(k == KT - 1))
                    mm.then_inc(S["qp_ps"], 1)

                def q_transposes(group):
                    pe.wait_ge(S["q_ok"], b * H + group * 4 + 4)
                    for j in range(4):
                        if j >= 2:
                            pe.wait_ge(S["qT_ok"], b * H + group * 4 + j - 1)
                        for t in range(TT):
                            mm = transpose((bank_t[0] if j % 2 == 0 else bank_q[0])[:, t * P:(t + 1) * P], q_s[:, t, j, :])
                        mm.then_inc(S["qT_ps"], 1)

                def scores(h, j):
                    pe.wait_ge(S["qT_ok"], b * H + h + 1)
                    for k in range(KT):
                        if k >= 2:
                            pe.wait_ge(S["exp_ok"], b * H * KT + h * KT + (k - 1))
                        pe.matmul(bank_s[k % 2][:], k_t[:, k * P:(k + 1) * P], q_t[:, j, :], start=True, stop=True).then_inc(S["s_ps"], 1)

                for t in range(TT):
                    if t >= 2:
                        pe.wait_ge(S["q_ok"], b * H + t - 1)
                    q_piece(0, t)
                pe.wait_ge(S["kn_ok"], b * 2 + 2)
                for t in range(TT):
                    mm = transpose(bank_t[1][:, t * P:(t + 1) * P], k_n[:, t, :])
                mm.then_inc(S["kT_ps"], 1)
                q_transposes(0)
                pe.wait_ge(S["kT_ok"], b + 1)
                pe.wait_ge(S["xpad_ok"], b * ET + ET)
                scores(0, 0)
                pe.wait_ge(S["v_ok"], b * 2 + 2)
                pe.wait_ge(S["u_ok"], b * ET + ET)
                for e in range(ET):
                    mm = pe.matmul(bank_t[1][0:XD, :], w_x[:, e, :], state[:, e, :], start=(e == 0), stop=(e == ET - 1))
                mm.then_inc(S["xd_ps"], 1)
                pe.wait_ge(S["xd_ok"], b + 1)
                pe.wait_ge(S["exp_ok"], b * H * KT + KT)
                for e in range(ET):
                    if e >= 2:
                        pe.wait_ge(S["dt_ev"], b * ET + e - 1)
                    pe.matmul(bank_s[e % 2][:], w_dt[:, e * P:(e + 1) * P], x_dbl[0:DR, :], start=True, stop=True).then_inc(S["dt_ps"], 1)
                wait_apart(pe, S["dt_ev"], b * ET + ET)

                def head(h, group, j, last_group):
                    if not last_group:
                        pe.wait_ge(S["q_ok"], b * H + h + 3)
                        pe.wait_ge(S["qT_ok"], b * H + group * 4 + 4)
                        q_piece(group + 1, j)
                    pe.wait_ge(S["exp_ok"], b * H * KT + h * KT + KT)
                    pe.wait_ge(S["o_ok"], b * H * 2 + h * 2)
                    for half in range(2):
                        for t in (2 * half, 2 * half + 1):
                            for k in range(KT):
                                mm = pe.matmul(bank_o[half][:, (t % 2) * (DH + 1):(t % 2 + 1) * (DH + 1)], probs[:, k, t * P:(t + 1) * P], v_aug[:, k, :],
                                               start=(k == 0), stop=(k == KT - 1))
                        mm.then_inc(S["pv_ps"], 1)
                    if not (last_group and j == 3):
                        if j == 3:
                            q_transposes(group + 1)
                        scores(h + 1, (j + 1) % 4)
                    pe.wait_ge(S["o_ok"], b * H * 2 + h * 2 + 2)
                    pe.wait_ge(S["oT_ok"], b * H + h)
                    for t in range(TT):
                        mm = transpose(bank_t[1][:, t * P:(t + 1) * P], o_s[:, t, :])
                    mm.then_inc(S["oT_ps"], 1)

                with pe.Fori(0, G - 1) as g:
                    for j in range(4):
                        head(g * 4 + j, g, j, False)
                for j in range(4):
                    head((G - 1) * 4 + j, G - 1, j, True)
                pe.wait_ge(S["o_ok"], b * H * 2 + H * 2)
                for h in range(H):
                    pe.wait_ge(S["oT_ok"], b * H + h + 1)
                    pe.wait_ge(S[f"wout_in{h % 4}"], b * G * 16 + (h // 4 * 16 + 16))
                    for t in range(TT):
                        mm = pe.matmul((bank_o + bank_s)[t][:], o_t[:, h, t * P:(t + 1) * P], wout[:, h % 4, :], start=(h == 0), stop=(h == H - 1))
                        if h == H - 1:
                            mm.then_inc(S["op_ps"], 1)
                    if h < H - 1:
                        mm.then_inc(S["wout_used"], 1)
                pe.wait_ge(S["ys_ok"], b + 1)
                for t in range(TT):
                    if t >= 2:
                        pe.wait_ge(S["x2_ok"], b * TT + t - 1)
                    for e in range(ET):
                        mm = transpose(bank_q[t % 2][:, e * P:(e + 1) * P], y[:, e, t * P:(t + 1) * P])
                    mm.then_inc(S["yT_ps"], 1)
                pe.wait_ge(S["xf_ok"], b * TT + TT)
                for k in range(KT):
                    if k >= 2:
                        pe.wait_ge(S["fT_ok"], b * KT + k - 1)
                    for t in range(TT):
                        mm = transpose(bank_t[k % 2][:, t * P:(t + 1) * P], x_row[:, t, k * P:(k + 1) * P])
                    mm.then_inc(S["fT_ps"], 1)
                pe.wait_ge(S["fT_ok"], b * KT + KT)
                for t in range(TT):
                    for k in range(KT):
                        mm = pe.matmul(bank_o[0][:, t * NE:(t + 1) * NE], norm[:, k, t * P:(t + 1) * P], w_gate[:, k, :], start=(k == 0), stop=(k == KT - 1))
                mm.then_inc(S["lg_ps"], 1)
                pe.wait_ge(S["act_ok"], b + 1)
                for t in range(TT):
                    pe.matmul(bank_o[1][:, t * NE:(t + 1) * NE], tri, r["act"][:, t, :], start=True, stop=False)
                    mm = pe.matmul(bank_o[1][:, t * NE:(t + 1) * NE], ones, cs[:, t, :], start=False, stop=True)
                mm.then_inc(S["rank_ps"], 1)

            xt_bank, gu_bank, ht_bank, y_bank = bank_q[0], bank_s[0], bank_s[1], bank_o[0]
            pe.wait_ge(S["slot_ok"], NB)
            pe.matmul(bank_q[1][:, 0:NE], ones, cs[:, 0, :], start=True, stop=True).then_inc(S["cnt_ps"], 1)

            def xt(blk):
                pe.wait_ge(S["blk_in"], blk * 32 + 32)
                for k in range(KT):
                    mm = transpose(xt_bank[:, k * P:(k + 1) * P], x_blk[:, k * P:(k + 1) * P])
                mm.then_inc(S["xt_ps"], 1)

            def gate_up(blk, e, i):
                pe.wait_ge(S["gulo_ok"], e + 1)
                pe.wait_ge(S["xtlo_ok"], blk + 1)
                for k in range(KT):
                    pe.matmul(gu_bank[:, 0:2 * INTER], xt_hi[:, k, :], gu_hi[i][:, k, :], start=(k == 0), stop=False)
                    pe.matmul(gu_bank[:, 0:2 * INTER], xt_hi[:, k, :], gu_lo[i][:, k, :], start=False, stop=False)
                    mm = pe.matmul(gu_bank[:, 0:2 * INTER], xt_lo[:, k, :], gu_hi[i][:, k, :], start=False, stop=(k == KT - 1))
                mm.then_inc(S["gu_ps"], 1)

            def ht(blk):
                pe.wait_ge(S["h_ok"], blk * 2 + 2)
                for k in range(2):
                    mm = transpose(ht_bank[:, k * P:(k + 1) * P], h_sb[:, k * P:(k + 1) * P])
                mm.then_inc(S["ht_ps"], 1)

            def down(blk, e, i):
                pe.wait_ge(S["dnlo_ok"], e + 1)
                pe.wait_ge(S["htlo_ok"], blk * 2 + 2)
                pe.wait_ge(S["yb_ok"], blk)
                pe.matmul(y_bank[:], ht_hi[:, 0:P], dn_hi[i][:, 0, :], start=True, stop=False)
                pe.matmul(y_bank[:], ht_hi[:, 0:P], dn_lo[i][:, 0, :], start=False, stop=False)
                pe.matmul(y_bank[:], ht_lo[:], dn_hi[i][:, 0, :], start=False, stop=False)
                pe.matmul(y_bank[:], ht_hi[:, P:], dn_hi[i][:, 1, :], start=False, stop=False)
                pe.matmul(y_bank[:], ht_hi[0:P // 2, P:], dn_lo[i][0:P // 2, 1, :], start=False, stop=True).then_inc(S["y_ps"], 1)

            xt(0)
            gate_up(0, 0, 0)
            xt(1)

            def expert(pair, i, after_next=True, following=True):
                e = pair * 2 + i
                more, c = span(pe, e)
                ht(c)
                with pe.Fori(0, more) as k:
                    blk = c + k
                    gate_up(blk + 1, e, i)
                    xt(blk + 2)
                    down(blk, e, i)
                    ht(blk + 1)
                if following:
                    gate_up(c + more + 1, e + 1, 1 - i)
                    xt(c + more + 2)
                down(c + more, e, i)

            each_expert(pe, expert)

        @block.scalar
        def _(act):
            def rs_seed(b, job, src, scale, eps, w=4):
                act.activation(rs_l[:, 0:w], src, ACT.Ln, scale=scale, bias=eps).then_inc(S["rs_ln"], 1)
                act.wait_ge(S["rs_ln"], b * RS_ALL + job + 1)
                act.activation(rs_y[:, 0:w], rs_l[:, 0:w], ACT.Exp, scale=-0.5).then_inc(S["rs_seed"], 1)

            act.preload_act_table_set(EXP_SET)
            act.wait_ge(S["w_in_sb"], 16 * N_W)
            act.activation(neg_a[:], neg_a[:], ACT.Exp).then_inc(S["act_step"], 1)
            act.wait_ge(S["act_step"], 1)
            act.activation(neg_a[:], neg_a[:], ACT.Identity, scale=-1.0).then_inc(S["neg_a_ok"], 1)
            act.wait_ge(S["neg_a_ok"], 1)

            with act.Fori(0, NB) as b:
                act.wait_ge(S["scan_ok"], b * H)
                for e in range(ET):
                    act.wait_ge(S["inp_ps"], b * ET + e + 1)
                    act.activation(x_pad[:, e, DC - 1:], bank_s[e % 2][:], ACT.Copy).then_inc(S["xpad_ok"], 1)
                for job, ln in ((RS_LN1, LN1), (RS_LN2, LN2)):
                    act.wait_ge(S["ag_ok"], b * LN_ALL * TT + (ln + 1) * TT)
                    rs_seed(b, job, mv[:, :, 1], 1.0, EPS_LN)
                for k in range(KT):
                    act.wait_ge(S["xT_ps"], b * KT + k + 1)
                    act.activation(xn_t[:, k, :], bank_q[k % 2][:], ACT.Identity, scale=g_norm[:, k:k + 1]).then_inc(S["xnT_ok"], 1)
                for t in range(TT):
                    act.wait_ge(S["kv_ps"], b * TT + (t // 2 * 2 + 2))
                    act.activation(junk[:, t, :], bank_o[t // 2][:, (t % 2) * 2 * DH:(t % 2) * 2 * DH + DH], ACT.Square,
                                   accum_out=rs_in[:, t:t + 1]).then_inc(S["ksq_ok"], 1)
                act.wait_ge(S["ksq_ok"], b * TT + TT)
                rs_seed(b, RS_K, rs_in[:], 1 / SCALE, EPS_L2 / SCALE)
                for half in range(2):
                    act.activation(v_aug[:, 2 * half:2 * half + 2, 0:DH], bank_o[half][:, :].rearrange("p (t n) -> p t n", t=2)[:, :, DH:],
                                   ACT.Copy).then_inc(S["v_ok"], 1)

                def q_squares(group, t):
                    act.wait_ge(S["qp_ps"], b * H + group * 4 + t + 1)
                    act.wait_ge(S["nw"], b * RS_ALL * 4 + (group * 4 + (t + RS_Q0)) * 4)
                    for j in range(4):
                        act.activation(junk[:, j, :], bank_q[t % 2][:, j * DH:(j + 1) * DH], ACT.Square,
                                       accum_out=rs_in[:, j:j + 1]).then_inc(S["qss_ok"], 1)
                    act.wait_ge(S["qss_ok"], b * H * 4 + group * 16 + (t * 4 + 4))
                    rs_seed(b, group * 4 + (t + RS_Q0), rs_in[:], 1 / 16, EPS_L2 / 4096)

                def q_transposed(group):
                    for j in range(4):
                        act.wait_ge(S["qT_ps"], b * H + group * 4 + j + 1)
                        act.activation(q_t[:, j, :], (bank_t[0] if j % 2 == 0 else bank_q[0])[:], ACT.Copy).then_inc(S["qT_ok"], 1)

                def exps(h):
                    act.wait_ge(S["pv_ps"], b * H * 2 + h * 2)
                    for k in range(KT):
                        act.wait_ge(S["s_ps"], b * H * KT + h * KT + (k + 1))
                        act.activation(probs[:, k, :], bank_s[k % 2][:], ACT.Exp).then_inc(S["exp_ok"], 1)

                for t in range(TT):
                    q_squares(0, t)
                act.wait_ge(S["kT_ps"], b + 1)
                act.activation(k_t[:], bank_t[1][:], ACT.Copy).then_inc(S["kT_ok"], 1)
                q_transposed(0)
                exps(0)
                for e in range(ET):
                    act.wait_ge(S["conv_ok"], b * ET * DC + ET * (DC - 1) + e + 1)
                    act.activation(state[:, e, :], dbu[:, e, :], ACT.Silu, bias=conv_b[:, e:e + 1]).then_inc(S["u_ok"], 1)
                act.wait_ge(S["xd_ps"], b + 1)
                act.activation(x_dbl[:], bank_t[1][0:XD, :], ACT.Copy).then_inc(S["xd_ok"], 1)
                act.wait_ge(S["u_ok"], b * ET + ET)
                for e in range(ET):
                    act.wait_ge(S["dt_ps"], b * ET + e + 1)
                    act.activation(dbu[:, e, :], bank_s[e % 2][:], ACT.Abs, bias=dt_b[:, e:e + 1]).then_inc(S["act_step"], 1)
                    act.activation(delta[:, e, :], bank_s[e % 2][:], ACT.Relu, bias=dt_b[:, e:e + 1]).then_inc(S["dt_ev"], 1)
                act.preload_act_table_set(EXP_SET)
                act.wait_ge(S["act_step"], b * ET + ET + 1)
                act.activation(dA3, dbu[:], ACT.Exp, scale=-1.0).then_inc(S["sp_e"], 1)
                act.wait_ge(S["sp_e"], b + 1)
                act.activation(y[:], dA3, ACT.Ln, bias=1.0).then_inc(S["sp_ln"], 1)

                def head(h, group, j, last_group):
                    act.wait_ge(S["scan_ok"], b * H + h)
                    for e in range(ET):
                        act.activation(dA3[:, e, 1:], delta[:, e, 1:], ACT.Exp,
                                       scale=neg_a[:, bass.ds(h, 1), e:e + 1].rearrange("p a c -> p (a c)")).then_inc(S["dA_ok"], 1)
                    if not last_group:
                        q_squares(group + 1, j)
                    if not (last_group and j == 3):
                        if j == 3:
                            q_transposed(group + 1)
                        exps(h + 1)
                    act.wait_ge(S["oT_ps"], b * H + h + 1)
                    act.activation(o_t[:, bass.ds(h, 1), :].rearrange("p a t -> p (a t)"), bank_t[1][:], ACT.Copy).then_inc(S["oT_ok"], 1)

                act.wait_ge(S["dve_step"], b * 1 + 2)
                with act.Fori(0, G - 1) as g:
                    for j in range(4):
                        head(g * 4 + j, g, j, False)
                for j in range(4):
                    head((G - 1) * 4 + j, G - 1, j, True)

                act.wait_ge(S["ag_ok"], b * LN_ALL * TT + (LNO + 1) * TT)
                rs_seed(b, RS_O, mv[:, :, 1], 1.0, EPS_LN)
                act.wait_ge(S["ag_ok"], b * LN_ALL * TT + (LNZ + 1) * TT)
                rs_seed(b, RS_Z, mv[:, :, 1], 1.0, EPS_LN)
                act.wait_ge(S["zr_ok"], b + 1)
                for t in range(TT):
                    act.activation(norm[:, t, :], x_sb[:, t, :], ACT.Silu, scale=rs_r[:, t:t + 1], bias=z_bias[:, t:t + 1]).then_inc(S["sz_ok"], 1)
                act.preload_act_table_set(EXP_SET)
                act.wait_ge(S["ag_ok"], b * LN_ALL * TT + (LNF + 1) * TT)
                rs_seed(b, RS_F, mv[:, :, 1], 1.0, EPS_LN)
                act.wait_ge(S["ys_ok"], b + 1)
                for k in range(KT):
                    act.wait_ge(S["fT_ps"], b * KT + k + 1)
                    act.activation(norm[:, k, :], bank_t[k % 2][:], ACT.Copy).then_inc(S["fT_ok"], 1)
                act.wait_ge(S["lgs_ok"], b + 1)
                act.activation(r["pr"][:], r["lg"][:], ACT.Exp).then_inc(S["rexp_ok"], 1)

            xt_bank, gu_bank, ht_bank, y_bank = bank_q[0], bank_s[0], bank_s[1], bank_o[0]

            def load_weights(e, i):
                act.dma_start(gu_w[i][:], a["gate_up_t"][bass.ds(e, 1)].rearrange("o (k p) n -> p (o k) n", p=P)).then_inc(S[f"gu_in{i}"], 16)
                act.dma_start(dn_w[i][:, 0, :], a["down_t"][bass.ds(e, 1), 0:P, :].rearrange("o p d -> (o p) d")).then_inc(S[f"dn_in{i}"], 16)
                for half in range(2):
                    act.dma_start(dn_w[i][half * (P // 2):(half + 1) * (P // 2), 1, :],
                                  a["down_t"][bass.ds(e, 1), P:, :].rearrange("o p d -> (o p) d")).then_inc(S[f"dn_in{i}"], 16)

            def split_gate_up(pair, i):
                act.wait_ge(S[f"gu_in{i}"], pair * 16 + 16)
                act.activation(gu_hi[i][:], gu_w[i][:], ACT.Copy).then_inc(S["guhi_ok"], 1)

            def split_down(pair, i):
                act.wait_ge(S[f"dn_in{i}"], pair * 48 + 48)
                act.activation(dn_hi[i][:], dn_w[i][:], ACT.Copy).then_inc(S["dnhi_ok"], 1)

            def xt(blk):
                act.wait_ge(S["xt_ps"], blk + 1)
                act.activation(xt_hi[:], xt_bank[:].rearrange("p (k t) -> p k t", k=KT), ACT.Copy).then_inc(S["xthi_ok"], 1)

            def silu(blk):
                act.wait_ge(S["gu_ps"], blk + 1)
                act.activation(silu_g[:], gu_bank[:, 0:INTER], ACT.Silu).then_inc(S["silu_ok"], 1)

            def ht(blk):
                act.wait_ge(S["ht_ps"], blk + 1)
                act.activation(ht_hi[:], ht_bank[:, 0:2 * P], ACT.Copy).then_inc(S["hthi_ok"], 1)

            def weigh(blk, e):
                act.wait_ge(S["added"], blk * 16)
                act.wait_ge(S["y_ps"], blk + 1)
                act.activation(y_both[:, bass.ds(blk % 2, 1), :].rearrange("p o d -> p (o d)"), y_bank[:], ACT.Copy,
                               scale=meta[:, bass.ds(blk, 1), bass.ds(e, 1)].rearrange("p o c -> p (o c)")).then_inc(S["yb_ok"], 1)

            act.wait_ge(S["slot_ok"], NB)
            for e in range(2):
                load_weights(e, e)
            split_gate_up(0, 0)
            split_down(0, 0)
            act.wait_ge(S["tab_ok"], 1)
            xt(0)
            silu(0)
            xt(1)

            def expert(pair, i, after_next=True, following=True):
                e = pair * 2 + i
                more, c = span(act, e)
                ht(c)
                if after_next:
                    act.wait_ge(S["gulo_ok"], e + 1)
                    act.wait_ge(S["dnlo_ok"], e + 1)
                    load_weights(e + 2, i)
                if following:
                    split_gate_up(pair + i, 1 - i)
                with act.Fori(0, more) as k:
                    blk = c + k
                    silu(blk + 1)
                    xt(blk + 2)
                    weigh(blk, e)
                    ht(blk + 1)
                if following:
                    split_down(pair + i, 1 - i)
                    silu(c + more + 1)
                    xt(c + more + 2)
                weigh(c + more, e)

            each_expert(act, expert)

        @block.vector
        def _(dve):
            chain = S["chain"]

            def newton(b, job, src, scale, eps, w=4):
                n = b * RS_ALL * 4 + job * 4
                dve.wait_ge(S["rs_seed"], b * RS_ALL + job + 1)
                dve.tensor_scalar(rs_x[:, 0:w], src, scale, eps, ALU.mult, ALU.add).then_inc(S["nw"], 1)
                dve.tensor_tensor(rs_t[:, 0:w], rs_y[:, 0:w], rs_y[:, 0:w], ALU.mult).then_inc(S["nw"], 1)
                dve.wait_ge(S["nw"], n + 2)
                dve.scalar_tensor_tensor(out=rs_t[:, 0:w], in0=rs_t[:, 0:w], scalar=-0.5, in1=rs_x[:, 0:w], op0=ALU.mult, op1=ALU.mult).then_inc(S["nw"], 1)
                dve.wait_ge(S["nw"], n + 3)
                dve.scalar_tensor_tensor(out=rs_r[:, 0:w], in0=rs_t[:, 0:w], scalar=1.5, in1=rs_y[:, 0:w], op0=ALU.add, op1=ALU.mult).then_inc(S["nw"], 1)
                dve.wait_ge(S["nw"], n + 4)

            def stats(b, ln, src, ready=None):
                n = b * LN_ALL * TT + ln * TT
                for t in range(TT):
                    if ready:
                        ready(t)
                    dve.bn_stats(st[:, t, :], src(t)).then_inc(S["bn_ok"], 1)
                for t in range(TT):
                    wait_apart(dve, S["bn_ok"], n + t + 1)
                    dve.bn_aggr(mv[:, t, :], st[:, t, :]).then_inc(S["ag_ok"], 1)
                dve.wait_ge(S["ag_ok"], n + TT)

            def apply(t, dst, src):
                return dve.tensor_scalar(dst, src, mv[:, t, 0:1], rs_r[:, t:t + 1], ALU.subtract, ALU.mult)

            dve.memset(v_aug[:, :, DH:], 1.0).then_inc(S["bc_free"], 1)
            dve.memset(cs[:, 0, :], 0.0).then_inc(S["dve_step"], 1)
            dve.wait_ge(S["w_in_sb"], 16 * N_W)
            dve.wait_ge(S["dve_step"], 1)

            N_CHAIN = [0]
            chain_per_row = CHAIN

            with dve.Fori(0, NB) as b:
                N_CHAIN[0] = 0

                def link(ins, apart=False):
                    N_CHAIN[0] += 1
                    ins.then_inc(chain, 1)
                    if apart:
                        wait_apart(dve, chain, b * chain_per_row + N_CHAIN[0])
                    else:
                        dve.wait_ge(chain, b * chain_per_row + N_CHAIN[0])

                link(dve.memset(x_pad[:, :, 0:DC - 1], 0.0))
                dve.wait_ge(S["x_in"], b * 16 + 16)
                stats(b, LN1, lambda t: x_sb[:, t, :])
                newton(b, RS_LN1, mv[:, :, 1], 1.0, EPS_LN)
                dve.wait_ge(S["fT_ok"], b * KT)
                dve.wait_ge(S["lg_ps"], b)
                for t in range(TT):
                    apply(t, norm[:, t, :], x_sb[:, t, :]).then_inc(S["ln_a"], 1)
                stats(b, LN2, lambda t: norm[:, t, :], ready=lambda t: dve.wait_ge(S["ln_a"], b * TT + t + 1))
                newton(b, RS_LN2, mv[:, :, 1], 1.0, EPS_LN)
                for t in range(TT):
                    apply(t, norm[:, t, :], norm[:, t, :]).then_inc(S["ln_x"], 1)
                for c in range(DC):
                    for e in range(ET):
                        if c == 0:
                            dve.wait_ge(S["xpad_ok"], b * ET + e + 1)
                            ins = dve.tensor_scalar(dbu[:, e, :], x_pad[:, e, 0:T], conv_w[:, e, 0:1], None, ALU.mult)
                        else:
                            dve.wait_ge(S["conv_ok"], b * ET * DC + (c - 1) * ET + e + 1)
                            ins = dve.scalar_tensor_tensor(out=dbu[:, e, :], in0=x_pad[:, e, c:c + T], scalar=conv_w[:, e, c:c + 1], in1=dbu[:, e, :],
                                                           op0=ALU.mult, op1=ALU.add)
                        ins.then_inc(S["conv_ok"], 1)
                newton(b, RS_K, rs_in[:], 1 / SCALE, EPS_L2 / SCALE)
                for half in range(2):
                    dve.wait_ge(S["v_ok"], b * 2 + half + 1)
                    dve.tensor_tensor(k_n[:, 2 * half:2 * half + 2, :], bank_o[half][:, :].rearrange("p (t n) -> p t n", t=2)[:, :, 0:DH],
                                      rs_r[:, 2 * half:2 * half + 2].unsqueeze(2).to_broadcast([P, 2, DH]), ALU.mult).then_inc(S["kn_ok"], 1)

                def q_norm(group, t):
                    dve.wait_ge(S["qss_ok"], b * H * 4 + group * 16 + (t * 4 + 4))
                    newton(b, group * 4 + (t + RS_Q0), rs_in[:], 1 / 16, EPS_L2 / 4096)
                    dve.wait_ge(S["qT_ps"], b * H + group * 4)
                    dve.tensor_tensor(q_s[:, t, :, :], bank_q[t % 2][:, :].rearrange("p (j d) -> p j d", j=4),
                                      rs_r[:].unsqueeze(2).to_broadcast([P, 4, DH]), ALU.mult).then_inc(S["q_ok"], 1)

                for t in range(TT):
                    q_norm(0, t)
                dve.wait_ge(S["sp_ln"], b + 1)
                link(dve.tensor_scalar(dbu[:], dA3, 1.0, -1.0, ALU.add, ALU.add))
                link(dve.tensor_tensor(dbu[:], dA3, dbu[:], ALU.subtract))
                link(dve.tensor_tensor(dbu[:], dbu[:], y[:], ALU.add))
                link(dve.tensor_tensor(delta[:], delta[:], dbu[:], ALU.add))
                dve.tensor_tensor(du[:], delta[:], state[:], ALU.mult)
                for e in range(ET):
                    dve.tensor_scalar(y[:, e, :], state[:, e, :], d_skip[:, e:e + 1], None, ALU.mult)
                link(dve.memset(dA3[:, :, 0:1], 0.0))
                dve.memset(rs_t[:, 0:1], 0.0).then_inc(S["dve_step"], 1)

                def head(h, group, j, last_group):
                    i = j % 2
                    bc = lambda t: t[:, i:i + 1, :].to_broadcast([P, ET, T])
                    dve.wait_ge(S[f"bc_in{i}"], b * (DS // 2) * 32 + group * 64 + (j // 2 * 32 + 32))
                    dve.tensor_tensor(dbu[:], du[:], bc(b_bc), ALU.mult).then_inc(S["dbu_ok"], 1)
                    if not last_group:
                        q_norm(group + 1, j)
                    dve.wait_ge(S["dA_ok"], b * DS * ET + h * ET + ET)
                    dve.wait_ge(S["dbu_ok"], b * DS + h + 1)
                    dve.tensor_tensor_scan(state[:].rearrange("p e t -> p (e t)"), dA, dbu[:].rearrange("p e t -> p (e t)"), 0.0,
                                           ALU.mult, ALU.add).then_inc(S["scan_ok"], 1)
                    dve.wait_ge(S["oT_ps"], b * H + h)
                    for half in range(2):
                        o = bank_o[half][:, 0:2 * (DH + 1)].rearrange("p (t n) -> p t n", t=2)
                        dve.wait_ge(S["pv_ps"], b * H * 2 + h * 2 + (half + 1))
                        dve.reciprocal(den[:, 2 * half:2 * half + 2].unsqueeze(2), o[:, :, DH:]).then_inc(S["den_ok"], 1)
                        dve.wait_ge(S["den_ok"], b * H * 2 + h * 2 + (half + 1))
                        dve.tensor_tensor(o_s[:, 2 * half:2 * half + 2, :], o[:, :, 0:DH], den[:, 2 * half:2 * half + 2].unsqueeze(2).to_broadcast([P, 2, DH]),
                                          ALU.mult).then_inc(S["o_ok"], 1)
                    dve.wait_ge(S["scan_ok"], b * DS + h + 1)
                    dve.tensor_tensor(dbu[:], state[:], bc(c_bc), ALU.mult).then_inc(S["bc_free"], 1)
                    dve.wait_ge(S["bc_free"], b * DS + h + 2)
                    dve.tensor_tensor(y[:], y[:], dbu[:], ALU.add).then_inc(S["y_ok"], 1)
                    dve.wait_ge(S["y_ok"], b * DS + h + 1)

                with dve.Fori(0, G - 1) as g:
                    for j in range(4):
                        head(g * 4 + j, g, j, False)
                for j in range(4):
                    head((G - 1) * 4 + j, G - 1, j, True)

                stats(b, LNO, lambda t: (bank_o + bank_s)[t][:], ready=lambda t: dve.wait_ge(S["op_ps"], b * TT + t + 1))
                newton(b, RS_O, mv[:, :, 1], 1.0, EPS_LN)
                for t in range(TT):
                    apply(t, norm[:, t, :], (bank_o + bank_s)[t][:]).then_inc(S["on_ok"], 1)
                dve.wait_ge(S["on_ok"], b * TT + TT)
                link(dve.tensor_tensor(norm[:], norm[:], g_out[:].unsqueeze(1).to_broadcast([P, TT, D]), ALU.mult))
                link(dve.tensor_tensor(x_sb[:], x_sb[:], norm[:], ALU.add))
                stats(b, LNZ, lambda t: x_sb[:, t, :])
                newton(b, RS_Z, mv[:, :, 1], 1.0, EPS_LN)
                dve.scalar_tensor_tensor(out=z_bias[:], in0=mv[:, :, 0], scalar=-1.0, in1=rs_r[:], op0=ALU.mult, op1=ALU.mult).then_inc(S["zr_ok"], 1)
                dve.wait_ge(S["sz_ok"], b * TT + TT)
                dve.tensor_tensor(y[:], y[:], norm[:], ALU.mult).then_inc(S["ys_ok"], 1)
                for t in range(TT):
                    dve.wait_ge(S["yT_ps"], b * TT + t + 1)
                    dve.tensor_tensor(x_sb[:, t, :], x_sb[:, t, :], bank_q[t % 2][:], ALU.add).then_inc(S["x2_ok"], 1)
                stats(b, LNF, lambda t: x_sb[:, t, :], ready=lambda t: dve.wait_ge(S["x2_ok"], b * TT + t + 1))
                newton(b, RS_F, mv[:, :, 1], 1.0, EPS_LN)
                dve.wait_ge(S["sent"], b * TT * 8 * 16)
                for t in range(TT):
                    apply(t, x_row[:, t, 0:D], x_sb[:, t, :]).then_inc(S["xf_ok"], 1)
                link(dve.tensor_copy(x_row[:, :, ID_COL:ID_COL + 1].bitcast(I32), const[:, bass.ds(b * TT + C_TOK, TT)].unsqueeze(2)))
                link(dve.memset(x_row[:, :, ID_COL + 1:], 0.0))

                wide = lambda t: t[:].unsqueeze(2).to_broadcast([P, TT, NE])
                exp_row = lambda c: const[:, c:c + NE].unsqueeze(1).to_broadcast([P, TT, NE])
                tt, ts = dve.tensor_tensor, dve.tensor_scalar
                red = lambda dst, src, op: link(dve.tensor_reduce(r1[dst][:].unsqueeze(2), src, AX, op))
                dve.wait_ge(S["lg_ps"], b + 1)
                logits = bank_o[0][:, 0:TT * NE].rearrange("p (t e) -> p t e", t=TT)
                red("mx", logits, ALU.max)
                tt(r["lg"][:], logits, wide(r1["mx"]), ALU.subtract).then_inc(S["lgs_ok"], 1)
                dve.wait_ge(S["rexp_ok"], b + 1)
                red("sm", r["pr"][:], ALU.add)
                link(dve.reciprocal(r1["rc"][:], r1["sm"][:]))
                link(tt(r["pr"][:], r["pr"][:], wide(r1["rc"]), ALU.mult), True)
                for t in range(TT):
                    link(dve.max(p8[:, t, :], r["pr"][:, t, :]), True)
                    link(dve.match_replace(r["rep"][:, t, :], p8[:, t, :], r["pr"][:, t, :], -1.0), t < TT - 1)
                red("s8", p8[:], ALU.add)
                link(ts(r1["s8"][:], r1["s8"][:], 1e-12, None, ALU.max))
                link(dve.reciprocal(r1["r8"][:], r1["s8"][:]))
                link(ts(r["sel"][:], r["rep"][:], 0.0, None, ALU.is_lt))
                link(tt(r["tvn"][:], r["pr"][:], r["sel"][:], ALU.mult))
                link(tt(r["tvn"][:], r["tvn"][:], wide(r1["r8"]), ALU.mult))
                link(ts(r["scl"][:], r["tvn"][:], alpha[:, 0:1], None, ALU.mult))
                link(dve.scalar_tensor_tensor(out=r["act"][:], in0=r["scl"][:], scalar=TAU, in1=r["sel"][:], op0=ALU.is_ge, op1=ALU.mult))
                red("any", r["act"][:], ALU.max)
                link(ts(r["ct"][:], r["sel"][:], 3.0e38, -3.0e38, ALU.mult, ALU.add))
                link(tt(r["scl"][:], r["scl"][:], r["ct"][:], ALU.add))
                red("mx2", r["scl"][:], ALU.max)
                link(tt(r["cand"][:], r["scl"][:], wide(r1["mx2"]), ALU.is_equal))
                link(tt(r["ct"][:], r["tvn"][:], r["cand"][:], ALU.mult))
                link(dve.scalar_tensor_tensor(out=r["ct"][:], in0=r["cand"][:], scalar=-1.0, in1=r["ct"][:], op0=ALU.add, op1=ALU.add))
                red("m2", r["ct"][:], ALU.max)
                link(tt(r["cand"][:], r["ct"][:], wide(r1["m2"]), ALU.is_equal))
                link(tt(r["fb"][:], r["cand"][:], exp_row(C_REV), ALU.mult))
                red("m3", r["fb"][:], ALU.max)
                link(tt(r["fb"][:], r["fb"][:], wide(r1["m3"]), ALU.is_equal))
                link(ts(r1["any"][:], r1["any"][:], -1.0, 1.0, ALU.mult, ALU.add))
                link(tt(r["fb"][:], r["fb"][:], wide(r1["any"]), ALU.mult))
                link(tt(r["act"][:], r["act"][:], r["fb"][:], ALU.max))
                for t in range(TT - 1):
                    link(tt(cs[:, t + 1, :], cs[:, t, :], r["act"][:, t, :], ALU.add))
                tt(cs[:, TT, :], cs[:, TT - 1, :], r["act"][:, TT - 1, :], ALU.add).then_inc(S["act_ok"], 1)
                link(tt(r["wts"][:], r["tvn"][:], r["act"][:], ALU.mult))
                red("s2", r["wts"][:], ALU.add)
                link(ts(r1["s2"][:], r1["s2"][:], 1e-12, None, ALU.max))
                link(dve.reciprocal(r1["rw"][:], r1["s2"][:]))
                link(tt(x_row[:, :, W_COL:W_COL + NE], r["wts"][:], wide(r1["rw"]), ALU.mult))
                dve.wait_ge(S["rank_ps"], b + 1)
                link(tt(r["slv"][:], bank_o[1][:, 0:TT * NE].rearrange("p (t e) -> p t e", t=TT), exp_row(C_BASE), ALU.add))
                link(tt(r["slv"][:], r["slv"][:], r["act"][:], ALU.mult))
                link(dve.tensor_copy(cs[:, 0, :], cs[:, TT, :]), True)
                for t in range(TT):
                    link(dve.max(s8[:, t, :], r["slv"][:, t, :]), t < TT - 1)
                link(ts(t8[:], s8[:], 0.0, const[:, C_TRASH:C_TRASH + 1], ALU.is_equal, ALU.mult))
                link(dve.scalar_tensor_tensor(out=t8[:], in0=t8[:], scalar=-1.0, in1=s8[:], op0=ALU.add, op1=ALU.add))
                dve.tensor_copy(slot[:], t8[:]).then_inc(S["slot_ok"], 1)
                dve.wait_ge(S["slot_ok"], b + 1)
            print("chain", N_CHAIN[0])
            assert N_CHAIN[0] == chain_per_row, N_CHAIN[0]

            xt_bank, gu_bank, ht_bank = bank_q[0], bank_s[0], bank_s[1]
            steps = [0]

            def step(ins):
                steps[0] += 1
                ins.then_inc(S["cnt_step"], 1)
                dve.wait_ge(S["cnt_step"], steps[0])

            step(dve.memset(pad[:], 0.0))
            step(dve.tensor_copy(pad[:, ID_COL:ID_COL + 1].bitcast(I32), const[:, C_PAD:C_PAD + 1]))
            dve.wait_ge(S["cnt_ps"], 1)
            step(dve.tensor_copy(n_f[:], bank_q[1][:, 0:NE]))
            step(dve.tensor_scalar(nb_f[:], n_f[:], float((MIN_BLK - 1) * P + 1), float(P - 1), ALU.max, ALU.add))
            step(dve.tensor_copy(nb_i[:], nb_f[:]))
            step(dve.tensor_scalar(nb_i[:], nb_i[:], P.bit_length() - 1, None, ALU.arith_shift_right))
            step(dve.tensor_copy(nb_f[:], nb_i[:]))
            step(dve.tensor_tensor_scan(cum_f[:], ones[:, 0:NE], nb_f[:], 0.0, ALU.mult, ALU.add))
            step(dve.tensor_copy(odd_i[:], cum_f[:, NE - 1:NE]))
            step(dve.tensor_scalar(odd_i[:], odd_i[:], 1, None, ALU.bitwise_and))
            step(dve.tensor_copy(odd_f[:], odd_i[:]))
            step(dve.tensor_tensor(cum_f[:], cum_f[:], nb_f[:], ALU.subtract))
            step(dve.tensor_tensor(nb_f[:, NE - 1:NE], nb_f[:, NE - 1:NE], odd_f[:], ALU.add))
            step(dve.tensor_tensor(odd_f[:], nb_f[:, NE - 1:NE], cum_f[:, NE - 1:NE], ALU.add))
            step(dve.tensor_scalar(odd_f[:], odd_f[:], 0.5, None, ALU.mult))
            step(dve.tensor_scalar(nb_f[:], nb_f[:], -1.0, None, ALU.add))
            for k, col in enumerate((nb_f, cum_f, n_f)):
                step(dve.tensor_copy(tab[:, k * NE:(k + 1) * NE], col[:]))
            dve.tensor_copy(tab[:, 3 * NE:], odd_f[:]).then_inc(S["tab_ok"], 1)
            dve.wait_ge(S["tab_ok"], 1)

            def split_gate_up(e, i):
                dve.wait_ge(S["guhi_ok"], e + 1)
                dve.tensor_tensor(gu_lo[i][:], gu_w[i][:], gu_hi[i][:].bitcast(F32), ALU.subtract).then_inc(S["gulo_ok"], 1)

            def split_down(e, i):
                dve.wait_ge(S["dnhi_ok"], e + 1)
                dve.tensor_tensor(dn_lo[i][:], dn_w[i][:], dn_hi[i][:].bitcast(F32), ALU.subtract).then_inc(S["dnlo_ok"], 1)

            def xt(blk):
                dve.wait_ge(S["xthi_ok"], blk + 1)
                dve.tensor_tensor(xt_lo[:], xt_bank[:].rearrange("p (k t) -> p k t", k=KT), xt_hi[:].bitcast(F32), ALU.subtract).then_inc(S["xtlo_ok"], 1)

            def hidden(blk):
                half = P // 2
                dve.wait_ge(S["silu_ok"], blk + 1)
                dve.tensor_tensor(h_sb[:, 0:P], silu_g[:, 0:P], gu_bank[:, INTER:INTER + P], ALU.mult).then_inc(S["h_ok"], 1)
                twice = lambda t: t.unsqueeze(1).to_broadcast([P, 2, half])
                dve.tensor_tensor(h_sb[:, P:].rearrange("p (o c) -> p o c", o=2), twice(silu_g[:, P:]), twice(gu_bank[:, INTER + P:2 * INTER]),
                                  ALU.mult).then_inc(S["h_ok"], 1)

            def ht(blk):
                half = P // 2
                dve.wait_ge(S["hthi_ok"], blk + 1)
                dve.tensor_tensor(ht_lo[:], ht_bank[:, 0:P], ht_hi[:, 0:P].bitcast(F32), ALU.subtract).then_inc(S["htlo_ok"], 1)
                dve.tensor_tensor(ht_hi[half:, P:], ht_bank[half:, P:2 * P], ht_hi[half:, P:].bitcast(F32), ALU.subtract).then_inc(S["htlo_ok"], 1)

            split_gate_up(0, 0)
            split_down(0, 0)
            xt(0)
            hidden(0)
            xt(1)

            def expert(pair, i, after_next=True, following=True):
                e = pair * 2 + i
                more, c = span(dve, e)
                ht(c)
                if following:
                    split_gate_up(e + 1, 1 - i)
                with dve.Fori(0, more) as k:
                    blk = c + k
                    hidden(blk + 1)
                    xt(blk + 2)
                    ht(blk + 1)
                if following:
                    split_down(e + 1, 1 - i)
                    hidden(c + more + 1)
                    xt(c + more + 2)

            each_expert(dve, expert)

        @block.gpsimd
        def _(pool):
            with pool.Fori(0, NB) as b:
                wait_apart(pool, S["slot_ok"], b + 1)
                for t in range(TT):
                    for k in range(TOPK):
                        if t + k > 0:
                            wait_apart(pool, S["sent"], b * TT * TOPK * 16 + (t * TOPK + k) * 16)
                        pool.indirect_dma_start(out=slots, out_offset=bass.IndirectOffsetOnAxis(ap=slot[:, t, k:k + 1].bitcast(U32), axis=0),
                                                in_=x_row[:, t, :], in_offset=None).then_inc(S["sent"], 16)

            pool.wait_ge(S["tab_ok"], 1)
            pairs = pool.value_load(tab[0:1, 3 * NE:3 * NE + 1], min_val=NE, max_val=MAX_BLK // 2 + 1)
            pool.dma_start(out[NTOK:, :], pad[:, 0:D]).then_inc(S["added"], 16)
            with pool.Fori(0, pairs) as pair:
                for i in range(2):
                    blk = pair * 2 + i
                    pool.wait_ge(S["yb_ok"], blk + 1)
                    pool.tensor_copy(ids[i][:], meta[:, bass.ds(blk, 1), NE:].rearrange("p o c -> p (o c)").bitcast(I32)).then_inc(S["ids_ok"], 1)
                    pool.wait_ge(S["ids_ok"], blk + 1)
                    wait_apart(pool, S["added"], blk * 16 + 16)
                    pool.indirect_dma_start(out=out, out_offset=bass.IndirectOffsetOnAxis(ap=ids[i][:].bitcast(U32), axis=0),
                                            in_=y_both[:, i, :], in_offset=None, compute_op=ALU.add).then_inc(S["added"], 16)


def kernel(**inputs):
    import concourse.bacc as _bacc
    from concourse.bass_utils import run_bass_kernel_spmd as _run

    i = {k.replace("L0_", ""): np.asarray(v) for k, v in inputs.items()}
    tiles = lambda v: v.reshape(-1, P).T
    arrays = {
        "x": i["x"].reshape(NTOK, D),
        "ctx_t": i["ctx_1024"].transpose(0, 2, 1).reshape(NB * DM, T),
        "g_norm": tiles(i["attn_g_norm"]),
        "wq": i["attn_Wq"], "wkv": i["attn_Wkv"], "wout": i["attn_Wout"], "g_out": i["attn_g_out"],
        "w_in_t": i["xattn_in_proj_w"].T,
        "conv_w": i["xattn_conv_w"], "conv_b": tiles(i["xattn_conv_b"]),
        "w_x_t": i["xattn_x_proj_w"].T, "w_dt_t": i["xattn_dt_proj_w"].T, "dt_b": tiles(i["xattn_dt_proj_b"]),
        "a_log": i["xattn_A_log"].reshape(ET, P, DS).transpose(1, 2, 0), "d_skip": tiles(i["xattn_D"]),
        "w_gate_t": i["ffn_gate_weight"].T,
        "gate_up_t": i["ffn_gate_up_proj"].transpose(0, 2, 1), "down_t": i["ffn_down_proj"].transpose(0, 2, 1),
        "alpha": i["ffn_layer_alpha"].reshape(1),
        "const": constants(),
    }
    arrays = {k: np.ascontiguousarray(v) for k, v in arrays.items()}
    nc = _bacc.Bacc("TRN2", target_bir_lowering=False, num_devices=1)
    a = {k: nc.dram_tensor(f"in_{k}", v.shape, mybir.dt.from_np(v.dtype), kind="ExternalInput").ap() for k, v in arrays.items()}
    a["out"] = nc.dram_tensor("out_0", (NTOK + P, D), F32, kind="ExternalOutput").ap()
    decoder_layer(nc, a)
    res = _run(nc, [{f"in_{k}": v for k, v in arrays.items()}], core_ids=[0])
    return res.results[0]["out_0"][:NTOK].reshape(NB, T, D)
```

```python
from contextlib import ExitStack

import numpy as np

import concourse.bass as bass
from concourse import mybir

F32 = mybir.dt.float32
F32R = mybir.dt.float32r
I32 = mybir.dt.int32
U32 = mybir.dt.uint32
ALU = mybir.AluOpType
ACT = mybir.ActivationFunctionType
AX = mybir.AxisListType.X

P = 128
NB, T, D = 4, 512, 512
TT, KT = T // P, D // P
H, DH = 16, 128
G = H // 4
DM, DI, DS, DC, DR = 256, 512, 16, 4, 16
ET, MT = DI // P, DM // P
XD = DR + 2 * DS
NE, INTER, TOPK, TAU = 32, 192, 8, 0.05
NTOK = NB * T
CAP = NTOK + 3 * P
MIN_BLK = 2
LAST_BEFORE = 4 * NE + 1
GU_COLS = KT * 2 * INTER
W_EXP = GU_COLS + 2 * D
N_RAW, N_SPLIT = 4, 4
W_PARTS = ((0, W_EXP * 3 // 10), (W_EXP * 3 // 10, W_EXP))
TRASH = NE * CAP
ROW = 560
W_COL, ID_COL = D, D + NE
EPS_LN, EPS_L2 = 1e-5, 1e-12
SCALE = 16.0
EXP_SET = "natural_log_exp_and_others"

Q_LATER = [f"q{piece}" for piece in range(4, H)]
FIRST_JOBS = ["ln1", "ln2", "k", "q0", "q1", "q2", "q3"]
ROW_JOBS = Q_LATER + ["ln1", "ln2", "k", "o", "q0", "q1", "z", "f", "q2", "q3"]
LAST_JOBS = Q_LATER + ["o", "z", "f"]
FIRST_NORMS, ROW_NORMS, LAST_NORMS = ["ln1", "ln2"], ["ln1", "ln2", "o", "z", "f"], ["o", "z", "f"]
FIRST_STEPS, ROW_STEPS = 6, 62

C_ID, C_TRI, C_ONE = 0, P, 2 * P
C_BASE, C_REV, C_TRASH, C_TOK = 3 * P, 3 * P + NE, 3 * P + 2 * NE, 3 * P + 2 * NE + 1
EXP_BLK = NTOK // P + 1
MAX_BLK = NTOK * TOPK // P + MIN_BLK * NE
C_PAD = C_TOK + NB * TT
C_ALL = C_PAD + 1


class Places:

    def __init__(self, jobs, norms, job0, norm0, step0):
        self.jobs, self.norms, self.job0, self.norm0, self.step0, self.steps = jobs, norms, job0, norm0, step0, 0

    def job(self, name):
        return self.job0 + self.jobs.index(name)

    def norm(self, name):
        return self.norm0 + self.norms.index(name)


def first_places():
    return Places(FIRST_JOBS, FIRST_NORMS, 0, 0, 0)


def row_places(b, last):
    return Places(LAST_JOBS if last else ROW_JOBS, LAST_NORMS if last else ROW_NORMS,
                  b * len(ROW_JOBS) + len(FIRST_JOBS), b * len(ROW_NORMS) + len(FIRST_NORMS), b * ROW_STEPS + FIRST_STEPS)


def constants():
    c = np.zeros((P, C_ALL), np.float32)
    p = np.arange(P)
    c[:, C_ID:C_ID + P] = np.eye(P)
    c[:, C_TRI:C_TRI + P] = p[:, None] < p[None, :]
    c[:, C_ONE:C_ONE + P] = 1.0
    c[:, C_BASE:C_BASE + NE] = np.arange(NE)[None, :] * CAP + 1
    c[:, C_REV:C_REV + NE] = NE - np.arange(NE)[None, :]
    c[:, C_TRASH] = TRASH + 1 + p
    c[:, C_TOK:C_PAD] = p[:, None] + P * np.arange(NB * TT)[None, :]
    c[:, C_PAD] = NTOK + p
    return c


def decoder_layer(nc, a):
    ctx = ExitStack()
    with ctx:
        def sb(name, shape, dt=F32):
            return ctx.enter_context(nc.sbuf_tensor(name, shape, dt))

        def sem(name):
            return ctx.enter_context(nc.semaphore(name))

        def dram(name, shape):
            return nc.dram_tensor(name, shape, F32, kind="Internal").ap()

        bank = [ctx.enter_context(nc.psum_tensor(f"bank{i}", [P, 512], F32)) for i in range(8)]
        bank_q, bank_s, bank_o, bank_t = bank[0:2], bank[2:4], bank[4:6], bank[6:8]

        bc_dram = dram("bc_dram", [NB, 2 * DS, T])
        slots = dram("slots", [TRASH + P, ROW])

        out = a["out"]

        x_sb = sb("x_sb", [P, TT, D])
        x_row = sb("x_row", [P, TT, ROW])
        slot = sb("slot", [P, TT, 8], I32)
        cs = sb("cs", [P, TT + 1, NE])
        const = sb("const", [P, C_ALL])
        ident, tri, ones = const[:, C_ID:C_ID + P], const[:, C_TRI:C_TRI + P], const[:, C_ONE:C_ONE + P]

        stage_a = ExitStack()
        def sb(name, shape, dt=F32):
            return stage_a.enter_context(nc.sbuf_tensor(name, shape, dt))

        wq = sb("wq", [P, KT, H * DH])
        wkv = sb("wkv", [P, KT, 2 * DH])
        w_in = sb("w_in", [P, MT, DI])
        w_x = sb("w_x", [P, ET, XD])
        w_dt = sb("w_dt", [DR, DI])
        w_gate = sb("w_gate", [P, KT, NE])
        g_norm = sb("g_norm", [P, KT])
        g_out = sb("g_out", [P, D])
        conv_w = sb("conv_w", [P, ET, DC])
        conv_b = sb("conv_b", [P, ET])
        dt_b = sb("dt_b", [P, ET])
        d_skip = sb("d_skip", [P, ET])
        neg_a = sb("neg_a", [P, DS, ET])
        alpha = sb("alpha", [P, 1])

        ctx_t = sb("ctx_t", [P, MT, T])
        xn_t = sb("xn_t", [P, KT, T])
        k_t = sb("k_t", [P, T])
        v_aug = sb("v_aug", [P, TT, DH + 1])
        q_s = sb("q_s", [P, TT, 4, DH])
        q_t = sb("q_t", [P, 4, T])
        probs = sb("probs", [P, KT, T])
        o_s = sb("o_s", [P, TT, DH])
        k_n = o_s
        o_t = sb("o_t", [P, H, T])
        wout = sb("wout", [P, 4, D])
        delta = sb("delta", [P, ET, T])
        du = sb("du", [P, ET, T])
        y = sb("y", [P, ET, T])
        decay = sb("decay", [P, ET * (T + DC - 1)])
        x_pad = decay[:, :].rearrange("p (e t) -> p e t", e=ET)
        dA = decay[:, 0:ET * T]
        dA3 = dA.rearrange("p (e t) -> p e t", e=ET)
        dbu = sb("dbu", [P, ET, T])
        state = sb("state", [P, ET, T])
        b_bc = sb("b_bc", [P, 2, T])
        c_bc = sb("c_bc", [P, 2, T])
        x_dbl = sb("x_dbl", [XD, T])
        junk = sb("junk", [P, 4, DH], mybir.dt.bfloat16)
        norm = probs
        x_first = q_s[:].rearrange("p t j d -> p t (j d)")
        end_s = o_t[:, 4:8, :]
        st = sb("st", [P, TT, 6])
        mv = sb("mv", [P, TT, 2])
        rs_in = sb("rs_in", [P, 4])
        rs_x = sb("rs_x", [P, 4])
        rs_l = sb("rs_l", [P, 4])
        rs_y = sb("rs_y", [P, 4])
        rs_t = sb("rs_t", [P, 4])
        rs_r = sb("rs_r", [P, 4])
        z_bias = sb("z_bias", [P, TT])
        den = sb("den", [P, TT])
        NAMES = ["lg", "pr", "rep", "sel", "tvn", "scl", "act", "cand", "ct", "fb", "wts", "slv"]
        r = {n: o_t[:].rearrange("p h t -> p (h t)")[:, i * TT * NE:(i + 1) * TT * NE].rearrange("p (t e) -> p t e", t=TT)
             for i, n in enumerate(NAMES)}
        p8 = sb("p8", [P, TT, 8])
        s8 = sb("s8", [P, TT, 8])
        t8 = sb("t8", [P, TT, 8])
        r1 = {n: sb("r1_" + n, [P, TT]) for n in ["mx", "sm", "rc", "s8", "r8", "any", "mx2", "m2", "m3", "s2", "rw"]}

        stage_a.close()

        def sb(name, shape, dt=F32):
            return ctx.enter_context(nc.sbuf_tensor(name, shape, dt))

        w_raw = sb("w_raw", [P, N_RAW, W_EXP])
        w_hi = sb("w_hi", [P, N_SPLIT, W_EXP], F32R)
        w_lo = sb("w_lo", [P, N_SPLIT, W_EXP], F32R)
        x_blk = sb("x_blk", [P, D])
        meta = sb("meta", [P, MAX_BLK + EXP_BLK + 1, NE + 1])
        ids = [sb(f"ids{i}", [P, 1], I32) for i in range(2)]
        xt_hi, xt_lo = sb("xt_hi", [P, KT, P], F32R), sb("xt_lo", [P, KT, P], F32R)
        silu_g = sb("silu_g", [P, INTER])
        h_sb = sb("h_sb", [P, 2 * P])
        ht_hi = sb("ht_hi", [P, 2 * P], F32R)
        ht_lo = sb("ht_lo", [P, P], F32R)
        y_both = sb("y_both", [P, 2, D])
        pad = sb("pad", [P, ROW])
        n_f, nb_f, cum_f = sb("n_f", [P, NE]), sb("nb_f", [P, NE]), sb("cum_f", [P, NE])
        second_f = sb("second_f", [P, NE])
        nb_i = sb("nb_i", [P, NE], I32)
        odd_i, odd_f = sb("odd_i", [P, 1], I32), sb("odd_f", [P, 1])
        tab = sb("tab", [P, 5 * NE + 2], I32)

        S = {n: sem(n) for n in """
            w_in_sb x_in xfirst_in ctx_in bc_written bc_in0 bc_in1 wout_in0 wout_in1 wout_in2 wout_in3 x2_out
            inp_ps xT_ps kv_ps kT_ps qp_ps qT_ps s_ps pv_ps oT_ps xd_ps dt_ps wout_used op_ps yT_ps fT_ps lg_ps rank_ps
            neg_a_ok act_step rs_ln rs_seed xpad_ok xnT_ok ksq_ok v_ok kT_ok u_ok xd_ok dt_ev sp_e sp_ln qss_ok qT_ok
            exp_ok dA_ok oT_ok sz_ok fT_ok rexp_ok
            dve_step bn_ok ag_ok nw ln_a ln_x conv_ok kn_ok q_ok scan_ok bc_free o_ok on_ok x1_ok zr_ok ys_ok x2_ok xf_ok dbu_ok den_ok y_ok chain
            lgs_ok act_ok slot_ok
            sent
            w_in pad_out blk_in
            cnt_ps xt_ps gu_ps ht_ps y_ps
            whi_ok xthi_ok silu_ok hthi_ok yb_ok
            pad_ok cnt_step tab_ok wlo_ok xtlo_ok h_ok htlo_ok
            ids_ok added
            """.split()}

        N_W = 15
        STATES_IN_LAST_GROUP = {0: DS - 4, 2: DS - 3}
        block = ctx.enter_context(nc.Block())

        def wait_apart(eng, semaphore, value):
            if isinstance(value, int):
                eng.wait_ge(semaphore, value)
                return
            count = eng.to_reg(value)
            eng.wait_ge(S["w_in_sb"], 16 * N_W)
            eng.wait_ge(semaphore, count)

        def span(eng, e):
            return (eng.value_load(tab[0:1, bass.ds(e, 1)], min_val=MIN_BLK - 1, max_val=EXP_BLK - 1),
                    eng.value_load(tab[0:1, bass.ds(e + NE, 1)], min_val=0, max_val=MAX_BLK))

        def each_row(eng, row):
            with eng.Fori(0, NB - 1) as b:
                row(b, row_places(b, False), False)
            row(NB - 1, row_places(NB - 1, True), True)

        def gate_up_w(w, e):
            return w[:, bass.ds(e % N_SPLIT, 1), 0:GU_COLS].rearrange("p o (k n) -> p (o k) n", k=KT)

        def down_w(w, e):
            return w[:, bass.ds(e % N_SPLIT, 1), GU_COLS:].rearrange("p o (r d) -> p (o r) d", r=2)

        def part_w(w, e, part, ring):
            return w[:, bass.ds(e % ring, 1), W_PARTS[part][0]:W_PARTS[part][1]].rearrange("p o n -> p (o n)")

        @block.sync
        def _(sp):
            def load(dst, src):
                sp.dma_start(dst, src).then_inc(S["w_in_sb"], 16)

            load(const[:], a["const"])
            load(w_in[:], a["w_in_t"].rearrange("(m p) e -> p m e", p=P))
            load(conv_w[:], a["conv_w"].rearrange("(e p) c -> p e c", p=P))
            load(conv_b[:], a["conv_b"])
            load(dt_b[:], a["dt_b"])
            load(d_skip[:], a["d_skip"])
            load(neg_a[:], a["a_log"])
            load(g_norm[:], a["g_norm"])
            load(w_x[:], a["w_x_t"].rearrange("(e p) k -> p e k", p=P))
            load(w_dt[:], a["w_dt_t"])
            load(wkv[:], a["wkv"].rearrange("(k p) n -> p k n", p=P))
            load(wq[:], a["wq"].rearrange("(k p) n -> p k n", p=P))
            load(w_gate[:], a["w_gate_t"].rearrange("(k p) n -> p k n", p=P))
            load(g_out[:], a["g_out"].partition_broadcast(P))
            sp.dma_start(alpha[:], a["alpha"].partition_broadcast(P)).then_inc(S["w_in_sb"], 16)

            def load_first(r):
                sp.dma_start(x_first, a["x"][bass.ds(r * T, T), :].rearrange("(t p) d -> p t d", p=P)).then_inc(S["xfirst_in"], 16)
                wait_apart(sp, S["inp_ps"], r * ET)
                sp.dma_start(ctx_t[:], a["ctx_t"][bass.ds(r * DM, DM), :].rearrange("(m p) l -> p m l", p=P)).then_inc(S["ctx_in"], 16)

            def load_x(r):
                sp.dma_start(x_sb[:], a["x"][bass.ds(r * T, T), :].rearrange("(t p) d -> p t d", p=P)).then_inc(S["x_in"], 16)

            def load_wout(h):
                sp.dma_start(wout[:, h % 4, :], a["wout"][h * DH:(h + 1) * DH, :]).then_inc(S[f"wout_in{h % 4}"], 16)

            def write_bc(r):
                wait_apart(sp, S["xd_ok"], r + 1)
                sp.dma_start(bc_dram[bass.ds(r, 1)].rearrange("o n t -> (o n) t"), x_dbl[DR:XD, :]).then_inc(S["bc_written"], 16)

            def load_bc(r, n):
                for i in range(2):
                    wait_apart(sp, S["bc_free"], r * DS + n + i)
                    for dst, row in ((b_bc, 0), (c_bc, DS)):
                        src = bc_dram[bass.ds(r, 1), bass.ds(n + (row + i), 1), :].rearrange("o n t -> (o n t)")
                        sp.dma_start(dst[:, i, :], src.partition_broadcast(P)).then_inc(S[f"bc_in{i}"], 16)

            load_first(0)
            load_x(0)
            for h in range(4):
                load_wout(h)
            write_bc(0)

            def row(b, at, last):
                wait_apart(sp, S["bc_written"], b * 16 + 16)
                with sp.Fori(0, DS // 2 - 1) as pair:
                    load_bc(b, pair * 2)
                if not last:
                    wait_apart(sp, S["qT_ps"], b * H + H)
                    load_first(b + 1)
                load_bc(b, DS - 2)
                for h in range(4, H):
                    sp.wait_ge(S["wout_used"], b * (H - 1) + (h - 3))
                    load_wout(h)
                if not last:
                    sp.wait_ge(S["op_ps"], b * TT + TT)
                    for h in range(4):
                        load_wout(h)
                    write_bc(b + 1)
                wait_apart(sp, S["x2_ok"], b * TT + TT)
                sp.dma_start(out[bass.ds(b * T, T), :].rearrange("(t p) d -> p t d", p=P), x_sb[:]).then_inc(S["x2_out"], 16)
                if not last:
                    sp.wait_ge(S["xf_ok"], b * TT + TT)
                    wait_apart(sp, S["x2_out"], b * 16 + 16)
                    load_x(b + 1)

            each_row(sp, row)

            def pad_expert(e):
                n = sp.value_load(tab[0:1, bass.ds(e + 2 * NE, 1)], min_val=0, max_val=NTOK)
                sp.dma_start(slots[bass.ds(e * CAP + n, P), :], pad[:]).then_inc(S["pad_out"], 16)

            def load_block(row, blk):
                sp.dma_start(x_blk[:], slots[bass.ds(row, P), 0:D]).then_inc(S["blk_in"], 16)
                sp.dma_start(meta[:, bass.ds(blk, 1), :].rearrange("p o c -> p (o c)"), slots[bass.ds(row, P), W_COL:ID_COL + 1]).then_inc(S["blk_in"], 16)

            sp.wait_ge(S["tab_ok"], 1)
            sp.wait_ge(S["sent"], NB * TT * TOPK * 16)
            for e in range(3):
                pad_expert(e)
            n = sp.value_load(tab[0:1, 3 * NE - 1:3 * NE], min_val=0, max_val=NTOK)
            for t in range(1, 3):
                sp.dma_start(slots[bass.ds(n + (NE - 1) * CAP + t * P, P), :], pad[:]).then_inc(S["pad_out"], 16)
            sp.wait_ge(S["x2_out"], NB * 16)
            sp.wait_ge(S["pad_out"], 5 * 16)
            load_block(0, 0)
            with sp.Fori(0, NE) as e:
                more, c = span(sp, e)
                second = sp.value_load(tab[0:1, bass.ds(e + 3 * NE, 1)], min_val=0, max_val=P)
                with sp.Fori(0, more) as k:
                    wait_apart(sp, S["xt_ps"], c + k + 1)
                    load_block(e * CAP + second + k * P, c + k + 1)
                sp.wait_ge(S["pad_out"], e * 16 + 80)
                wait_apart(sp, S["xt_ps"], c + more + 1)
                load_block((e + 1) % NE * CAP, c + more + 1)
                pad_expert((e + 3) % NE)
            pairs = sp.value_load(tab[0:1, 4 * NE:4 * NE + 1], min_val=NE, max_val=MAX_BLK // 2 + 1)
            wait_apart(sp, S["xt_ps"], pairs * 2 + 1)
            load_block(0, pairs * 2 + 1)
            sp.wait_ge(S["blk_in"], pairs * 64 + 64)
            sp.wait_ge(S["w_in"], (NE + 4) * 2 * 16)
            sp.wait_ge(S["pad_out"], (NE + 5) * 16)
            wait_apart(sp, S["added"], pairs * 32 + 16)

        @block.tensor
        def _(pe):
            def transpose(out, src):
                return pe.transpose(out, src, ident)

            pe.wait_ge(S["w_in_sb"], 16 * N_W)

            def norm_transposes(r):
                pe.wait_ge(S["ln_x"], r * TT + TT)
                pe.wait_ge(S["dt_ev"], r * ET + ET)
                for k in range(KT):
                    if k >= 2:
                        pe.wait_ge(S["xnT_ok"], r * KT + k - 1)
                    for t in range(TT):
                        mm = transpose(bank_q[k % 2][:, t * P:(t + 1) * P], norm[:, t, k * P:(k + 1) * P])
                    mm.then_inc(S["xT_ps"], 1)

            def scan_input(r, e):
                pe.wait_ge(S["ctx_in"], r * 16 + 16)
                pe.wait_ge(S["qT_ok"], r * H)
                if e >= 2:
                    pe.wait_ge(S["xpad_ok"], r * ET + e - 1)
                for m in range(MT):
                    mm = pe.matmul(bank_q[e % 2][:], w_in[:, m, e * P:(e + 1) * P], ctx_t[:, m, :], start=(m == 0), stop=(m == MT - 1))
                mm.then_inc(S["inp_ps"], 1)

            def keys_values(r):
                pe.wait_ge(S["xnT_ok"], r * KT + KT)
                pe.wait_ge(S["xd_ok"], r + 1)
                for t in range(TT):
                    for k in range(KT):
                        mm = pe.matmul(bank_t[t // 2][:, (t % 2) * 2 * DH:(t % 2 + 1) * 2 * DH], xn_t[:, k, t * P:(t + 1) * P], wkv[:, k, :],
                                       start=(k == 0), stop=(k == KT - 1))
                    mm.then_inc(S["kv_ps"], 1)

            def scan_params(r):
                pe.wait_ge(S["oT_ok"], r * H)
                pe.wait_ge(S["u_ok"], r * ET + ET)
                for e in range(ET):
                    mm = pe.matmul(bank_t[1][0:XD, :], w_x[:, e, :], state[:, e, :], start=(e == 0), stop=(e == ET - 1))
                mm.then_inc(S["xd_ps"], 1)

            def deltas(r):
                pe.wait_ge(S["xd_ok"], r + 1)
                pe.wait_ge(S["xpad_ok"], r * ET + ET)
                for e in range(ET):
                    if e >= 2:
                        pe.wait_ge(S["dt_ev"], r * ET + e - 1)
                    pe.matmul(bank_q[e % 2][:], w_dt[:, e * P:(e + 1) * P], x_dbl[0:DR, :], start=True, stop=True).then_inc(S["dt_ps"], 1)

            def q_piece(group, t):
                for k in range(KT):
                    rhs = wq[:, k, bass.ds(group * 4 * DH, 4 * DH)]
                    mm = pe.matmul(bank_q[t % 2][:], xn_t[:, k, t * P:(t + 1) * P], rhs, start=(k == 0), stop=(k == KT - 1))
                mm.then_inc(S["qp_ps"], 1)

            def first_queries(r):
                pe.wait_ge(S["xnT_ok"], r * KT + KT)
                for t in range(TT):
                    if t >= 2:
                        pe.wait_ge(S["q_ok"], r * H + t - 1)
                    q_piece(0, t)

            def key_transposes(r):
                pe.wait_ge(S["kn_ok"], r * 2 + 2)
                pe.wait_ge(S["v_ok"], r * 2 + 2)
                for t in range(TT):
                    mm = transpose(bank_t[1][:, t * P:(t + 1) * P], k_n[:, t, :])
                mm.then_inc(S["kT_ps"], 1)

            def q_transposes(r, group):
                pe.wait_ge(S["q_ok"], r * H + group * 4 + 4)
                for j in range(4):
                    if j >= 2:
                        pe.wait_ge(S["qT_ok"], r * H + group * 4 + j - 1)
                    for t in range(TT):
                        mm = transpose((bank_t[0] if j % 2 == 0 else bank_q[0])[:, t * P:(t + 1) * P], q_s[:, t, j, :])
                    mm.then_inc(S["qT_ps"], 1)

            def scores(r, h, j):
                pe.wait_ge(S["qT_ok"], r * H + h + 1)
                for k in range(KT):
                    if k >= 2:
                        pe.wait_ge(S["exp_ok"], r * H * KT + h * KT + (k - 1))
                    pe.matmul(bank_s[k % 2][:], k_t[:, k * P:(k + 1) * P], q_t[:, j, :], start=True, stop=True).then_inc(S["s_ps"], 1)

            def first_scores(r):
                pe.wait_ge(S["kT_ok"], r + 1)
                scores(r, 0, 0)

            def head(r, h, group, j, last_group):
                if not last_group:
                    pe.wait_ge(S["q_ok"], r * H + h + 3)
                    pe.wait_ge(S["qT_ok"], r * H + group * 4 + 4)
                    q_piece(group + 1, j)
                pe.wait_ge(S["exp_ok"], r * H * KT + h * KT + KT)
                pe.wait_ge(S["o_ok"], r * H * 2 + h * 2)
                for half in range(2):
                    for t in (2 * half, 2 * half + 1):
                        for k in range(KT):
                            mm = pe.matmul(bank_o[half][:, (t % 2) * (DH + 1):(t % 2 + 1) * (DH + 1)], probs[:, k, t * P:(t + 1) * P], v_aug[:, k, :],
                                           start=(k == 0), stop=(k == KT - 1))
                    mm.then_inc(S["pv_ps"], 1)
                if not (last_group and j == 3):
                    if j == 3:
                        q_transposes(r, group + 1)
                    scores(r, h + 1, (j + 1) % 4)
                pe.wait_ge(S["o_ok"], r * H * 2 + h * 2 + 2)
                pe.wait_ge(S["oT_ok"], r * H + h)
                for t in range(TT):
                    mm = transpose(bank_t[1][:, t * P:(t + 1) * P], o_s[:, t, :])
                mm.then_inc(S["oT_ps"], 1)

            def out_proj(b, h):
                pe.wait_ge(S["oT_ok"], b * H + h + 1)
                pe.wait_ge(S[f"wout_in{h % 4}"], b * G * 16 + (h // 4 * 16 + 16))
                for t in range(TT):
                    mm = pe.matmul((bank_o + bank_s)[t][:], o_t[:, h, t * P:(t + 1) * P], wout[:, h % 4, :], start=(h == 0), stop=(h == H - 1))
                    if h == H - 1:
                        mm.then_inc(S["op_ps"], 1)
                if h < H - 1:
                    mm.then_inc(S["wout_used"], 1)

            def scan_transposes(b):
                pe.wait_ge(S["on_ok"], b * TT + TT)
                pe.wait_ge(S["ys_ok"], b + 1)
                for t in range(TT):
                    if t >= 2:
                        pe.wait_ge(S["x2_ok"], b * TT + t - 1)
                    for e in range(ET):
                        mm = transpose(bank_s[t % 2][:, e * P:(e + 1) * P], y[:, e, t * P:(t + 1) * P])
                    mm.then_inc(S["yT_ps"], 1)

            def logits(b):
                pe.wait_ge(S["xf_ok"], b * TT + TT)
                for k in range(KT):
                    if k >= 2:
                        pe.wait_ge(S["fT_ok"], b * KT + k - 1)
                    for t in range(TT):
                        mm = transpose(bank_o[k % 2][:, t * P:(t + 1) * P], x_row[:, t, k * P:(k + 1) * P])
                    mm.then_inc(S["fT_ps"], 1)
                pe.wait_ge(S["fT_ok"], b * KT + KT)
                for t in range(TT):
                    for k in range(KT):
                        mm = pe.matmul(bank_o[0][:, t * NE:(t + 1) * NE], end_s[:, k, t * P:(t + 1) * P], w_gate[:, k, :], start=(k == 0), stop=(k == KT - 1))
                mm.then_inc(S["lg_ps"], 1)

            def ranks(b):
                pe.wait_ge(S["act_ok"], b + 1)
                for t in range(TT):
                    pe.matmul(bank_o[1][:, t * NE:(t + 1) * NE], tri, r["act"][:, t, :], start=True, stop=False)
                    mm = pe.matmul(bank_o[1][:, t * NE:(t + 1) * NE], ones, cs[:, t, :], start=False, stop=True)
                mm.then_inc(S["rank_ps"], 1)

            for e in range(ET):
                scan_input(0, e)
            scan_params(0)
            deltas(0)
            norm_transposes(0)
            keys_values(0)
            first_queries(0)
            key_transposes(0)
            q_transposes(0, 0)
            first_scores(0)

            def row(b, at, last):
                wait_apart(pe, S["slot_ok"], b)
                with pe.Fori(0, G - 1) as g:
                    for j in range(4):
                        head(b, g * 4 + j, g, j, False)
                for j in range(4):
                    head(b, (G - 1) * 4 + j, G - 1, j, True)
                pe.wait_ge(S["o_ok"], b * H * 2 + H * 2)
                for h in range(H):
                    out_proj(b, h)
                    if last:
                        continue
                    if h == 4:
                        scan_input(b + 1, 0)
                        scan_input(b + 1, 1)
                    elif h == 5:
                        scan_input(b + 1, 2)
                        scan_input(b + 1, 3)
                    elif h == 8:
                        scan_params(b + 1)
                    elif h == 10:
                        deltas(b + 1)
                    elif h == 12:
                        norm_transposes(b + 1)
                    elif h == 14:
                        keys_values(b + 1)
                if not last:
                    first_queries(b + 1)
                scan_transposes(b)
                logits(b)
                if not last:
                    key_transposes(b + 1)
                    q_transposes(b + 1, 0)
                    pe.wait_ge(S["x2_ok"], b * TT + TT)
                    first_scores(b + 1)
                ranks(b)

            each_row(pe, row)

            xt_bank, gu_bank, ht_bank, y_bank = bank_q[0], bank_s[0], bank_s[1], bank_o[0]
            pe.wait_ge(S["slot_ok"], NB)
            pe.matmul(bank_q[1][:, 0:NE], ones, cs[:, 0, :], start=True, stop=True).then_inc(S["cnt_ps"], 1)

            def xt(blk):
                pe.wait_ge(S["blk_in"], blk * 32 + 32)
                for k in range(KT):
                    mm = transpose(xt_bank[:, k * P:(k + 1) * P], x_blk[:, k * P:(k + 1) * P])
                mm.then_inc(S["xt_ps"], 1)

            def gate_up(blk, e):
                hi, lo = gate_up_w(w_hi, e), gate_up_w(w_lo, e)
                pe.wait_ge(S["wlo_ok"], e * 2 + 2)
                pe.wait_ge(S["xtlo_ok"], blk + 1)
                for k in range(KT):
                    pe.matmul(gu_bank[:, 0:2 * INTER], xt_hi[:, k, :], hi[:, k, :], start=(k == 0), stop=False)
                    pe.matmul(gu_bank[:, 0:2 * INTER], xt_hi[:, k, :], lo[:, k, :], start=False, stop=False)
                    mm = pe.matmul(gu_bank[:, 0:2 * INTER], xt_lo[:, k, :], hi[:, k, :], start=False, stop=(k == KT - 1))
                mm.then_inc(S["gu_ps"], 1)

            def ht(blk):
                pe.wait_ge(S["h_ok"], blk * 2 + 2)
                for k in range(2):
                    mm = transpose(ht_bank[:, k * P:(k + 1) * P], h_sb[:, k * P:(k + 1) * P])
                mm.then_inc(S["ht_ps"], 1)

            def down(blk, e):
                hi, lo = down_w(w_hi, e), down_w(w_lo, e)
                pe.wait_ge(S["htlo_ok"], blk * 2 + 2)
                pe.wait_ge(S["yb_ok"], blk)
                pe.matmul(y_bank[:], ht_hi[:, 0:P], hi[:, 0, :], start=True, stop=False)
                pe.matmul(y_bank[:], ht_hi[:, 0:P], lo[:, 0, :], start=False, stop=False)
                pe.matmul(y_bank[:], ht_lo[:], hi[:, 0, :], start=False, stop=False)
                pe.matmul(y_bank[:], ht_hi[:, P:], hi[:, 1, :], start=False, stop=False)
                pe.matmul(y_bank[:], ht_hi[0:P // 2, P:], lo[0:P // 2, 1, :], start=False, stop=True).then_inc(S["y_ps"], 1)

            def expert(e, first):
                more = pe.value_load(tab[0:1, bass.ds(e, 1)], min_val=MIN_BLK - 1, max_val=EXP_BLK - 1)
                c = 0
                if not first:
                    before = pe.value_load(tab[0:1, bass.ds(e + LAST_BEFORE, 1)], min_val=0, max_val=MAX_BLK)
                    c = before + 1
                xt(c + 1)
                if not first:
                    down(before, e - 1)
                ht(c)
                with pe.Fori(0, more) as k:
                    blk = c + k
                    gate_up(blk + 1, e)
                    xt(blk + 2)
                    down(blk, e)
                    ht(blk + 1)
                gate_up(c + more + 1, e + 1)
                return c + more

            pe.wait_ge(S["tab_ok"], 1)
            xt(0)
            gate_up(0, 0)
            expert(0, True)
            with pe.Fori(1, NE) as e:
                expert(e, False)
            last = pe.value_load(tab[0:1, LAST_BEFORE + NE:LAST_BEFORE + NE + 1], min_val=0, max_val=MAX_BLK + 1)
            xt(last + 2)
            down(last, NE - 1)

        @block.scalar
        def _(act):
            def rs_seed(job, src, scale, eps, w=4):
                act.activation(rs_l[:, 0:w], src, ACT.Ln, scale=scale, bias=eps).then_inc(S["rs_ln"], 1)
                act.wait_ge(S["rs_ln"], job + 1)
                act.activation(rs_y[:, 0:w], rs_l[:, 0:w], ACT.Exp, scale=-0.5).then_inc(S["rs_seed"], 1)

            def norm_seed(at, name):
                act.wait_ge(S["ag_ok"], at.norm(name) * TT + TT)
                rs_seed(at.job(name), mv[:, :, 1], 1.0, EPS_LN)

            act.preload_act_table_set(EXP_SET)
            act.wait_ge(S["w_in_sb"], 16 * N_W)
            act.activation(neg_a[:], neg_a[:], ACT.Exp).then_inc(S["act_step"], 1)
            act.wait_ge(S["act_step"], 1)
            act.activation(neg_a[:], neg_a[:], ACT.Identity, scale=-1.0).then_inc(S["neg_a_ok"], 1)
            act.wait_ge(S["neg_a_ok"], 1)

            def norm_transposed(r):
                for k in range(KT):
                    act.wait_ge(S["xT_ps"], r * KT + k + 1)
                    act.activation(xn_t[:, k, :], bank_q[k % 2][:], ACT.Identity, scale=g_norm[:, k:k + 1]).then_inc(S["xnT_ok"], 1)

            def scan_input(r):
                act.wait_ge(S["scan_ok"], r * H)
                for e in range(ET):
                    act.wait_ge(S["inp_ps"], r * ET + e + 1)
                    act.activation(x_pad[:, e, DC - 1:], bank_q[e % 2][:], ACT.Copy).then_inc(S["xpad_ok"], 1)

            def scan_u(r):
                for e in range(ET):
                    act.wait_ge(S["conv_ok"], r * ET * DC + ET * (DC - 1) + e + 1)
                    act.activation(state[:, e, :], dbu[:, e, :], ACT.Silu, bias=conv_b[:, e:e + 1]).then_inc(S["u_ok"], 1)
                act.preload_act_table_set(EXP_SET)

            def keys_values(r, at):
                act.wait_ge(S["nw"], at.job("k") * 4)
                for t in range(TT):
                    act.wait_ge(S["kv_ps"], r * TT + (t // 2 * 2 + 2))
                    act.activation(junk[:, t, :], bank_t[t // 2][:, (t % 2) * 2 * DH:(t % 2) * 2 * DH + DH], ACT.Square,
                                   accum_out=rs_in[:, t:t + 1]).then_inc(S["ksq_ok"], 1)
                act.wait_ge(S["ksq_ok"], r * TT + TT)
                rs_seed(at.job("k"), rs_in[:], 1 / SCALE, EPS_L2 / SCALE)
                for half in range(2):
                    act.activation(v_aug[:, 2 * half:2 * half + 2, 0:DH], bank_t[half][:, :].rearrange("p (t n) -> p t n", t=2)[:, :, DH:],
                                   ACT.Copy).then_inc(S["v_ok"], 1)

            def scan_params(r):
                act.wait_ge(S["xd_ps"], r + 1)
                act.activation(x_dbl[:], bank_t[1][0:XD, :], ACT.Copy).then_inc(S["xd_ok"], 1)
                for e in range(ET):
                    act.wait_ge(S["dt_ps"], r * ET + e + 1)
                    act.activation(dbu[:, e, :], bank_q[e % 2][:], ACT.Abs, bias=dt_b[:, e:e + 1]).then_inc(S["act_step"], 1)
                    act.activation(delta[:, e, :], bank_q[e % 2][:], ACT.Relu, bias=dt_b[:, e:e + 1]).then_inc(S["dt_ev"], 1)
                act.wait_ge(S["act_step"], r * ET + ET + 1)
                act.activation(dA3, dbu[:], ACT.Exp, scale=-1.0).then_inc(S["sp_e"], 1)

            def scan_log(r):
                act.wait_ge(S["sp_e"], r + 1)
                act.activation(du[:], dA3, ACT.Ln, bias=1.0).then_inc(S["sp_ln"], 1)

            def q_squares(r, piece, t, job):
                act.wait_ge(S["qp_ps"], r * H + piece + 1)
                act.wait_ge(S["nw"], job * 4)
                for j in range(4):
                    act.activation(junk[:, j, :], bank_q[t % 2][:, j * DH:(j + 1) * DH], ACT.Square,
                                   accum_out=rs_in[:, j:j + 1]).then_inc(S["qss_ok"], 1)
                act.wait_ge(S["qss_ok"], r * H * 4 + piece * 4 + 4)
                rs_seed(job, rs_in[:], 1 / 16, EPS_L2 / 4096)

            def key_transposed(r):
                act.wait_ge(S["kT_ps"], r + 1)
                act.activation(k_t[:], bank_t[1][:], ACT.Copy).then_inc(S["kT_ok"], 1)

            def q_transposed(r, group):
                for j in range(4):
                    act.wait_ge(S["qT_ps"], r * H + group * 4 + j + 1)
                    act.activation(q_t[:, j, :], (bank_t[0] if j % 2 == 0 else bank_q[0])[:], ACT.Copy).then_inc(S["qT_ok"], 1)

            def exps(r, h):
                act.wait_ge(S["pv_ps"], r * H * 2 + h * 2)
                for k in range(KT):
                    act.wait_ge(S["s_ps"], r * H * KT + h * KT + (k + 1))
                    act.activation(probs[:, k, :], bank_s[k % 2][:], ACT.Exp).then_inc(S["exp_ok"], 1)

            def decays(r, n):
                act.wait_ge(S["scan_ok"], r * DS + n)
                for e in range(ET):
                    act.activation(dA3[:, e, 1:], delta[:, e, 1:], ACT.Exp,
                                   scale=neg_a[:, bass.ds(n, 1), e:e + 1].rearrange("p a c -> p (a c)")).then_inc(S["dA_ok"], 1)

            def head(r, h, group, j, last_group, at):
                if not last_group:
                    decays(r, h)
                elif j in STATES_IN_LAST_GROUP:
                    decays(r, STATES_IN_LAST_GROUP[j])
                if not last_group:
                    q_squares(r, group * 4 + 4 + j, j, at.job("q4") + group * 4 + j)
                if not (last_group and j == 3):
                    if j == 3:
                        q_transposed(r, group + 1)
                    exps(r, h + 1)
                act.wait_ge(S["oT_ps"], r * H + h + 1)
                act.activation(o_t[:, bass.ds(h, 1), :].rearrange("p a t -> p (a t)"), bank_t[1][:], ACT.Copy).then_inc(S["oT_ok"], 1)

            at = first_places()
            scan_input(0)
            scan_u(0)
            norm_seed(at, "ln1")
            norm_seed(at, "ln2")
            scan_params(0)
            scan_log(0)
            norm_transposed(0)
            keys_values(0, at)
            for t in range(TT):
                q_squares(0, t, t, at.job(f"q{t}"))
            key_transposed(0)
            q_transposed(0, 0)
            exps(0, 0)

            def row(b, at, last):
                act.wait_ge(S["dve_step"], b + 2)
                act.wait_ge(S["slot_ok"], b)
                with act.Fori(0, G - 1) as g:
                    for j in range(4):
                        head(b, g * 4 + j, g, j, False, at)
                for j in range(4):
                    head(b, (G - 1) * 4 + j, G - 1, j, True, at)
                for n in range(DS - 2, DS):
                    decays(b, n)
                if not last:
                    scan_input(b + 1)
                    scan_u(b + 1)
                    norm_seed(at, "ln1")
                    norm_seed(at, "ln2")
                    scan_params(b + 1)
                    scan_log(b + 1)
                    norm_transposed(b + 1)
                    keys_values(b + 1, at)
                norm_seed(at, "o")
                if not last:
                    for t in range(2):
                        q_squares(b + 1, t, t, at.job(f"q{t}"))
                norm_seed(at, "z")
                act.wait_ge(S["zr_ok"], b + 1)
                for t in range(TT):
                    act.activation(end_s[:, t, :], x_sb[:, t, :], ACT.Silu, scale=rs_r[:, t:t + 1], bias=z_bias[:, t:t + 1]).then_inc(S["sz_ok"], 1)
                act.preload_act_table_set(EXP_SET)
                norm_seed(at, "f")
                act.wait_ge(S["ys_ok"], b + 1)
                for k in range(KT):
                    act.wait_ge(S["fT_ps"], b * KT + k + 1)
                    act.activation(end_s[:, k, :], bank_o[k % 2][:], ACT.Copy).then_inc(S["fT_ok"], 1)
                if not last:
                    for t in range(2, TT):
                        q_squares(b + 1, t, t, at.job(f"q{t}"))
                act.wait_ge(S["lgs_ok"], b + 1)
                act.activation(r["pr"][:], r["lg"][:], ACT.Exp).then_inc(S["rexp_ok"], 1)
                if not last:
                    key_transposed(b + 1)
                    q_transposed(b + 1, 0)
                    exps(b + 1, 0)

            each_row(act, row)

            xt_bank, gu_bank, ht_bank, y_bank = bank_q[0], bank_s[0], bank_s[1], bank_o[0]

            def load_part(e, part):
                if not (isinstance(e, int) and e + part == 0):
                    act.wait_ge(S["w_in"], (e * 2 + part) * 16)
                act.dma_start(part_w(w_raw, e, part, N_RAW),
                              a["w_exp"][bass.ds(e % NE, 1), :, W_PARTS[part][0]:W_PARTS[part][1]].rearrange("o p n -> (o p) n")).then_inc(S["w_in"], 16)

            def split(e, part):
                act.wait_ge(S["w_in"], (e * 2 + part + 1) * 16)
                act.activation(part_w(w_hi, e, part, N_SPLIT), part_w(w_raw, e, part, N_RAW), ACT.Copy).then_inc(S["whi_ok"], 1)

            def xt(blk):
                act.wait_ge(S["xt_ps"], blk + 1)
                act.activation(xt_hi[:], xt_bank[:].rearrange("p (k t) -> p k t", k=KT), ACT.Copy).then_inc(S["xthi_ok"], 1)

            def silu(blk):
                act.wait_ge(S["gu_ps"], blk + 1)
                act.activation(silu_g[:], gu_bank[:, 0:INTER], ACT.Silu).then_inc(S["silu_ok"], 1)

            def ht(blk):
                act.wait_ge(S["ht_ps"], blk + 1)
                act.activation(ht_hi[:], ht_bank[:, 0:2 * P], ACT.Copy).then_inc(S["hthi_ok"], 1)

            def weigh(blk, e):
                act.wait_ge(S["added"], blk * 16)
                act.wait_ge(S["y_ps"], blk + 1)
                act.activation(y_both[:, bass.ds(blk % 2, 1), :].rearrange("p o d -> p (o d)"), y_bank[:], ACT.Copy,
                               scale=meta[:, bass.ds(blk, 1), bass.ds(e, 1)].rearrange("p o c -> p (o c)")).then_inc(S["yb_ok"], 1)

            act.wait_ge(S["slot_ok"], NB)
            for e in range(4):
                for part in range(2):
                    load_part(e, part)
            for e in range(3):
                for part in range(2):
                    split(e, part)
            act.wait_ge(S["tab_ok"], 1)
            xt(0)
            silu(0)
            xt(1)
            with act.Fori(0, NE) as e:
                more, c = span(act, e)
                ht(c)
                split(e + 3, 0)
                act.wait_ge(S["wlo_ok"], e * 2 + 2)
                load_part(e + 4, 0)
                with act.Fori(0, more) as k:
                    blk = c + k
                    silu(blk + 1)
                    xt(blk + 2)
                    weigh(blk, e)
                    ht(blk + 1)
                split(e + 3, 1)
                load_part(e + 4, 1)
                silu(c + more + 1)
                xt(c + more + 2)
                weigh(c + more, e)

        @block.vector
        def _(dve):
            chain = S["chain"]

            def newton(job, src, scale, eps, w=4):
                n = job * 4
                dve.wait_ge(S["rs_seed"], job + 1)
                dve.tensor_scalar(rs_x[:, 0:w], src, scale, eps, ALU.mult, ALU.add).then_inc(S["nw"], 1)
                dve.tensor_tensor(rs_t[:, 0:w], rs_y[:, 0:w], rs_y[:, 0:w], ALU.mult).then_inc(S["nw"], 1)
                dve.wait_ge(S["nw"], n + 2)
                dve.scalar_tensor_tensor(out=rs_t[:, 0:w], in0=rs_t[:, 0:w], scalar=-0.5, in1=rs_x[:, 0:w], op0=ALU.mult, op1=ALU.mult).then_inc(S["nw"], 1)
                dve.wait_ge(S["nw"], n + 3)
                dve.scalar_tensor_tensor(out=rs_r[:, 0:w], in0=rs_t[:, 0:w], scalar=1.5, in1=rs_y[:, 0:w], op0=ALU.add, op1=ALU.mult).then_inc(S["nw"], 1)
                dve.wait_ge(S["nw"], n + 4)

            def norm_stats(at, name, src, ready=None):
                n = at.norm(name) * TT
                for t in range(TT):
                    if ready:
                        ready(t)
                    dve.bn_stats(st[:, t, :], src(t)).then_inc(S["bn_ok"], 1)
                for t in range(TT):
                    wait_apart(dve, S["bn_ok"], n + t + 1)
                    dve.bn_aggr(mv[:, t, :], st[:, t, :]).then_inc(S["ag_ok"], 1)
                dve.wait_ge(S["ag_ok"], n + TT)
                newton(at.job(name), mv[:, :, 1], 1.0, EPS_LN)

            def apply(t, dst, src):
                return dve.tensor_scalar(dst, src, mv[:, t, 0:1], rs_r[:, t:t + 1], ALU.subtract, ALU.mult)

            dve.memset(v_aug[:, :, DH:], 1.0).then_inc(S["bc_free"], 1)
            dve.memset(cs[:, 0, :], 0.0).then_inc(S["dve_step"], 1)
            dve.wait_ge(S["w_in_sb"], 16 * N_W)
            dve.wait_ge(S["dve_step"], 1)

            def linked(at):
                def link(ins, apart=False):
                    at.steps += 1
                    ins.then_inc(chain, 1)
                    if apart:
                        wait_apart(dve, chain, at.step0 + at.steps)
                    else:
                        dve.wait_ge(chain, at.step0 + at.steps)
                return link

            def first_norms(r, at):
                dve.wait_ge(S["xfirst_in"], r * 16 + 16)
                norm_stats(at, "ln1", lambda t: x_first[:, t, :])
                for t in range(TT):
                    apply(t, norm[:, t, :], x_first[:, t, :]).then_inc(S["ln_a"], 1)
                norm_stats(at, "ln2", lambda t: norm[:, t, :], ready=lambda t: dve.wait_ge(S["ln_a"], r * TT + t + 1))
                for t in range(TT):
                    apply(t, norm[:, t, :], norm[:, t, :]).then_inc(S["ln_x"], 1)

            def convolution(r, link):
                link(dve.memset(x_pad[:, :, 0:DC - 1], 0.0))
                for pair in range(ET // 2):
                    for c in range(DC):
                        for e in (2 * pair, 2 * pair + 1):
                            if c == 0:
                                dve.wait_ge(S["xpad_ok"], r * ET + e + 1)
                                ins = dve.tensor_scalar(dbu[:, e, :], x_pad[:, e, 0:T], conv_w[:, e, 0:1], None, ALU.mult)
                            else:
                                dve.wait_ge(S["conv_ok"], r * ET * DC + pair * 2 * DC + (c - 1) * 2 + e % 2 + 1)
                                ins = dve.scalar_tensor_tensor(out=dbu[:, e, :], in0=x_pad[:, e, c:c + T], scalar=conv_w[:, e, c:c + 1], in1=dbu[:, e, :],
                                                               op0=ALU.mult, op1=ALU.add)
                            ins.then_inc(S["conv_ok"], 1)

            def keys(r, at):
                newton(at.job("k"), rs_in[:], 1 / SCALE, EPS_L2 / SCALE)
                for half in range(2):
                    dve.wait_ge(S["v_ok"], r * 2 + half + 1)
                    dve.tensor_tensor(k_n[:, 2 * half:2 * half + 2, :], bank_t[half][:, :].rearrange("p (t n) -> p t n", t=2)[:, :, 0:DH],
                                      rs_r[:, 2 * half:2 * half + 2].unsqueeze(2).to_broadcast([P, 2, DH]), ALU.mult).then_inc(S["kn_ok"], 1)

            def q_norm(r, group, t, job):
                dve.wait_ge(S["qss_ok"], r * H * 4 + group * 16 + (t * 4 + 4))
                newton(job, rs_in[:], 1 / 16, EPS_L2 / 4096)
                dve.wait_ge(S["qT_ps"], r * H + group * 4)
                dve.tensor_tensor(q_s[:, t, :, :], bank_q[t % 2][:, :].rearrange("p (j d) -> p j d", j=4),
                                  rs_r[:].unsqueeze(2).to_broadcast([P, 4, DH]), ALU.mult).then_inc(S["q_ok"], 1)

            def deltas(r, link):
                dve.wait_ge(S["sp_ln"], r + 1)
                link(dve.tensor_scalar(dbu[:], dA3, 1.0, -1.0, ALU.add, ALU.add))
                link(dve.tensor_tensor(dbu[:], dA3, dbu[:], ALU.subtract))
                link(dve.tensor_tensor(dbu[:], dbu[:], du[:], ALU.add))
                link(dve.tensor_tensor(delta[:], delta[:], dbu[:], ALU.add))
                link(dve.tensor_tensor(du[:], delta[:], state[:], ALU.mult))

            def skip(r):
                for e in range(ET):
                    dve.tensor_scalar(y[:, e, :], state[:, e, :], d_skip[:, e:e + 1], None, ALU.mult)
                dve.memset(dA3[:, :, 0:1], 0.0).then_inc(S["dve_step"], 1)
                dve.wait_ge(S["dve_step"], r + 2)

            def state_input(r, n, fill):
                dve.wait_ge(S[f"bc_in{fill[0]}"], r * (DS // 2) * 32 + fill[1] * 32 + 32)
                dve.tensor_tensor(dbu[:], du[:], b_bc[:, fill[0]:fill[0] + 1, :].to_broadcast([P, ET, T]), ALU.mult).then_inc(S["dbu_ok"], 1)

            def state_scan(r, n):
                dve.wait_ge(S["dA_ok"], r * DS * ET + n * ET + ET)
                dve.wait_ge(S["dbu_ok"], r * DS + n + 1)
                dve.tensor_tensor_scan(state[:].rearrange("p e t -> p (e t)"), dA, dbu[:].rearrange("p e t -> p (e t)"), 0.0,
                                       ALU.mult, ALU.add).then_inc(S["scan_ok"], 1)

            def state_output(r, n, i):
                dve.wait_ge(S["scan_ok"], r * DS + n + 1)
                dve.tensor_tensor(dbu[:], state[:], c_bc[:, i:i + 1, :].to_broadcast([P, ET, T]), ALU.mult).then_inc(S["bc_free"], 1)
                dve.wait_ge(S["bc_free"], r * DS + n + 2)
                dve.tensor_tensor(y[:], y[:], dbu[:], ALU.add).then_inc(S["y_ok"], 1)
                dve.wait_ge(S["y_ok"], r * DS + n + 1)

            def head(r, h, group, j, last_group, at):
                n = None
                if not last_group:
                    n, i, turn = h, j % 2, group * 2 + j // 2
                elif j in STATES_IN_LAST_GROUP:
                    n = STATES_IN_LAST_GROUP[j]
                    i, turn = n % 2, n // 2
                if n is not None:
                    state_input(r, n, (i, turn))
                if not last_group:
                    q_norm(r, group + 1, j, at.job("q4") + group * 4 + j)
                if n is not None:
                    state_scan(r, n)
                dve.wait_ge(S["oT_ps"], r * H + h)
                for half in range(2):
                    o = bank_o[half][:, 0:2 * (DH + 1)].rearrange("p (t n) -> p t n", t=2)
                    dve.wait_ge(S["pv_ps"], r * H * 2 + h * 2 + (half + 1))
                    dve.reciprocal(den[:, 2 * half:2 * half + 2].unsqueeze(2), o[:, :, DH:]).then_inc(S["den_ok"], 1)
                for half in range(2):
                    o = bank_o[half][:, 0:2 * (DH + 1)].rearrange("p (t n) -> p t n", t=2)
                    dve.wait_ge(S["den_ok"], r * H * 2 + h * 2 + (half + 1))
                    dve.tensor_tensor(o_s[:, 2 * half:2 * half + 2, :], o[:, :, 0:DH], den[:, 2 * half:2 * half + 2].unsqueeze(2).to_broadcast([P, 2, DH]),
                                      ALU.mult).then_inc(S["o_ok"], 1)
                if n is not None:
                    state_output(r, n, i)

            at = first_places()
            link = linked(at)
            convolution(0, link)
            first_norms(0, at)
            deltas(0, link)
            skip(0)
            keys(0, at)
            for t in range(TT):
                q_norm(0, 0, t, at.job(f"q{t}"))
            assert at.steps == FIRST_STEPS, at.steps

            def row(b, at, last):
                link = linked(at)
                with dve.Fori(0, G - 1) as g:
                    for j in range(4):
                        head(b, g * 4 + j, g, j, False, at)
                for j in range(4):
                    head(b, (G - 1) * 4 + j, G - 1, j, True, at)
                for n in range(DS - 2, DS):
                    state_input(b, n, (n % 2, n // 2))
                    state_scan(b, n)
                    state_output(b, n, n % 2)
                if not last:
                    convolution(b + 1, link)
                    first_norms(b + 1, at)
                    deltas(b + 1, link)
                    keys(b + 1, at)
                norm_stats(at, "o", lambda t: (bank_o + bank_s)[t][:], ready=lambda t: dve.wait_ge(S["op_ps"], b * TT + t + 1))
                for t in range(TT):
                    apply(t, end_s[:, t, :], (bank_o + bank_s)[t][:]).then_inc(S["on_ok"], 1)
                dve.wait_ge(S["on_ok"], b * TT + TT)
                link(dve.tensor_tensor(end_s, end_s, g_out[:].unsqueeze(1).to_broadcast([P, TT, D]), ALU.mult))
                dve.wait_ge(S["x_in"], b * 16 + 16)
                link(dve.tensor_tensor(x_sb[:], x_sb[:], end_s, ALU.add))
                if not last:
                    for t in range(2):
                        q_norm(b + 1, 0, t, at.job(f"q{t}"))
                norm_stats(at, "z", lambda t: x_sb[:, t, :])
                dve.scalar_tensor_tensor(out=z_bias[:], in0=mv[:, :, 0], scalar=-1.0, in1=rs_r[:], op0=ALU.mult, op1=ALU.mult).then_inc(S["zr_ok"], 1)
                dve.wait_ge(S["sz_ok"], b * TT + TT)
                dve.tensor_tensor(y[:], y[:], end_s, ALU.mult).then_inc(S["ys_ok"], 1)
                for t in range(TT):
                    dve.wait_ge(S["yT_ps"], b * TT + t + 1)
                    dve.tensor_tensor(x_sb[:, t, :], x_sb[:, t, :], bank_s[t % 2][:], ALU.add).then_inc(S["x2_ok"], 1)
                norm_stats(at, "f", lambda t: x_sb[:, t, :], ready=lambda t: dve.wait_ge(S["x2_ok"], b * TT + t + 1))
                dve.wait_ge(S["sent"], b * TT * TOPK * 16)
                for t in range(TT):
                    apply(t, x_row[:, t, 0:D], x_sb[:, t, :]).then_inc(S["xf_ok"], 1)
                link(dve.tensor_copy(x_row[:, :, ID_COL:ID_COL + 1].bitcast(I32), const[:, bass.ds(b * TT + C_TOK, TT)].unsqueeze(2)))
                link(dve.memset(x_row[:, :, ID_COL + 1:], 0.0))
                if not last:
                    skip(b + 1)
                    for t in range(2, TT):
                        q_norm(b + 1, 0, t, at.job(f"q{t}"))

                wide = lambda t: t[:].unsqueeze(2).to_broadcast([P, TT, NE])
                exp_row = lambda c: const[:, c:c + NE].unsqueeze(1).to_broadcast([P, TT, NE])
                tt, ts = dve.tensor_tensor, dve.tensor_scalar
                red = lambda dst, src, op: link(dve.tensor_reduce(r1[dst][:].unsqueeze(2), src, AX, op))
                dve.wait_ge(S["lg_ps"], b + 1)
                logits = bank_o[0][:, 0:TT * NE].rearrange("p (t e) -> p t e", t=TT)
                red("mx", logits, ALU.max)
                tt(r["lg"][:], logits, wide(r1["mx"]), ALU.subtract).then_inc(S["lgs_ok"], 1)
                dve.wait_ge(S["rexp_ok"], b + 1)
                red("sm", r["pr"][:], ALU.add)
                link(dve.reciprocal(r1["rc"][:], r1["sm"][:]))
                link(tt(r["pr"][:], r["pr"][:], wide(r1["rc"]), ALU.mult), True)
                for t in range(TT):
                    link(dve.max(p8[:, t, :], r["pr"][:, t, :]), True)
                    link(dve.match_replace(r["rep"][:, t, :], p8[:, t, :], r["pr"][:, t, :], -1.0), t < TT - 1)
                red("s8", p8[:], ALU.add)
                link(ts(r1["s8"][:], r1["s8"][:], 1e-12, None, ALU.max))
                link(dve.reciprocal(r1["r8"][:], r1["s8"][:]))
                link(ts(r["sel"][:], r["rep"][:], 0.0, None, ALU.is_lt))
                link(tt(r["tvn"][:], r["pr"][:], r["sel"][:], ALU.mult))
                link(tt(r["tvn"][:], r["tvn"][:], wide(r1["r8"]), ALU.mult))
                link(ts(r["scl"][:], r["tvn"][:], alpha[:, 0:1], None, ALU.mult))
                link(dve.scalar_tensor_tensor(out=r["act"][:], in0=r["scl"][:], scalar=TAU, in1=r["sel"][:], op0=ALU.is_ge, op1=ALU.mult))
                red("any", r["act"][:], ALU.max)
                link(ts(r["ct"][:], r["sel"][:], 3.0e38, -3.0e38, ALU.mult, ALU.add))
                link(tt(r["scl"][:], r["scl"][:], r["ct"][:], ALU.add))
                red("mx2", r["scl"][:], ALU.max)
                link(tt(r["cand"][:], r["scl"][:], wide(r1["mx2"]), ALU.is_equal))
                link(tt(r["ct"][:], r["tvn"][:], r["cand"][:], ALU.mult))
                link(dve.scalar_tensor_tensor(out=r["ct"][:], in0=r["cand"][:], scalar=-1.0, in1=r["ct"][:], op0=ALU.add, op1=ALU.add))
                red("m2", r["ct"][:], ALU.max)
                link(tt(r["cand"][:], r["ct"][:], wide(r1["m2"]), ALU.is_equal))
                link(tt(r["fb"][:], r["cand"][:], exp_row(C_REV), ALU.mult))
                red("m3", r["fb"][:], ALU.max)
                link(tt(r["fb"][:], r["fb"][:], wide(r1["m3"]), ALU.is_equal))
                link(ts(r1["any"][:], r1["any"][:], -1.0, 1.0, ALU.mult, ALU.add))
                link(tt(r["fb"][:], r["fb"][:], wide(r1["any"]), ALU.mult))
                link(tt(r["act"][:], r["act"][:], r["fb"][:], ALU.max))
                for t in range(TT - 1):
                    link(tt(cs[:, t + 1, :], cs[:, t, :], r["act"][:, t, :], ALU.add))
                tt(cs[:, TT, :], cs[:, TT - 1, :], r["act"][:, TT - 1, :], ALU.add).then_inc(S["act_ok"], 1)
                link(tt(r["wts"][:], r["tvn"][:], r["act"][:], ALU.mult))
                red("s2", r["wts"][:], ALU.add)
                link(ts(r1["s2"][:], r1["s2"][:], 1e-12, None, ALU.max))
                link(dve.reciprocal(r1["rw"][:], r1["s2"][:]))
                link(tt(x_row[:, :, W_COL:W_COL + NE], r["wts"][:], wide(r1["rw"]), ALU.mult))
                dve.wait_ge(S["rank_ps"], b + 1)
                link(tt(r["slv"][:], bank_o[1][:, 0:TT * NE].rearrange("p (t e) -> p t e", t=TT), exp_row(C_BASE), ALU.add))
                link(tt(r["slv"][:], r["slv"][:], r["act"][:], ALU.mult))
                link(dve.tensor_copy(cs[:, 0, :], cs[:, TT, :]), True)
                for t in range(TT):
                    link(dve.max(s8[:, t, :], r["slv"][:, t, :]), t < TT - 1)
                link(ts(t8[:], s8[:], 0.0, const[:, C_TRASH:C_TRASH + 1], ALU.is_equal, ALU.mult))
                link(dve.scalar_tensor_tensor(out=t8[:], in0=t8[:], scalar=-1.0, in1=s8[:], op0=ALU.add, op1=ALU.add))
                dve.tensor_copy(slot[:], t8[:]).then_inc(S["slot_ok"], 1)
                dve.wait_ge(S["slot_ok"], b + 1)
                assert last or at.steps == ROW_STEPS, at.steps

            each_row(dve, row)

            xt_bank, gu_bank, ht_bank = bank_q[0], bank_s[0], bank_s[1]
            steps = [0]

            def step(ins):
                steps[0] += 1
                ins.then_inc(S["cnt_step"], 1)
                dve.wait_ge(S["cnt_step"], steps[0])

            step(dve.memset(pad[:], 0.0))
            step(dve.tensor_copy(pad[:, ID_COL:ID_COL + 1].bitcast(I32), const[:, C_PAD:C_PAD + 1]))
            dve.wait_ge(S["cnt_ps"], 1)
            step(dve.tensor_copy(n_f[:], bank_q[1][:, 0:NE]))
            step(dve.tensor_scalar(nb_f[:], n_f[:], float((MIN_BLK - 1) * P + 1), float(P - 1), ALU.max, ALU.add))
            step(dve.tensor_copy(nb_i[:], nb_f[:]))
            step(dve.tensor_scalar(nb_i[:], nb_i[:], P.bit_length() - 1, None, ALU.arith_shift_right))
            step(dve.tensor_copy(nb_f[:], nb_i[:]))
            step(dve.tensor_tensor_scan(cum_f[:], ones[:, 0:NE], nb_f[:], 0.0, ALU.mult, ALU.add))
            step(dve.tensor_copy(odd_i[:], cum_f[:, NE - 1:NE]))
            step(dve.tensor_scalar(odd_i[:], odd_i[:], 1, None, ALU.bitwise_and))
            step(dve.tensor_copy(odd_f[:], odd_i[:]))
            step(dve.tensor_tensor(cum_f[:], cum_f[:], nb_f[:], ALU.subtract))
            step(dve.tensor_tensor(nb_f[:, NE - 1:NE], nb_f[:, NE - 1:NE], odd_f[:], ALU.add))
            step(dve.tensor_tensor(odd_f[:], nb_f[:, NE - 1:NE], cum_f[:, NE - 1:NE], ALU.add))
            step(dve.tensor_scalar(odd_f[:], odd_f[:], 0.5, None, ALU.mult))
            step(dve.tensor_scalar(nb_f[:], nb_f[:], -1.0, None, ALU.add))
            step(dve.tensor_scalar(second_f[:], n_f[:], float(P), None, ALU.min))
            for k, col in enumerate((nb_f, cum_f, n_f, second_f)):
                step(dve.tensor_copy(tab[:, k * NE:(k + 1) * NE], col[:]))
            step(dve.tensor_copy(tab[:, 4 * NE:4 * NE + 1], odd_f[:]))
            step(dve.tensor_scalar(odd_f[:], odd_f[:], 2.0, -1.0, ALU.mult, ALU.add))
            step(dve.tensor_copy(tab[:, LAST_BEFORE + NE:], odd_f[:]))
            step(dve.tensor_scalar(cum_f[:], cum_f[:], 1.0, -1.0, ALU.max, ALU.add))
            dve.tensor_copy(tab[:, LAST_BEFORE:LAST_BEFORE + NE], cum_f[:]).then_inc(S["tab_ok"], 1)
            dve.wait_ge(S["tab_ok"], 1)

            def split(e, part):
                dve.wait_ge(S["whi_ok"], e * 2 + (part + 1))
                dve.tensor_tensor(part_w(w_lo, e, part, N_SPLIT), part_w(w_raw, e, part, N_RAW), part_w(w_hi, e, part, N_SPLIT).bitcast(F32),
                                  ALU.subtract).then_inc(S["wlo_ok"], 1)

            def xt(blk):
                dve.wait_ge(S["xthi_ok"], blk + 1)
                dve.tensor_tensor(xt_lo[:], xt_bank[:].rearrange("p (k t) -> p k t", k=KT), xt_hi[:].bitcast(F32), ALU.subtract).then_inc(S["xtlo_ok"], 1)

            def hidden(blk):
                half = P // 2
                dve.wait_ge(S["silu_ok"], blk + 1)
                dve.tensor_tensor(h_sb[:, 0:P], silu_g[:, 0:P], gu_bank[:, INTER:INTER + P], ALU.mult).then_inc(S["h_ok"], 1)
                twice = lambda t: t.unsqueeze(1).to_broadcast([P, 2, half])
                dve.tensor_tensor(h_sb[:, P:].rearrange("p (o c) -> p o c", o=2), twice(silu_g[:, P:]), twice(gu_bank[:, INTER + P:2 * INTER]),
                                  ALU.mult).then_inc(S["h_ok"], 1)

            def ht(blk):
                half = P // 2
                dve.wait_ge(S["hthi_ok"], blk + 1)
                dve.tensor_tensor(ht_lo[:], ht_bank[:, 0:P], ht_hi[:, 0:P].bitcast(F32), ALU.subtract).then_inc(S["htlo_ok"], 1)
                dve.tensor_tensor(ht_hi[half:, P:], ht_bank[half:, P:2 * P], ht_hi[half:, P:].bitcast(F32), ALU.subtract).then_inc(S["htlo_ok"], 1)

            for e in range(2):
                for part in range(2):
                    split(e, part)
            xt(0)
            hidden(0)
            xt(1)
            with dve.Fori(0, NE) as e:
                more, c = span(dve, e)
                ht(c)
                split(e + 2, 0)
                with dve.Fori(0, more) as k:
                    blk = c + k
                    hidden(blk + 1)
                    xt(blk + 2)
                    ht(blk + 1)
                split(e + 2, 1)
                hidden(c + more + 1)
                xt(c + more + 2)

        @block.gpsimd
        def _(pool):
            with pool.Fori(0, NB) as b:
                wait_apart(pool, S["slot_ok"], b + 1)
                for t in range(TT):
                    for k in range(TOPK):
                        if t + k > 0:
                            wait_apart(pool, S["sent"], b * TT * TOPK * 16 + (t * TOPK + k) * 16)
                        pool.indirect_dma_start(out=slots, out_offset=bass.IndirectOffsetOnAxis(ap=slot[:, t, k:k + 1].bitcast(U32), axis=0),
                                                in_=x_row[:, t, :], in_offset=None).then_inc(S["sent"], 16)

            pool.wait_ge(S["tab_ok"], 1)
            pairs = pool.value_load(tab[0:1, 4 * NE:4 * NE + 1], min_val=NE, max_val=MAX_BLK // 2 + 1)
            pool.dma_start(out[NTOK:, :], pad[:, 0:D]).then_inc(S["added"], 16)
            with pool.Fori(0, pairs) as pair:
                for i in range(2):
                    blk = pair * 2 + i
                    pool.wait_ge(S["yb_ok"], blk + 1)
                    pool.tensor_copy(ids[i][:], meta[:, bass.ds(blk, 1), NE:].rearrange("p o c -> p (o c)").bitcast(I32)).then_inc(S["ids_ok"], 1)
                    pool.wait_ge(S["ids_ok"], blk + 1)
                    wait_apart(pool, S["added"], blk * 16 + 16)
                    pool.indirect_dma_start(out=out, out_offset=bass.IndirectOffsetOnAxis(ap=ids[i][:].bitcast(U32), axis=0),
                                            in_=y_both[:, i, :], in_offset=None, compute_op=ALU.add).then_inc(S["added"], 16)


def expert_weights(gate_up, down):
    gu = gate_up.transpose(0, 2, 1).reshape(NE, KT, P, 2 * INTER).transpose(0, 2, 1, 3).reshape(NE, P, GU_COLS)
    dn = down.transpose(0, 2, 1)
    return np.concatenate([gu, dn[:, 0:P], np.concatenate([dn[:, P:], dn[:, P:]], axis=1)], axis=2)


def kernel(**inputs):
    import concourse.bacc as _bacc
    from concourse.bass_utils import run_bass_kernel_spmd as _run

    i = {k.replace("L0_", ""): np.asarray(v) for k, v in inputs.items()}
    tiles = lambda v: v.reshape(-1, P).T
    arrays = {
        "x": i["x"].reshape(NTOK, D),
        "ctx_t": i["ctx_1024"].transpose(0, 2, 1).reshape(NB * DM, T),
        "g_norm": tiles(i["attn_g_norm"]),
        "wq": i["attn_Wq"], "wkv": i["attn_Wkv"], "wout": i["attn_Wout"], "g_out": i["attn_g_out"],
        "w_in_t": i["xattn_in_proj_w"].T,
        "conv_w": i["xattn_conv_w"], "conv_b": tiles(i["xattn_conv_b"]),
        "w_x_t": i["xattn_x_proj_w"].T, "w_dt_t": i["xattn_dt_proj_w"].T, "dt_b": tiles(i["xattn_dt_proj_b"]),
        "a_log": i["xattn_A_log"].reshape(ET, P, DS).transpose(1, 2, 0), "d_skip": tiles(i["xattn_D"]),
        "w_gate_t": i["ffn_gate_weight"].T,
        "w_exp": expert_weights(i["ffn_gate_up_proj"], i["ffn_down_proj"]),
        "alpha": i["ffn_layer_alpha"].reshape(1),
        "const": constants(),
    }
    arrays = {k: np.ascontiguousarray(v) for k, v in arrays.items()}
    nc = _bacc.Bacc("TRN2", target_bir_lowering=False, num_devices=1)
    a = {k: nc.dram_tensor(f"in_{k}", v.shape, mybir.dt.from_np(v.dtype), kind="ExternalInput").ap() for k, v in arrays.items()}
    a["out"] = nc.dram_tensor("out_0", (NTOK + P, D), F32, kind="ExternalOutput").ap()
    decoder_layer(nc, a)
    res = _run(nc, [{f"in_{k}": v for k, v in arrays.items()}], core_ids=[0])
    return res.results[0]["out_0"][:NTOK].reshape(NB, T, D)
```

```python
from contextlib import ExitStack

import numpy as np

import concourse.bass as bass
from concourse import mybir

F32 = mybir.dt.float32
F32R = mybir.dt.float32r
I32 = mybir.dt.int32
U32 = mybir.dt.uint32
ALU = mybir.AluOpType
ACT = mybir.ActivationFunctionType
AX = mybir.AxisListType.X

P = 128
NB, T, D = 4, 512, 512
TT, KT = T // P, D // P
H, DH = 16, 128
G = H // 4
GROUP = 4 * DH
DM, DI, DS, DC, DR = 256, 512, 16, 4, 16
ET, MT = DI // P, DM // P
XD = DR + 2 * DS
NE, INTER, TOPK, TAU = 32, 192, 8, 0.05
NTOK = NB * T
CAP = NTOK // 2 + 3 * P
MIN_BLK = 2
SENT = TT // 2 * TOPK * 16
T_MORE, T_BEFORE, T_TOKENS, T_BLOCKS, T_PAIRS, LAST_BEFORE = 0, NE, 2 * NE, 4 * NE, 6 * NE, 6 * NE + 1
GU_COLS = KT * 2 * INTER
W_EXP = GU_COLS + 2 * D
N_RAW, N_SPLIT = 4, 4
W_PARTS = ((0, W_EXP * 3 // 10), (W_EXP * 3 // 10, W_EXP))
TRASH = NE * CAP
ROW = 560
W_COL, ID_COL = D, D + NE
EPS_LN, EPS_L2 = 1e-5, 1e-12
SCALE = 16.0
EXP_SET = "natural_log_exp_and_others"

Q_LATER = [f"q{piece}" for piece in range(4, H)]
FIRST_JOBS = ["ln1", "ln2", "k", "q0", "q1", "q2", "q3"]
ROW_JOBS = Q_LATER + ["ln1", "ln2", "k", "q0", "q1", "o", "z", "q2", "f", "q3"]
LAST_JOBS = Q_LATER + ["o", "z", "f"]
FIRST_NORMS, ROW_NORMS, LAST_NORMS = ["ln1", "ln2"], ["ln1", "ln2", "o", "z", "f"], ["o", "z", "f"]
FIRST_STEPS, ROW_STEPS = 6, 58
SPLIT_ORDER = [1, 2, 0, 3]

C_ID, C_TRI, C_ONE = 0, P, 2 * P
C_BASE, C_REV, C_TRASH, C_TOK = 3 * P, 3 * P + NE, 3 * P + 2 * NE, 3 * P + 2 * NE + 1
EXP_BLK = NTOK // P + 1
MAX_BLK = NTOK * TOPK // P + MIN_BLK * NE
C_PAD = C_TOK + NB * TT
C_ALL = C_PAD + 1


class Places:

    def __init__(self, jobs, norms, job0, norm0, step0):
        self.jobs, self.norms, self.job0, self.norm0, self.step0, self.steps = jobs, norms, job0, norm0, step0, 0

    def job(self, name):
        return self.job0 + self.jobs.index(name)

    def norm(self, name):
        return self.norm0 + self.norms.index(name)


def first_places():
    return Places(FIRST_JOBS, FIRST_NORMS, 0, 0, 0)


def row_places(b, last):
    return Places(LAST_JOBS if last else ROW_JOBS, LAST_NORMS if last else ROW_NORMS,
                  b * len(ROW_JOBS) + len(FIRST_JOBS), b * len(ROW_NORMS) + len(FIRST_NORMS), b * ROW_STEPS + FIRST_STEPS)


def constants():
    c = np.zeros((P, C_ALL), np.float32)
    p = np.arange(P)
    c[:, C_ID:C_ID + P] = np.eye(P)
    c[:, C_TRI:C_TRI + P] = p[:, None] < p[None, :]
    c[:, C_ONE:C_ONE + P] = 1.0
    c[:, C_BASE:C_BASE + NE] = np.arange(NE)[None, :] * CAP + 1
    c[:, C_REV:C_REV + NE] = NE - np.arange(NE)[None, :]
    c[:, C_TRASH] = TRASH + 1 + p
    c[:, C_TOK:C_PAD] = p[:, None] + P * np.arange(NB * TT)[None, :]
    c[:, C_PAD] = NTOK + p
    return c


def decoder_layer(nc, a):
    ctx = ExitStack()
    with ctx:
        def sb(name, shape, dt=F32):
            return ctx.enter_context(nc.sbuf_tensor(name, shape, dt))

        def sem(name):
            return ctx.enter_context(nc.semaphore(name))

        def dram(name, shape):
            return nc.dram_tensor(name, shape, F32, kind="Internal").ap()

        bank = [ctx.enter_context(nc.psum_tensor(f"bank{i}", [P, 512], F32)) for i in range(8)]
        bank_q, bank_s, bank_o, bank_t = bank[0:2], bank[2:4], bank[4:6], bank[6:8]
        bank_qT = [bank_t[0], bank_q[0], bank_t[0], bank_q[1]]

        bc_dram = dram("bc_dram", [NB, 2 * DS, T])
        wq_dram = dram("wq_dram", [G, P, 2, KT, GROUP])
        slots = [dram(f"slots_{name}", [TRASH + P, ROW]) for name in ("even", "odd")]

        out = a["out"]

        x_sb = sb("x_sb", [P, TT, D])
        x_row = sb("x_row", [P, TT, ROW])
        slot = sb("slot", [P, TT, 8], I32)
        cs = sb("cs", [P, TT + 2, NE])
        const = sb("const", [P, C_ALL])
        ident, tri, ones = const[:, C_ID:C_ID + P], const[:, C_TRI:C_TRI + P], const[:, C_ONE:C_ONE + P]

        stage_a = ExitStack()
        def sb(name, shape, dt=F32):
            return stage_a.enter_context(nc.sbuf_tensor(name, shape, dt))

        wq = sb("wq", [P, 2, KT, GROUP], F32R)
        wkv_hi, wkv_lo = sb("wkv_hi", [P, KT, 2 * DH], F32R), sb("wkv_lo", [P, KT, 2 * DH], F32R)
        xn_hi, xn_lo = sb("xn_hi", [P, KT, T], F32R), sb("xn_lo", [P, KT, T], F32R)
        w_x = sb("w_x", [P, ET, XD])
        w_dt = sb("w_dt", [DR, DI])
        w_gate = sb("w_gate", [P, KT, NE])
        g_norm = sb("g_norm", [P, KT])
        g_out = sb("g_out", [P, D])
        conv_w = sb("conv_w", [P, ET, DC])
        conv_b = sb("conv_b", [P, ET])
        dt_b = sb("dt_b", [P, ET])
        d_skip = sb("d_skip", [P, ET])
        neg_a = sb("neg_a", [P, DS, ET])
        alpha = sb("alpha", [P, 1])

        k_t = sb("k_t", [P, T])
        k_hi, k_lo = sb("k_hi", [P, T], F32R), sb("k_lo", [P, T], F32R)
        v_aug = sb("v_aug", [P, TT, DH + 1])
        q_s = sb("q_s", [P, TT, 4, DH])
        q_t = sb("q_t", [P, 2, T])
        q_hi, q_lo = sb("q_hi", [P, 2, T], F32R), sb("q_lo", [P, 2, T], F32R)
        probs = sb("probs", [P, KT, T])
        o_s = sb("o_s", [P, TT, DH])
        k_n = o_s
        o_t = sb("o_t", [P, H, T])
        wout = sb("wout", [P, 4, D])
        delta = sb("delta", [P, ET, T])
        du = sb("du", [P, ET, T])
        y = sb("y", [P, ET, T])
        decay = sb("decay", [P, ET * (T + DC - 1)])
        x_pad = decay[:, :].rearrange("p (e t) -> p e t", e=ET)
        dA = decay[:, 0:ET * T]
        dA3 = dA.rearrange("p (e t) -> p e t", e=ET)
        dbu = sb("dbu", [P, ET, T])
        state = sb("state", [P, ET, T])
        b_bc = sb("b_bc", [P, 2, T])
        c_bc = sb("c_bc", [P, 2, T])
        x_dbl = sb("x_dbl", [XD, T])
        junk = sb("junk", [P, 4, DH], mybir.dt.bfloat16)
        norm = probs
        x_first = q_s[:].rearrange("p t j d -> p t (j d)")
        ctx_t, w_in = q_t, x_row[:, 0:MT, 0:DI]
        wq_raw = o_t[:].rearrange("p h t -> p (h t)").rearrange("p (k n) -> p k n", k=KT)
        wkv_raw = b_bc[:].rearrange("p i t -> p (i t)").rearrange("p (k n) -> p k n", k=KT)
        raw_of = lambda g: wq_raw[:, :, g * GROUP:(g + 1) * GROUP]
        wq_hi = [wq[:, 0], du[:].bitcast(F32R), x_sb[:].bitcast(F32R), y[:].bitcast(F32R)]
        wq_lo = [wq[:, 1]] + [raw_of(g).bitcast(F32R) for g in range(1, G)]
        end_s = o_t[:, 4:8, :]
        st = sb("st", [P, TT, 6])
        mv = sb("mv", [P, TT, 2])
        rs_in = sb("rs_in", [P, 4])
        rs_x = sb("rs_x", [P, 4])
        rs_l = sb("rs_l", [P, 4])
        rs_y = sb("rs_y", [P, 4])
        rs_t = sb("rs_t", [P, 4])
        rs_r = sb("rs_r", [P, 4])
        z_bias = sb("z_bias", [P, TT])
        den = sb("den", [P, TT])
        NAMES = ["lg", "pr", "rep", "sel", "tvn", "scl", "act", "cand", "ct", "fb", "wts", "slv"]
        r = {n: o_t[:].rearrange("p h t -> p (h t)")[:, i * TT * NE:(i + 1) * TT * NE].rearrange("p (t e) -> p t e", t=TT)
             for i, n in enumerate(NAMES)}
        p8 = sb("p8", [P, TT, 8])
        s8 = sb("s8", [P, TT, 8])
        t8 = sb("t8", [P, TT, 8])
        r1 = {n: sb("r1_" + n, [P, TT]) for n in ["mx", "sm", "rc", "s8", "r8", "any", "mx2", "m2", "m3", "s2", "rw"]}

        stage_a.close()

        def sb(name, shape, dt=F32):
            return ctx.enter_context(nc.sbuf_tensor(name, shape, dt))

        w_raw = sb("w_raw", [P, N_RAW, W_EXP])
        w_hi = sb("w_hi", [P, N_SPLIT, W_EXP], F32R)
        w_lo = sb("w_lo", [P, N_SPLIT, W_EXP], F32R)
        x_blk = sb("x_blk", [P, D])
        meta = sb("meta", [P, MAX_BLK + EXP_BLK + 1, NE + 1])
        ids = [sb(f"ids{i}", [P, 1], I32) for i in range(2)]
        xt_hi, xt_lo = sb("xt_hi", [P, KT, P], F32R), sb("xt_lo", [P, KT, P], F32R)
        silu_g = sb("silu_g", [P, INTER])
        h_sb = sb("h_sb", [P, 2 * P])
        ht_hi = sb("ht_hi", [P, 2 * P], F32R)
        ht_lo = sb("ht_lo", [P, P], F32R)
        y_both = sb("y_both", [P, 2, D])
        pad = sb("pad", [P, ROW])
        n_f, list_f, nb_f, cum_f = sb("n_f", [P, 2, NE]), sb("list_f", [P, 2, NE]), sb("nb_f", [P, NE]), sb("cum_f", [P, NE])
        list_i = sb("list_i", [P, 2, NE], I32)
        odd_i, odd_f = sb("odd_i", [P, 1], I32), sb("odd_f", [P, 1])
        tab = sb("tab", [P, LAST_BEFORE + NE + 1], I32)

        S = {n: sem(n) for n in """
            w_in_sb x_in xfirst_in ctx_in bc_written bc_in0 bc_in1 wkv_in wq_in wq_out0 wq_out1 wq_out2 wq_out3 wq_in0 wq_in1 wout_in0 wout_in1 wout_in2 wout_in3 x2_out
            inp_ps xT_ps kv_ps kT_ps qp_ps qT_ps s_ps pv_ps oT_ps xd_ps dt_ps wout_used op_ps yT_ps fT_ps lg_ps rank_ps
            neg_a_ok act_step rs_ln rs_seed xpad_ok xnT_ok ksq_ok v_ok kT_ok wqhi_ok wkvhi_ok u_ok xd_ok dt_ev sp_e sp_ln qss_ok qT_ok
            exp_ok dA_ok oT_ok sz_ok fT_ok rexp_ok
            dve_step bn_ok ag_ok nw ln_a ln_x wqlo_ok wkvlo_ok xlo_ok klo_ok qlo_ok conv_ok kn_ok q_ok scan_ok bc_free o_ok on_ok x1_ok zr_ok ys_ok x2_ok xf_ok dbu_ok den_ok y_ok chain
            lgs_ok act_ok slot_ok
            sent0 sent1
            w_in pad_out blk_in
            cnt_ps xt_ps gu_ps ht_ps y_ps
            whi_ok xthi_ok silu_ok hthi_ok yb_ok
            cnt_step tab_ok wlo_ok xtlo_ok h_ok htlo_ok
            ids_ok added
            """.split()}

        N_W = 12
        STATES_IN_LAST_GROUP = {0: DS - 4, 2: DS - 3}
        INPUTS_IN_LAST_GROUP = {1: DS - 3}

        block = ctx.enter_context(nc.Block())

        def wait_apart(eng, semaphore, value):
            if isinstance(value, int):
                eng.wait_ge(semaphore, value)
                return
            count = eng.to_reg(value)
            eng.wait_ge(S["w_in_sb"], 16 * N_W)
            eng.wait_ge(semaphore, count)

        def wq_stored(eng):
            for g in range(G):
                eng.wait_ge(S[f"wq_out{g}"], 2 * 16)

        def span(eng, e):
            return (eng.value_load(tab[0:1, bass.ds(e, 1)], min_val=MIN_BLK - 1, max_val=EXP_BLK - 1),
                    eng.value_load(tab[0:1, bass.ds(e + T_BEFORE, 1)], min_val=0, max_val=MAX_BLK))

        def each_row(eng, row):
            with eng.Fori(0, NB - 1) as b:
                row(b, row_places(b, False), False)
            row(NB - 1, row_places(NB - 1, True), True)

        def gate_up_w(w, e):
            return w[:, bass.ds(e % N_SPLIT, 1), 0:GU_COLS].rearrange("p o (k n) -> p (o k) n", k=KT)

        def down_w(w, e):
            return w[:, bass.ds(e % N_SPLIT, 1), GU_COLS:].rearrange("p o (r d) -> p (o r) d", r=2)

        def part_w(w, e, part, ring):
            return w[:, bass.ds(e % ring, 1), W_PARTS[part][0]:W_PARTS[part][1]].rearrange("p o n -> p (o n)")

        @block.sync
        def _(sp):
            def load_ctx(r):
                sp.dma_start(ctx_t[:], a["ctx_t"][bass.ds(r * DM, DM), :].rearrange("(m p) l -> p m l", p=P)).then_inc(S["ctx_in"], 16)
                sp.dma_start(w_in, a["w_in_t"].rearrange("(m p) e -> p m e", p=P)).then_inc(S["ctx_in"], 16)

            def load_first(r):
                sp.dma_start(x_first, a["x"][bass.ds(r * T, T), :].rearrange("(t p) d -> p t d", p=P)).then_inc(S["xfirst_in"], 16)

            def load(dst, src):
                sp.dma_start(dst, src).then_inc(S["w_in_sb"], 16)

            load_first(0)
            load_ctx(0)
            load(const[:], a["const"])
            load(conv_w[:], a["conv_w"].rearrange("(e p) c -> p e c", p=P))
            load(conv_b[:], a["conv_b"])
            load(dt_b[:], a["dt_b"])
            load(d_skip[:], a["d_skip"])
            load(neg_a[:], a["a_log"])
            load(g_norm[:], a["g_norm"])
            load(w_x[:], a["w_x_t"].rearrange("(e p) k -> p e k", p=P))
            load(w_dt[:], a["w_dt_t"])
            load(w_gate[:], a["w_gate_t"].rearrange("(k p) n -> p k n", p=P))
            load(g_out[:], a["g_out"].partition_broadcast(P))
            sp.dma_start(alpha[:], a["alpha"].partition_broadcast(P)).then_inc(S["w_in_sb"], 16)

            def load_x(r):
                sp.dma_start(x_sb[:], a["x"][bass.ds(r * T, T), :].rearrange("(t p) d -> p t d", p=P)).then_inc(S["x_in"], 16)

            def load_wout(h):
                sp.dma_start(wout[:, h % 4, :], a["wout"][h * DH:(h + 1) * DH, :]).then_inc(S[f"wout_in{h % 4}"], 16)

            def write_bc(r):
                wait_apart(sp, S["xd_ok"], r + 1)
                sp.dma_start(bc_dram[bass.ds(r, 1)].rearrange("o n t -> (o n) t"), x_dbl[DR:XD, :]).then_inc(S["bc_written"], 16)

            def first_bc(r):
                wait_apart(sp, S["bc_written"], r * 16 + 16)
                load_bc(r, 0)

            def load_bc(r, n):
                for i in range(2):
                    wait_apart(sp, S["bc_free"], r * DS + n + i)
                    for dst, row in ((b_bc, 0), (c_bc, DS)):
                        src = bc_dram[bass.ds(r, 1), bass.ds(n + (row + i), 1), :].rearrange("o n t -> (o n t)")
                        sp.dma_start(dst[:, i, :], src.partition_broadcast(P)).then_inc(S[f"bc_in{i}"], 16)

            def store_wq(g):
                sp.wait_ge(S["wqhi_ok"], SPLIT_ORDER.index(g) + 1)
                sp.wait_ge(S["wqlo_ok"], SPLIT_ORDER.index(g) + 1)
                for part, src in ((0, wq_hi[g]), (1, wq_lo[g])):
                    sp.dma_start(wq_dram[g][:, part], src.bitcast(F32)).then_inc(S[f"wq_out{g}"], 16)

            sp.dma_start(wkv_raw, a["wkv"].rearrange("(k p) n -> p k n", p=P)).then_inc(S["wkv_in"], 16)
            sp.dma_start(wq_raw, a["wq"].rearrange("(k p) n -> p k n", p=P)).then_inc(S["wq_in"], 16)
            for h in range(4):
                load_wout(h)
            for g in SPLIT_ORDER[:-1]:
                store_wq(g)
            write_bc(0)
            store_wq(SPLIT_ORDER[-1])
            wq_stored(sp)
            load_x(0)
            sp.wait_ge(S["wkvlo_ok"], 1)
            first_bc(0)

            def row(b, at, last):
                with sp.Fori(1, DS // 2 - 2) as pair:
                    load_bc(b, pair * 2)
                load_bc(b, DS - 4)
                if not last:
                    wait_apart(sp, S["qT_ps"], b * H + H)
                    load_first(b + 1)
                load_bc(b, DS - 2)
                if not last:
                    wait_apart(sp, S["s_ps"], b * H * KT + H * KT)
                    for i in range(2):
                        wait_apart(sp, S[f"sent{i}"], b * SENT)
                    load_ctx(b + 1)
                for h in range(4, H):
                    sp.wait_ge(S["wout_used"], b * (H - 1) + (h - 3))
                    load_wout(h)
                if not last:
                    sp.wait_ge(S["op_ps"], b * TT + TT)
                    for h in range(4):
                        load_wout(h)
                    write_bc(b + 1)
                    first_bc(b + 1)
                wait_apart(sp, S["x2_ok"], b * TT + TT)
                sp.dma_start(out[bass.ds(b * T, T), :].rearrange("(t p) d -> p t d", p=P), x_sb[:]).then_inc(S["x2_out"], 16)
                if not last:
                    sp.wait_ge(S["xf_ok"], b * TT + TT)
                    wait_apart(sp, S["x2_out"], b * 16 + 16)
                    load_x(b + 1)

            each_row(sp, row)

            def entry(column, e, low, high):
                return sp.value_load(tab[0:1, bass.ds(e + column, 1)], min_val=low, max_val=high)

            def list_tokens(e):
                return [entry(T_TOKENS + i * NE, e, 0, NTOK // 2) for i in range(2)]

            def pad_list(e, i, tokens):
                sp.dma_start(slots[i][bass.ds(e * CAP + tokens, P), :], pad[:]).then_inc(S["pad_out"], 16)

            def load_blocks(e, i, blocks, before):
                with sp.Fori(0, blocks) as k:
                    load_block(i, e * CAP + k * P, before + k)

            def load_block(i, row, blk):
                wait_apart(sp, S["xt_ps"], blk)
                sp.dma_start(x_blk[:], slots[i][bass.ds(row, P), 0:D]).then_inc(S["blk_in"], 16)
                sp.dma_start(meta[:, bass.ds(blk, 1), :].rearrange("p o c -> p (o c)"), slots[i][bass.ds(row, P), W_COL:ID_COL + 1]).then_inc(S["blk_in"], 16)

            sp.wait_ge(S["tab_ok"], 1)
            sp.wait_ge(S["x2_out"], NB * 16)
            first, last = list_tokens(0), list_tokens(NE - 1)
            for i in range(2):
                wait_apart(sp, S[f"sent{i}"], NB * SENT)
                pad_list(0, i, first[i])
            pad_list(NE - 1, 1, last[1] + P)
            with sp.Fori(0, NE) as e:
                before = entry(T_BEFORE, e, 0, MAX_BLK)
                even, odd = (entry(T_BLOCKS + i * NE, e, 1, NTOK // 2 // P + 1) for i in range(2))
                ahead = (e + 1) % NE
                tokens = list_tokens(ahead)
                wait_apart(sp, S["pad_out"], e * 32 + 3 * 16)
                load_blocks(e, 0, even, before)
                for i in range(2):
                    pad_list(ahead, i, tokens[i])
                load_blocks(e, 1, odd, before + even)
            pairs = sp.value_load(tab[0:1, T_PAIRS:T_PAIRS + 1], min_val=NE, max_val=MAX_BLK // 2 + 1)
            for i in range(2):
                load_block(i, 0, pairs * 2 + i)
            sp.wait_ge(S["blk_in"], pairs * 64 + 64)
            sp.wait_ge(S["w_in"], (NE + 4) * 2 * 16)
            sp.wait_ge(S["pad_out"], (2 * NE + 3) * 16)
            wait_apart(sp, S["added"], pairs * 32 + 16)

        @block.tensor
        def _(pe):
            def transpose(out, src):
                return pe.transpose(out, src, ident)

            pe.wait_ge(S["w_in_sb"], 16 * N_W)

            def norm_transposes(r, first, ks):
                pe.wait_ge(S["ln_x"], r * TT + TT)
                if first:
                    pe.wait_ge(S["xpad_ok"], r * ET + ET)
                else:
                    pe.wait_ge(S["qT_ok"], r * H)
                    pe.wait_ge(S["qlo_ok"], r * G * 2)
                for k in ks:
                    if k >= 2:
                        pe.wait_ge(S["xlo_ok"], r * KT + k - 1)
                    for t in range(TT):
                        mm = transpose(bank_q[k % 2][:, t * P:(t + 1) * P], norm[:, t, k * P:(k + 1) * P])
                    mm.then_inc(S["xT_ps"], 1)

            def scan_input(r, first, e):
                pe.wait_ge(S["ctx_in"], r * 32 + 32)
                if not first:
                    pe.wait_ge(S["xlo_ok"], r * KT + KT)
                if e >= 2:
                    pe.wait_ge(S["xpad_ok"], r * ET + e - 1)
                for m in range(MT):
                    mm = pe.matmul(bank_q[e % 2][:], w_in[:, m, e * P:(e + 1) * P], ctx_t[:, m, :], start=(m == 0), stop=(m == MT - 1))
                mm.then_inc(S["inp_ps"], 1)

            def keys_values(r, first):
                pe.wait_ge(S["xlo_ok"], r * KT + KT)
                pe.wait_ge(S["wkvlo_ok"], 1)
                if first:
                    pe.wait_ge(S["xd_ok"], r + 1)
                else:
                    pe.wait_ge(S["oT_ok"], r * H)
                for t in range(TT):
                    tile = slice(t * P, (t + 1) * P)
                    dst = bank_t[t // 2][:, (t % 2) * 2 * DH:(t % 2 + 1) * 2 * DH]
                    for k in range(KT):
                        pe.matmul(dst, xn_hi[:, k, tile], wkv_hi[:, k, :], start=(k == 0), stop=False)
                        pe.matmul(dst, xn_hi[:, k, tile], wkv_lo[:, k, :], start=False, stop=False)
                        mm = pe.matmul(dst, xn_lo[:, k, tile], wkv_hi[:, k, :], start=False, stop=(k == KT - 1))
                    mm.then_inc(S["kv_ps"], 1)

            def scan_params(r, first):
                if not first:
                    pe.wait_ge(S["v_ok"], r * 2 + 2)
                    pe.wait_ge(S["kn_ok"], r * 2 + 2)
                pe.wait_ge(S["u_ok"], r * ET + ET)
                for e in range(ET):
                    mm = pe.matmul(bank_t[1][0:XD, :], w_x[:, e, :], state[:, e, :], start=(e == 0), stop=(e == ET - 1))
                mm.then_inc(S["xd_ps"], 1)

            def deltas(r, first):
                pe.wait_ge(S["xd_ok"], r + 1)
                if first:
                    pe.wait_ge(S["xlo_ok"], r * KT + KT)
                else:
                    pe.wait_ge(S["q_ok"], r * H * 4 + 8)
                pe.wait_ge(S["xpad_ok"], r * ET + ET)
                for e in range(ET):
                    if e >= 2:
                        pe.wait_ge(S["dt_ev"], r * ET + e - 1)
                    pe.matmul(bank_q[e % 2][:], w_dt[:, e * P:(e + 1) * P], x_dbl[0:DR, :], start=True, stop=True).then_inc(S["dt_ps"], 1)

            def q_piece(loads, t):
                tile = slice(t * P, (t + 1) * P)
                for k in range(KT):
                    if t == 0 and k % (KT // 2) == 0 and not (isinstance(loads, int) and loads == 0):
                        pe.wait_ge(S[f"wq_in{k // (KT // 2)}"], loads * 16)
                    pe.matmul(bank_q[t % 2][:], xn_hi[:, k, tile], wq[:, 0, k, :], start=(k == 0), stop=False)
                    pe.matmul(bank_q[t % 2][:], xn_hi[:, k, tile], wq[:, 1, k, :], start=False, stop=False)
                    mm = pe.matmul(bank_q[t % 2][:], xn_lo[:, k, tile], wq[:, 0, k, :], start=False, stop=(k == KT - 1))
                mm.then_inc(S["qp_ps"], 1)

            def first_queries(r, first, ts):
                pe.wait_ge(S["xlo_ok"], r * KT + KT)
                pe.wait_ge(S["wqlo_ok"], SPLIT_ORDER.index(0) + 1)
                for t in ts:
                    if first and t >= 2:
                        pe.wait_ge(S["q_ok"], r * H * 4 + (t - 1) * 4)
                    elif t >= 2:
                        pe.wait_ge(S["dt_ev"], r * ET + ET)
                    elif first:
                        pe.wait_ge(S["dt_ev"], r * ET + ET)
                    else:
                        pe.wait_ge(S["xpad_ok"], r * ET + ET)
                    q_piece(r * G, t)

            def key_transposes(r):
                pe.wait_ge(S["kn_ok"], r * 2 + 2)
                pe.wait_ge(S["v_ok"], r * 2 + 2)
                pe.wait_ge(S["xd_ok"], r + 1)
                for t in range(TT):
                    mm = transpose(bank_t[1][:, t * P:(t + 1) * P], k_n[:, t, :])
                mm.then_inc(S["kT_ps"], 1)

            def q_transposes(r, group, j):
                pe.wait_ge(S["q_ok"], r * H * 4 + group * 16 + 16)
                pe.wait_ge(S["qT_ok"], r * H + group * 4 + j)
                pe.wait_ge(S["qlo_ok"], r * G * 2 + group * 2)
                for i in (j, j + 1):
                    for t in range(TT):
                        mm = transpose(bank_qT[i][:, t * P:(t + 1) * P], q_s[:, t, i, :])
                    mm.then_inc(S["qT_ps"], 1)

            def scores(r, h, group, j):
                if j < 2:
                    pe.wait_ge(S["qT_ok"], r * H + h + 1)
                else:
                    pe.wait_ge(S["klo_ok"], r + 1)
                    pe.wait_ge(S["qlo_ok"], r * G * 2 + group * 2 + (j - 1))
                for k in range(KT):
                    tile = slice(k * P, (k + 1) * P)
                    if k >= 2:
                        pe.wait_ge(S["exp_ok"], r * H * KT + h * KT + (k - 1))
                    if j < 2:
                        mm = pe.matmul(bank_s[k % 2][:], k_t[:, tile], q_t[:, j, :], start=True, stop=True)
                    else:
                        pe.matmul(bank_s[k % 2][:], k_hi[:, tile], q_hi[:, j - 2, :], start=True, stop=False)
                        pe.matmul(bank_s[k % 2][:], k_lo[:, tile], q_hi[:, j - 2, :], start=False, stop=False)
                        mm = pe.matmul(bank_s[k % 2][:], k_hi[:, tile], q_lo[:, j - 2, :], start=False, stop=True)
                    mm.then_inc(S["s_ps"], 1)

            def first_scores(r):
                pe.wait_ge(S["kT_ok"], r * 2 + 2)
                scores(r, 0, 0, 0)

            def weighted_values(r, h):
                pe.wait_ge(S["exp_ok"], r * H * KT + h * KT + KT)
                pe.wait_ge(S["o_ok"], r * H * TT + h * TT)
                for half in range(2):
                    for t in (2 * half, 2 * half + 1):
                        for k in range(KT):
                            mm = pe.matmul(bank_o[half][:, (t % 2) * (DH + 1):(t % 2 + 1) * (DH + 1)], probs[:, k, t * P:(t + 1) * P], v_aug[:, k, :],
                                           start=(k == 0), stop=(k == KT - 1))
                    mm.then_inc(S["pv_ps"], 1)

            def head(r, h, group, j, last_group):
                def next_queries(t):
                    pe.wait_ge(S["q_ok"], r * H * 4 + group * 16 + (t + 3) * 4)
                    pe.wait_ge(S["qT_ok"], r * H + group * 4 + 4)
                    pe.wait_ge(S["qlo_ok"], r * G * 2 + group * 2 + 2)
                    q_piece(r * G + group + 1, t)

                if not last_group and j in (0, 2):
                    next_queries(0 if j == 0 else 3)
                if j < 3:
                    scores(r, h + 1, group, j + 1)
                elif not last_group:
                    pe.wait_ge(S["slot_ok"], r)
                    q_transposes(r, group + 1, 0)
                    scores(r, h + 1, group + 1, 0)
                pe.wait_ge(S["o_ok"], r * H * TT + h * TT + TT)
                pe.wait_ge(S["oT_ok"], r * H + h)
                for t in range(TT):
                    mm = transpose(bank_t[1][:, t * P:(t + 1) * P], o_s[:, t, :])
                mm.then_inc(S["oT_ps"], 1)
                if not last_group and j == 3:
                    q_transposes(r, group + 1, 2)
                if not last_group and j in (0, 1):
                    next_queries(j + 1)
                if not (last_group and j == 3):
                    weighted_values(r, h + 1)

            def out_proj(b, h):
                pe.wait_ge(S["oT_ok"], b * H + h + 1)
                pe.wait_ge(S[f"wout_in{h % 4}"], b * G * 16 + (h // 4 * 16 + 16))
                for t in range(TT):
                    mm = pe.matmul((bank_o + bank_s)[t][:], o_t[:, h, t * P:(t + 1) * P], wout[:, h % 4, :], start=(h == 0), stop=(h == H - 1))
                    if h == H - 1:
                        mm.then_inc(S["op_ps"], 1)
                if h < H - 1:
                    mm.then_inc(S["wout_used"], 1)

            def scan_transposes(b):
                pe.wait_ge(S["on_ok"], b * TT + TT)
                pe.wait_ge(S["ys_ok"], b * TT + TT)
                for t in range(TT):
                    if t >= 2:
                        pe.wait_ge(S["x2_ok"], b * TT + t - 1)
                    for e in range(ET):
                        mm = transpose(bank_s[t % 2][:, e * P:(e + 1) * P], y[:, e, t * P:(t + 1) * P])
                    mm.then_inc(S["yT_ps"], 1)

            def logits(b):
                pe.wait_ge(S["xf_ok"], b * TT + TT)
                for k in range(KT):
                    if k >= 2:
                        pe.wait_ge(S["fT_ok"], b * KT + k - 1)
                    for t in range(TT):
                        mm = transpose(bank_o[k % 2][:, t * P:(t + 1) * P], x_row[:, t, k * P:(k + 1) * P])
                    mm.then_inc(S["fT_ps"], 1)
                pe.wait_ge(S["fT_ok"], b * KT + KT)
                for t in range(TT):
                    for k in range(KT):
                        mm = pe.matmul(bank_o[0][:, t * NE:(t + 1) * NE], end_s[:, k, t * P:(t + 1) * P], w_gate[:, k, :], start=(k == 0), stop=(k == KT - 1))
                mm.then_inc(S["lg_ps"], 1)

            def ranks(b, last):
                pe.wait_ge(S["act_ok"], b + 1)
                if not last:
                    pe.wait_ge(S["qlo_ok"], (b + 1) * G * 2 + 2)
                pe.matmul(bank_t[0][:, 0:TT * NE], tri, r["act"], start=True, stop=False)
                mm = pe.matmul(bank_t[0][:, 0:TT * NE], ones, cs[:, 0:TT, :], start=False, stop=True)
                mm.then_inc(S["rank_ps"], 1)

            for e in range(ET):
                scan_input(0, True, e)
            norm_transposes(0, True, range(2))
            scan_params(0, True)
            norm_transposes(0, True, range(2, KT))
            deltas(0, True)
            keys_values(0, True)
            first_queries(0, True, range(TT))
            key_transposes(0)
            q_transposes(0, 0, 0)
            q_transposes(0, 0, 2)
            first_scores(0)
            weighted_values(0, 0)

            def row(b, at, last):
                with pe.Fori(0, G - 1) as g:
                    for j in range(4):
                        head(b, g * 4 + j, g, j, False)
                for j in range(4):
                    head(b, (G - 1) * 4 + j, G - 1, j, True)
                pe.wait_ge(S["o_ok"], b * H * TT + H * TT)
                for h in range(H):
                    out_proj(b, h)
                    if last:
                        continue
                    if h == 3:
                        norm_transposes(b + 1, False, range(2))
                    elif h == 4:
                        norm_transposes(b + 1, False, range(2, KT))
                    elif h == 5:
                        scan_input(b + 1, False, 0)
                        scan_input(b + 1, False, 1)
                    elif h == 6:
                        keys_values(b + 1, False)
                    elif h == 7:
                        scan_input(b + 1, False, 2)
                        scan_input(b + 1, False, 3)
                    elif h == 8:
                        first_queries(b + 1, False, range(2))
                    elif h == 9:
                        scan_params(b + 1, False)
                    elif h == 10:
                        deltas(b + 1, False)
                    elif h == 14:
                        key_transposes(b + 1)
                if not last:
                    first_queries(b + 1, False, range(2, TT))
                scan_transposes(b)
                logits(b)
                if not last:
                    q_transposes(b + 1, 0, 0)
                    q_transposes(b + 1, 0, 2)
                    pe.wait_ge(S["x2_ok"], b * TT + TT)
                    first_scores(b + 1)
                    pe.wait_ge(S["lgs_ok"], b + 1)
                    weighted_values(b + 1, 0)
                ranks(b, last)

            each_row(pe, row)

            xt_bank, gu_bank, ht_bank, y_bank = bank_q[0], bank_s[0], bank_s[1], bank_o[0]
            pe.wait_ge(S["slot_ok"], NB)
            pe.matmul(bank_q[1][:, 0:2 * NE], ones, cs[:, 0:2, :], start=True, stop=True).then_inc(S["cnt_ps"], 1)

            def xt(blk):
                pe.wait_ge(S["blk_in"], blk * 32 + 32)
                for k in range(KT):
                    mm = transpose(xt_bank[:, k * P:(k + 1) * P], x_blk[:, k * P:(k + 1) * P])
                mm.then_inc(S["xt_ps"], 1)

            def gate_up(blk, e):
                hi, lo = gate_up_w(w_hi, e), gate_up_w(w_lo, e)
                pe.wait_ge(S["wlo_ok"], e * 2 + 2)
                pe.wait_ge(S["xtlo_ok"], blk + 1)
                for k in range(KT):
                    pe.matmul(gu_bank[:, 0:2 * INTER], xt_hi[:, k, :], hi[:, k, :], start=(k == 0), stop=False)
                    pe.matmul(gu_bank[:, 0:2 * INTER], xt_hi[:, k, :], lo[:, k, :], start=False, stop=False)
                    mm = pe.matmul(gu_bank[:, 0:2 * INTER], xt_lo[:, k, :], hi[:, k, :], start=False, stop=(k == KT - 1))
                mm.then_inc(S["gu_ps"], 1)

            def ht(blk):
                pe.wait_ge(S["h_ok"], blk * 2 + 2)
                for k in range(2):
                    mm = transpose(ht_bank[:, k * P:(k + 1) * P], h_sb[:, k * P:(k + 1) * P])
                mm.then_inc(S["ht_ps"], 1)

            def down(blk, e):
                hi, lo = down_w(w_hi, e), down_w(w_lo, e)
                pe.wait_ge(S["htlo_ok"], blk * 2 + 2)
                pe.wait_ge(S["yb_ok"], blk)
                pe.matmul(y_bank[:], ht_hi[:, 0:P], hi[:, 0, :], start=True, stop=False)
                pe.matmul(y_bank[:], ht_hi[:, 0:P], lo[:, 0, :], start=False, stop=False)
                pe.matmul(y_bank[:], ht_lo[:], hi[:, 0, :], start=False, stop=False)
                pe.matmul(y_bank[:], ht_hi[:, P:], hi[:, 1, :], start=False, stop=False)
                pe.matmul(y_bank[:], ht_hi[0:P // 2, P:], lo[0:P // 2, 1, :], start=False, stop=True).then_inc(S["y_ps"], 1)

            def expert(e, first):
                more = pe.value_load(tab[0:1, bass.ds(e, 1)], min_val=MIN_BLK - 1, max_val=EXP_BLK - 1)
                c = 0
                if not first:
                    before = pe.value_load(tab[0:1, bass.ds(e + LAST_BEFORE, 1)], min_val=0, max_val=MAX_BLK)
                    c = before + 1
                xt(c + 1)
                if not first:
                    down(before, e - 1)
                ht(c)
                with pe.Fori(0, more) as k:
                    blk = c + k
                    gate_up(blk + 1, e)
                    xt(blk + 2)
                    down(blk, e)
                    ht(blk + 1)
                gate_up(c + more + 1, e + 1)
                return c + more

            pe.wait_ge(S["tab_ok"], 1)
            xt(0)
            gate_up(0, 0)
            expert(0, True)
            with pe.Fori(1, NE) as e:
                expert(e, False)
            last = pe.value_load(tab[0:1, LAST_BEFORE + NE:LAST_BEFORE + NE + 1], min_val=0, max_val=MAX_BLK + 1)
            xt(last + 2)
            down(last, NE - 1)

        @block.scalar
        def _(act):
            def rs_seed(job, src, scale, eps, w=4):
                act.activation(rs_l[:, 0:w], src, ACT.Ln, scale=scale, bias=eps).then_inc(S["rs_ln"], 1)
                act.wait_ge(S["rs_ln"], job + 1)
                act.activation(rs_y[:, 0:w], rs_l[:, 0:w], ACT.Exp, scale=-0.5).then_inc(S["rs_seed"], 1)

            def norm_seed(at, name):
                act.wait_ge(S["ag_ok"], at.norm(name) * TT + TT)
                rs_seed(at.job(name), mv[:, :, 1], 1.0, EPS_LN)

            act.preload_act_table_set(EXP_SET)
            def norm_transposed(r, ks=range(KT)):
                for k in ks:
                    act.wait_ge(S["xT_ps"], r * KT + k + 1)
                    act.activation(xn_hi[:, k, :], bank_q[k % 2][:], ACT.Identity, scale=g_norm[:, k:k + 1]).then_inc(S["xnT_ok"], 1)

            def scan_input(r):
                act.wait_ge(S["scan_ok"], r * H)
                for e in range(ET):
                    act.wait_ge(S["inp_ps"], r * ET + e + 1)
                    act.activation(x_pad[:, e, DC - 1:], bank_q[e % 2][:], ACT.Copy).then_inc(S["xpad_ok"], 1)

            def scan_u(r):
                for e in range(ET):
                    act.wait_ge(S["conv_ok"], r * ET * DC + ET * (DC - 1) + e + 1)
                    act.activation(state[:, e, :], dbu[:, e, :], ACT.Silu, bias=conv_b[:, e:e + 1]).then_inc(S["u_ok"], 1)
                act.preload_act_table_set(EXP_SET)

            def keys_values(r, at):
                act.wait_ge(S["nw"], at.job("k") * 4)
                for t in range(TT):
                    act.wait_ge(S["kv_ps"], r * TT + (t // 2 * 2 + 2))
                    act.activation(junk[:, t, :], bank_t[t // 2][:, (t % 2) * 2 * DH:(t % 2) * 2 * DH + DH], ACT.Square,
                                   accum_out=rs_in[:, t:t + 1]).then_inc(S["ksq_ok"], 1)
                act.wait_ge(S["ksq_ok"], r * TT + TT)
                rs_seed(at.job("k"), rs_in[:], 1 / SCALE, EPS_L2 / SCALE)
                for half in range(2):
                    act.activation(v_aug[:, 2 * half:2 * half + 2, 0:DH], bank_t[half][:, :].rearrange("p (t n) -> p t n", t=2)[:, :, DH:],
                                   ACT.Copy).then_inc(S["v_ok"], 1)

            def scan_rows(r):
                act.wait_ge(S["xd_ps"], r + 1)
                act.activation(x_dbl[:], bank_t[1][0:XD, :], ACT.Copy).then_inc(S["xd_ok"], 1)

            def scan_params(r):
                for e in range(ET):
                    act.wait_ge(S["dt_ps"], r * ET + e + 1)
                    act.activation(dbu[:, e, :], bank_q[e % 2][:], ACT.Abs, bias=dt_b[:, e:e + 1]).then_inc(S["act_step"], 1)
                    act.activation(delta[:, e, :], bank_q[e % 2][:], ACT.Relu, bias=dt_b[:, e:e + 1]).then_inc(S["dt_ev"], 1)
                act.wait_ge(S["act_step"], r * ET + ET + 1)
                act.activation(dA3, dbu[:], ACT.Exp, scale=-1.0).then_inc(S["sp_e"], 1)

            def scan_log(r):
                act.wait_ge(S["wq_out1"], 2 * 16)
                act.wait_ge(S["sp_e"], r + 1)
                act.activation(du[:], dA3, ACT.Ln, bias=1.0).then_inc(S["sp_ln"], 1)

            def q_squares(r, piece, t, job):
                act.wait_ge(S["qp_ps"], r * H + piece + 1)
                act.wait_ge(S["nw"], job * 4)
                for j in range(4):
                    act.activation(junk[:, j, :], bank_q[t % 2][:, j * DH:(j + 1) * DH], ACT.Square,
                                   accum_out=rs_in[:, j:j + 1]).then_inc(S["qss_ok"], 1)
                act.wait_ge(S["qss_ok"], r * H * 4 + piece * 4 + 4)
                rs_seed(job, rs_in[:], 1 / 16, EPS_L2 / 4096)

            def q_scaled(r, first_piece, t, job):
                act.wait_ge(S["nw"], job * 4 + 4)
                act.wait_ge(S["qT_ps"], r * H + first_piece)
                for j in range(4):
                    act.activation(q_s[:, t, j, :], bank_q[t % 2][:, j * DH:(j + 1) * DH], ACT.Copy, scale=rs_r[:, j:j + 1]).then_inc(S["q_ok"], 1)

            def key_transposed(r):
                act.wait_ge(S["kT_ps"], r + 1)
                act.activation(k_t[:], bank_t[1][:], ACT.Copy).then_inc(S["kT_ok"], 1)
                act.activation(k_hi[:], bank_t[1][:], ACT.Copy).then_inc(S["kT_ok"], 1)

            def q_transposed(r, group, j):
                for i in (j, j + 1):
                    act.wait_ge(S["qT_ps"], r * H + group * 4 + i + 1)
                    act.activation(q_t[:, i, :] if i < 2 else q_hi[:, i - 2, :], bank_qT[i][:], ACT.Copy).then_inc(S["qT_ok"], 1)

            def split_wq(g):
                act.wait_ge(S["wq_in"], 16)
                act.activation(wq_hi[g], raw_of(g), ACT.Copy).then_inc(S["wqhi_ok"], 1)

            def exps(r, h, ks=range(KT)):
                act.wait_ge(S["pv_ps"], r * H * 2 + h * 2)
                for k in ks:
                    act.wait_ge(S["s_ps"], r * H * KT + h * KT + (k + 1))
                    act.activation(probs[:, k, :], bank_s[k % 2][:], ACT.Exp).then_inc(S["exp_ok"], 1)

            def decays(r, n):
                act.wait_ge(S["scan_ok"], r * DS + n)
                for e in range(ET):
                    act.activation(dA3[:, e, 1:], delta[:, e, 1:], ACT.Exp,
                                   scale=neg_a[:, bass.ds(n, 1), e:e + 1].rearrange("p a c -> p (a c)")).then_inc(S["dA_ok"], 1)

            def first_decays(r):
                act.wait_ge(S["dve_step"], r + 2)
                decays(r, 0)

            def head(r, h, group, j, last_group, at):
                def squares(t):
                    q_squares(r, group * 4 + 4 + t, t, at.job("q4") + group * 4 + t)

                def scaled(t):
                    q_scaled(r, group * 4 + 4, t, at.job("q4") + group * 4 + t)

                def divide():
                    act.wait_ge(S["oT_ps"], r * H + h)
                    for t in range(TT):
                        act.wait_ge(S["den_ok"], r * H * 2 + h * 2 + (t // 2 + 1))
                        act.activation(o_s[:, t, :], bank_o[t // 2][:, (t % 2) * (DH + 1):(t % 2) * (DH + 1) + DH], ACT.Copy,
                                       scale=den[:, t:t + 1]).then_inc(S["o_ok"], 1)

                if last_group and j == 3:
                    divide()
                elif last_group or j != 2:
                    if not last_group and j == 1:
                        squares(1)
                    if not last_group and j == 3:
                        q_transposed(r, group + 1, 0)
                    exps(r, h + 1, range(2))
                    divide()
                    exps(r, h + 1, range(2, KT))
                    if not last_group and j == 0:
                        squares(0)
                    if not last_group and j == 1:
                        scaled(1)
                else:
                    squares(2)
                    divide()
                    scaled(2)
                    squares(3)
                    exps(r, h + 1)
                    scaled(3)
                if j == 0:
                    act.wait_ge(S["slot_ok"], r)
                act.wait_ge(S["oT_ps"], r * H + h + 1)
                act.activation(o_t[:, bass.ds(h, 1), :].rearrange("p a t -> p (a t)"), bank_t[1][:], ACT.Copy).then_inc(S["oT_ok"], 1)
                if not last_group and j == 3:
                    q_transposed(r, group + 1, 2)
                if not last_group:
                    decays(r, h + 1)
                elif j in INPUTS_IN_LAST_GROUP:
                    decays(r, INPUTS_IN_LAST_GROUP[j])
                if not last_group and j == 0:
                    scaled(0)

            def load_part(e, part):
                if not (isinstance(e, int) and e + part == 0):
                    act.wait_ge(S["w_in"], (e * 2 + part) * 16)
                act.dma_start(part_w(w_raw, e, part, N_RAW),
                              a["w_exp"][bass.ds(e % NE, 1), :, W_PARTS[part][0]:W_PARTS[part][1]].rearrange("o p n -> (o p) n")).then_inc(S["w_in"], 16)

            at = first_places()
            norm_seed(at, "ln1")
            norm_seed(at, "ln2")
            act.wait_ge(S["w_in_sb"], 16 * N_W)
            act.activation(neg_a[:], neg_a[:], ACT.Exp).then_inc(S["act_step"], 1)
            act.wait_ge(S["act_step"], 1)
            act.activation(neg_a[:], neg_a[:], ACT.Identity, scale=-1.0).then_inc(S["neg_a_ok"], 1)
            act.wait_ge(S["neg_a_ok"], 1)
            scan_input(0)
            scan_u(0)
            norm_transposed(0, range(2))
            act.wait_ge(S["wkv_in"], 16)
            act.activation(wkv_hi[:], wkv_raw, ACT.Copy).then_inc(S["wkvhi_ok"], 1)
            for g in SPLIT_ORDER[:2]:
                split_wq(g)
            norm_transposed(0, range(2, KT))
            scan_rows(0)
            split_wq(SPLIT_ORDER[2])
            scan_params(0)
            scan_log(0)
            split_wq(SPLIT_ORDER[3])
            keys_values(0, at)
            for t in range(TT):
                q_squares(0, t, t, at.job(f"q{t}"))
                q_scaled(0, 0, t, at.job(f"q{t}"))
            key_transposed(0)
            q_transposed(0, 0, 0)
            q_transposed(0, 0, 2)
            exps(0, 0)
            first_decays(0)
            wq_stored(act)

            def row(b, at, last):
                with act.Fori(0, G - 1) as g:
                    for j in range(4):
                        head(b, g * 4 + j, g, j, False, at)
                for j in range(4):
                    head(b, (G - 1) * 4 + j, G - 1, j, True, at)
                decays(b, DS - 2)
                if not last:
                    norm_seed(at, "ln1")
                    norm_seed(at, "ln2")
                    norm_transposed(b + 1)
                decays(b, DS - 1)
                if last:
                    act.wait_ge(S["qp_ps"], NB * H)
                    for e in range(4):
                        for part in range(2):
                            load_part(e, part)
                if not last:
                    keys_values(b + 1, at)
                    scan_input(b + 1)
                    scan_u(b + 1)
                    for t in range(2):
                        q_squares(b + 1, t, t, at.job(f"q{t}"))
                        q_scaled(b + 1, 0, t, at.job(f"q{t}"))
                    scan_rows(b + 1)
                    scan_params(b + 1)
                    scan_log(b + 1)
                    key_transposed(b + 1)
                norm_seed(at, "o")
                norm_seed(at, "z")
                act.wait_ge(S["zr_ok"], b + 1)
                for t in range(TT):
                    act.activation(end_s[:, t, :], x_sb[:, t, :], ACT.Silu, scale=rs_r[:, t:t + 1], bias=z_bias[:, t:t + 1]).then_inc(S["sz_ok"], 1)
                act.preload_act_table_set(EXP_SET)
                if not last:
                    q_squares(b + 1, 2, 2, at.job("q2"))
                    q_scaled(b + 1, 0, 2, at.job("q2"))
                norm_seed(at, "f")
                act.wait_ge(S["ys_ok"], b * TT + TT)
                for k in range(KT):
                    act.wait_ge(S["fT_ps"], b * KT + k + 1)
                    act.activation(end_s[:, k, :], bank_o[k % 2][:], ACT.Copy).then_inc(S["fT_ok"], 1)
                if not last:
                    q_squares(b + 1, 3, 3, at.job("q3"))
                    q_scaled(b + 1, 0, 3, at.job("q3"))
                    first_decays(b + 1)
                act.wait_ge(S["lgs_ok"], b + 1)
                act.activation(r["pr"][:], r["lg"][:], ACT.Exp).then_inc(S["rexp_ok"], 1)
                if not last:
                    q_transposed(b + 1, 0, 0)
                    q_transposed(b + 1, 0, 2)
                    exps(b + 1, 0)

            each_row(act, row)

            xt_bank, gu_bank, ht_bank, y_bank = bank_q[0], bank_s[0], bank_s[1], bank_o[0]

            def split(e, part):
                act.wait_ge(S["w_in"], (e * 2 + part + 1) * 16)
                act.activation(part_w(w_hi, e, part, N_SPLIT), part_w(w_raw, e, part, N_RAW), ACT.Copy).then_inc(S["whi_ok"], 1)

            def xt(blk):
                act.wait_ge(S["xt_ps"], blk + 1)
                act.activation(xt_hi[:], xt_bank[:].rearrange("p (k t) -> p k t", k=KT), ACT.Copy).then_inc(S["xthi_ok"], 1)

            def silu(blk):
                act.wait_ge(S["gu_ps"], blk + 1)
                act.activation(silu_g[:], gu_bank[:, 0:INTER], ACT.Silu).then_inc(S["silu_ok"], 1)

            def ht(blk):
                act.wait_ge(S["ht_ps"], blk + 1)
                act.activation(ht_hi[:], ht_bank[:, 0:2 * P], ACT.Copy).then_inc(S["hthi_ok"], 1)

            def weigh(blk, e):
                act.wait_ge(S["added"], blk * 16)
                act.wait_ge(S["y_ps"], blk + 1)
                act.activation(y_both[:, bass.ds(blk % 2, 1), :].rearrange("p o d -> p (o d)"), y_bank[:], ACT.Copy,
                               scale=meta[:, bass.ds(blk, 1), bass.ds(e, 1)].rearrange("p o c -> p (o c)")).then_inc(S["yb_ok"], 1)

            act.wait_ge(S["slot_ok"], NB)
            for e in range(3):
                for part in range(2):
                    split(e, part)
            act.wait_ge(S["tab_ok"], 1)
            xt(0)
            silu(0)
            xt(1)
            with act.Fori(0, NE) as e:
                more, c = span(act, e)
                ht(c)
                split(e + 3, 0)
                act.wait_ge(S["wlo_ok"], e * 2 + 2)
                load_part(e + 4, 0)
                with act.Fori(0, more) as k:
                    blk = c + k
                    silu(blk + 1)
                    xt(blk + 2)
                    weigh(blk, e)
                    ht(blk + 1)
                split(e + 3, 1)
                load_part(e + 4, 1)
                silu(c + more + 1)
                xt(c + more + 2)
                weigh(c + more, e)

        @block.vector
        def _(dve):
            chain = S["chain"]

            def newton(job, src, scale, eps, w=4):
                n = job * 4
                dve.wait_ge(S["rs_seed"], job + 1)
                dve.tensor_scalar(rs_x[:, 0:w], src, scale, eps, ALU.mult, ALU.add).then_inc(S["nw"], 1)
                dve.tensor_tensor(rs_t[:, 0:w], rs_y[:, 0:w], rs_y[:, 0:w], ALU.mult).then_inc(S["nw"], 1)
                dve.wait_ge(S["nw"], n + 2)
                dve.scalar_tensor_tensor(out=rs_t[:, 0:w], in0=rs_t[:, 0:w], scalar=-0.5, in1=rs_x[:, 0:w], op0=ALU.mult, op1=ALU.mult).then_inc(S["nw"], 1)
                dve.wait_ge(S["nw"], n + 3)
                dve.scalar_tensor_tensor(out=rs_r[:, 0:w], in0=rs_t[:, 0:w], scalar=1.5, in1=rs_y[:, 0:w], op0=ALU.add, op1=ALU.mult).then_inc(S["nw"], 1)
                dve.wait_ge(S["nw"], n + 4)

            def norm_stats(at, name, src, ready=None):
                n = at.norm(name) * TT
                for t in range(TT):
                    if ready:
                        ready(t)
                    dve.bn_stats(st[:, t, :], src(t)).then_inc(S["bn_ok"], 1)
                for t in range(TT):
                    wait_apart(dve, S["bn_ok"], n + t + 1)
                    dve.bn_aggr(mv[:, t, :], st[:, t, :]).then_inc(S["ag_ok"], 1)
                dve.wait_ge(S["ag_ok"], n + TT)
                newton(at.job(name), mv[:, :, 1], 1.0, EPS_LN)

            def apply(t, dst, src):
                return dve.tensor_scalar(dst, src, mv[:, t, 0:1], rs_r[:, t:t + 1], ALU.subtract, ALU.mult)

            dve.memset(v_aug[:, :, DH:], 1.0).then_inc(S["bc_free"], 1)
            dve.memset(cs[:, 0:2, :], 0.0).then_inc(S["dve_step"], 1)
            dve.wait_ge(S["dve_step"], 1)

            def linked(at):
                def link(ins, apart=False, wait=True):
                    at.steps += 1
                    ins.then_inc(chain, 1)
                    if not wait:
                        return
                    if apart:
                        wait_apart(dve, chain, at.step0 + at.steps)
                    else:
                        dve.wait_ge(chain, at.step0 + at.steps)
                return link

            def first_norms(r, at):
                dve.wait_ge(S["xfirst_in"], r * 16 + 16)
                norm_stats(at, "ln1", lambda t: x_first[:, t, :])
                for t in range(TT):
                    apply(t, norm[:, t, :], x_first[:, t, :]).then_inc(S["ln_a"], 1)
                norm_stats(at, "ln2", lambda t: norm[:, t, :], ready=lambda t: dve.wait_ge(S["ln_a"], r * TT + t + 1))
                for t in range(TT):
                    apply(t, norm[:, t, :], norm[:, t, :]).then_inc(S["ln_x"], 1)

            def convolution(r, link):
                link(dve.memset(x_pad[:, :, 0:DC - 1], 0.0))
                for pair in range(ET // 2):
                    for c in range(DC):
                        for e in (2 * pair, 2 * pair + 1):
                            if c == 0:
                                dve.wait_ge(S["xpad_ok"], r * ET + e + 1)
                                ins = dve.tensor_scalar(dbu[:, e, :], x_pad[:, e, 0:T], conv_w[:, e, 0:1], None, ALU.mult)
                            else:
                                dve.wait_ge(S["conv_ok"], r * ET * DC + pair * 2 * DC + (c - 1) * 2 + e % 2 + 1)
                                ins = dve.scalar_tensor_tensor(out=dbu[:, e, :], in0=x_pad[:, e, c:c + T], scalar=conv_w[:, e, c:c + 1], in1=dbu[:, e, :],
                                                               op0=ALU.mult, op1=ALU.add)
                            ins.then_inc(S["conv_ok"], 1)

            def split_wq(g):
                dve.wait_ge(S["wqhi_ok"], SPLIT_ORDER.index(g) + 1)
                dve.tensor_tensor(wq_lo[g], raw_of(g), wq_hi[g].bitcast(F32), ALU.subtract).then_inc(S["wqlo_ok"], 1)

            def norm_lo(r, ks=range(KT)):
                for k in ks:
                    dve.wait_ge(S["xnT_ok"], r * KT + k + 1)
                    dve.scalar_tensor_tensor(out=xn_lo[:, k, :], in0=bank_q[k % 2][:], scalar=g_norm[:, k:k + 1], in1=xn_hi[:, k, :].bitcast(F32),
                                             op0=ALU.mult, op1=ALU.subtract).then_inc(S["xlo_ok"], 1)

            def k_rest(r):
                dve.wait_ge(S["kT_ok"], r * 2 + 2)
                dve.tensor_tensor(k_lo[:], bank_t[1][:], k_hi[:].bitcast(F32), ALU.subtract).then_inc(S["klo_ok"], 1)

            def q_rest(r, group):
                for i in (2, 3):
                    dve.wait_ge(S["qT_ok"], r * H + group * 4 + i + 1)
                    dve.tensor_tensor(q_lo[:, i - 2, :], bank_qT[i][:], q_hi[:, i - 2, :].bitcast(F32), ALU.subtract).then_inc(S["qlo_ok"], 1)

            def keys(r, at):
                newton(at.job("k"), rs_in[:], 1 / SCALE, EPS_L2 / SCALE)
                for half in range(2):
                    dve.wait_ge(S["v_ok"], r * 2 + half + 1)
                    dve.tensor_tensor(k_n[:, 2 * half:2 * half + 2, :], bank_t[half][:, :].rearrange("p (t n) -> p t n", t=2)[:, :, 0:DH],
                                      rs_r[:, 2 * half:2 * half + 2].unsqueeze(2).to_broadcast([P, 2, DH]), ALU.mult).then_inc(S["kn_ok"], 1)

            def q_norm(r, group, t, job):
                dve.wait_ge(S["qss_ok"], r * H * 4 + group * 16 + (t * 4 + 4))
                newton(job, rs_in[:], 1 / 16, EPS_L2 / 4096)

            def deltas(r, link, between=(lambda: None,) * 2):
                dve.wait_ge(S["sp_ln"], r + 1)
                link(dve.tensor_scalar(dbu[:], dA3, 1.0, -1.0, ALU.add, ALU.add))
                between[0]()
                link(dve.tensor_tensor(dbu[:], dA3, dbu[:], ALU.subtract))
                between[1]()
                link(dve.tensor_tensor(dbu[:], dbu[:], du[:], ALU.add))
                link(dve.tensor_tensor(delta[:], delta[:], dbu[:], ALU.add))
                link(dve.tensor_tensor(du[:], delta[:], state[:], ALU.mult))

            def skip(r):
                for e in range(ET):
                    dve.tensor_scalar(y[:, e, :], state[:, e, :], d_skip[:, e:e + 1], None, ALU.mult)
                dve.memset(dA3[:, :, 0:1], 0.0).then_inc(S["dve_step"], 1)
                dve.wait_ge(S["dve_step"], r + 2)

            def state_input(r, n, fill):
                dve.wait_ge(S[f"bc_in{fill[0]}"], r * (DS // 2) * 32 + fill[1] * 32 + 32)
                dve.tensor_tensor(dbu[:], du[:], b_bc[:, fill[0]:fill[0] + 1, :].to_broadcast([P, ET, T]), ALU.mult).then_inc(S["dbu_ok"], 1)

            def state_scan(r, n):
                dve.wait_ge(S["dA_ok"], r * DS * ET + n * ET + ET)
                dve.wait_ge(S["dbu_ok"], r * DS + n + 1)
                dve.tensor_tensor_scan(state[:].rearrange("p e t -> p (e t)"), dA, dbu[:].rearrange("p e t -> p (e t)"), 0.0,
                                       ALU.mult, ALU.add).then_inc(S["scan_ok"], 1)

            def state_product(r, n, i):
                dve.wait_ge(S["scan_ok"], r * DS + n + 1)
                dve.tensor_tensor(dbu[:], state[:], c_bc[:, i:i + 1, :].to_broadcast([P, ET, T]), ALU.mult).then_inc(S["bc_free"], 1)

            def state_sum(r, n):
                dve.wait_ge(S["bc_free"], r * DS + n + 2)
                dve.tensor_tensor(y[:], y[:], dbu[:], ALU.add).then_inc(S["y_ok"], 1)
                dve.wait_ge(S["y_ok"], r * DS + n + 1)

            def head(r, h, group, j, last_group, at):
                def next_norm(t):
                    q_norm(r, group + 1, t, at.job("q4") + group * 4 + t)

                n = None
                if not last_group:
                    n, i = h, j % 2
                elif j in STATES_IN_LAST_GROUP:
                    n = STATES_IN_LAST_GROUP[j]
                    i = n % 2
                for half in range(2):
                    o = bank_o[half][:, 0:2 * (DH + 1)].rearrange("p (t n) -> p t n", t=2)
                    dve.wait_ge(S["pv_ps"], r * H * 2 + h * 2 + (half + 1))
                    dve.reciprocal(den[:, 2 * half:2 * half + 2].unsqueeze(2), o[:, :, DH:]).then_inc(S["den_ok"], 1)
                if not last_group and j == 2:
                    next_norm(2)
                if n is not None:
                    state_scan(r, n)
                if not last_group and j == 1:
                    next_norm(1)
                if n is not None:
                    state_product(r, n, i)
                if not last_group and j == 2:
                    next_norm(3)
                if n is not None:
                    state_sum(r, n)
                if not last_group and j == 0:
                    next_norm(0)
                if not last_group and j == 3:
                    q_rest(r, group + 1)
                if not last_group:
                    state_input(r, h + 1, ((j + 1) % 2, group * 2 + (j + 1) // 2))
                elif j in INPUTS_IN_LAST_GROUP:
                    n = INPUTS_IN_LAST_GROUP[j]
                    state_input(r, n, (n % 2, n // 2))

            at = first_places()
            link = linked(at)
            first_norms(0, at)
            dve.wait_ge(S["w_in_sb"], 16 * N_W)
            convolution(0, link)
            norm_lo(0, range(2))
            dve.wait_ge(S["wkvhi_ok"], 1)
            dve.tensor_tensor(wkv_lo[:], wkv_raw, wkv_hi[:].bitcast(F32), ALU.subtract).then_inc(S["wkvlo_ok"], 1)
            for g in SPLIT_ORDER[:2]:
                split_wq(g)
            norm_lo(0, range(2, KT))
            split_wq(SPLIT_ORDER[2])
            keys(0, at)
            for t in range(TT - 2):
                q_norm(0, 0, t, at.job(f"q{t}"))
                if t == 0:
                    split_wq(SPLIT_ORDER[3])
            deltas(0, link, [lambda: q_norm(0, 0, TT - 2, at.job(f"q{TT - 2}")), lambda: q_norm(0, 0, TT - 1, at.job(f"q{TT - 1}"))])
            k_rest(0)
            q_rest(0, 0)
            wq_stored(dve)
            skip(0)
            state_input(0, 0, (0, 0))
            assert at.steps == FIRST_STEPS, at.steps

            def row(b, at, last):
                link = linked(at)
                with dve.Fori(0, G - 1) as g:
                    for j in range(4):
                        head(b, g * 4 + j, g, j, False, at)
                for j in range(4):
                    head(b, (G - 1) * 4 + j, G - 1, j, True, at)
                if not last:
                    first_norms(b + 1, at)
                    norm_lo(b + 1)
                for n in range(DS - 2, DS):
                    state_input(b, n, (n % 2, n // 2))
                    state_scan(b, n)
                    state_product(b, n, n % 2)
                    state_sum(b, n)
                if not last:
                    keys(b + 1, at)
                    convolution(b + 1, link)
                    for t in range(2):
                        q_norm(b + 1, 0, t, at.job(f"q{t}"))
                    deltas(b + 1, link)
                    k_rest(b + 1)
                norm_stats(at, "o", lambda t: (bank_o + bank_s)[t][:], ready=lambda t: dve.wait_ge(S["op_ps"], b * TT + t + 1))
                for t in range(TT):
                    dve.scalar_tensor_tensor(out=end_s[:, t, :], in0=(bank_o + bank_s)[t][:], scalar=mv[:, t, 0:1], in1=g_out[:],
                                             op0=ALU.subtract, op1=ALU.mult).then_inc(S["on_ok"], 1)
                dve.wait_ge(S["x_in"], b * 16 + 16)
                for t in range(TT):
                    dve.wait_ge(S["on_ok"], b * TT + t + 1)
                    dve.scalar_tensor_tensor(out=x_sb[:, t, :], in0=end_s[:, t, :], scalar=rs_r[:, t:t + 1], in1=x_sb[:, t, :],
                                             op0=ALU.mult, op1=ALU.add).then_inc(S["x1_ok"], 1)
                norm_stats(at, "z", lambda t: x_sb[:, t, :], ready=lambda t: dve.wait_ge(S["x1_ok"], b * TT + t + 1))
                dve.scalar_tensor_tensor(out=z_bias[:], in0=mv[:, :, 0], scalar=-1.0, in1=rs_r[:], op0=ALU.mult, op1=ALU.mult).then_inc(S["zr_ok"], 1)
                for t in range(TT):
                    dve.wait_ge(S["sz_ok"], b * TT + t + 1)
                    dve.tensor_tensor(y[:, t, :], y[:, t, :], end_s[:, t, :], ALU.mult).then_inc(S["ys_ok"], 1)
                if not last:
                    q_norm(b + 1, 0, 2, at.job("q2"))
                for t in range(TT):
                    dve.wait_ge(S["yT_ps"], b * TT + t + 1)
                    dve.tensor_tensor(x_sb[:, t, :], x_sb[:, t, :], bank_s[t % 2][:], ALU.add).then_inc(S["x2_ok"], 1)
                norm_stats(at, "f", lambda t: x_sb[:, t, :], ready=lambda t: dve.wait_ge(S["x2_ok"], b * TT + t + 1))
                for i in range(2):
                    dve.wait_ge(S[f"sent{i}"], b * SENT)
                for t in range(TT):
                    apply(t, x_row[:, t, 0:D], x_sb[:, t, :]).then_inc(S["xf_ok"], 1)
                link(dve.tensor_copy(x_row[:, :, ID_COL:ID_COL + 1].bitcast(I32), const[:, bass.ds(b * TT + C_TOK, TT)].unsqueeze(2)))
                link(dve.memset(x_row[:, :, ID_COL + 1:], 0.0))
                if not last:
                    skip(b + 1)
                    state_input(b + 1, 0, (0, 0))
                    q_norm(b + 1, 0, 3, at.job("q3"))

                wide = lambda t: t[:].unsqueeze(2).to_broadcast([P, TT, NE])
                exp_row = lambda c: const[:, c:c + NE].unsqueeze(1).to_broadcast([P, TT, NE])
                tt, ts = dve.tensor_tensor, dve.tensor_scalar
                red = lambda dst, src, op, wait=True: link(dve.tensor_reduce(r1[dst][:].unsqueeze(2), src, AX, op), wait=wait)
                dve.wait_ge(S["lg_ps"], b + 1)
                logits = bank_o[0][:, 0:TT * NE].rearrange("p (t e) -> p t e", t=TT)
                red("mx", logits, ALU.max)
                tt(r["lg"][:], logits, wide(r1["mx"]), ALU.subtract).then_inc(S["lgs_ok"], 1)
                dve.wait_ge(S["rexp_ok"], b + 1)
                red("sm", r["pr"][:], ALU.add)
                link(dve.reciprocal(r1["rc"][:], r1["sm"][:]))
                link(tt(r["pr"][:], r["pr"][:], wide(r1["rc"]), ALU.mult), True)
                for t in range(TT):
                    link(dve.max(p8[:, t, :], r["pr"][:, t, :]), True, wait=(t == TT - 1))
                for t in range(TT):
                    link(dve.match_replace(r["rep"][:, t, :], p8[:, t, :], r["pr"][:, t, :], -1.0), wait=False)
                red("s8", p8[:], ALU.add)
                link(ts(r1["s8"][:], r1["s8"][:], 1e-12, None, ALU.max), wait=False)
                link(ts(r["sel"][:], r["rep"][:], 0.0, None, ALU.is_lt))
                if not last:
                    q_rest(b + 1, 0)
                link(dve.reciprocal(r1["r8"][:], r1["s8"][:]), wait=False)
                link(ts(r["ct"][:], r["sel"][:], 3.0e38, -3.0e38, ALU.mult, ALU.add), wait=False)
                link(tt(r["tvn"][:], r["pr"][:], r["sel"][:], ALU.mult))
                link(tt(r["tvn"][:], r["tvn"][:], wide(r1["r8"]), ALU.mult))
                link(ts(r["scl"][:], r["tvn"][:], alpha[:, 0:1], None, ALU.mult))
                link(dve.scalar_tensor_tensor(out=r["act"][:], in0=r["scl"][:], scalar=TAU, in1=r["sel"][:], op0=ALU.is_ge, op1=ALU.mult), wait=False)
                link(tt(r["fb"][:], r["scl"][:], r["ct"][:], ALU.add))
                red("any", r["act"][:], ALU.max, wait=False)
                red("mx2", r["fb"][:], ALU.max)
                link(ts(r1["any"][:], r1["any"][:], -1.0, 1.0, ALU.mult, ALU.add), wait=False)
                link(tt(r["cand"][:], r["fb"][:], wide(r1["mx2"]), ALU.is_equal))
                link(tt(r["ct"][:], r["tvn"][:], r["cand"][:], ALU.mult))
                link(dve.scalar_tensor_tensor(out=r["ct"][:], in0=r["cand"][:], scalar=-1.0, in1=r["ct"][:], op0=ALU.add, op1=ALU.add))
                red("m2", r["ct"][:], ALU.max)
                link(tt(r["cand"][:], r["ct"][:], wide(r1["m2"]), ALU.is_equal))
                link(tt(r["fb"][:], r["cand"][:], exp_row(C_REV), ALU.mult))
                red("m3", r["fb"][:], ALU.max)
                link(tt(r["fb"][:], r["fb"][:], wide(r1["m3"]), ALU.is_equal))
                link(tt(r["fb"][:], r["fb"][:], wide(r1["any"]), ALU.mult))
                link(tt(r["act"][:], r["act"][:], r["fb"][:], ALU.max))
                tt(cs[:, 2:4, :], cs[:, 0:2, :], r["act"][:, 0:2, :], ALU.add).then_inc(S["act_ok"], 1)
                link(tt(r["wts"][:], r["tvn"][:], r["act"][:], ALU.mult))
                dve.wait_ge(S["act_ok"], b + 1)
                link(tt(cs[:, 4:6, :], cs[:, 2:4, :], r["act"][:, 2:4, :], ALU.add), wait=False)
                red("s2", r["wts"][:], ALU.add)
                link(ts(r1["s2"][:], r1["s2"][:], 1e-12, None, ALU.max))
                link(dve.reciprocal(r1["rw"][:], r1["s2"][:]))
                link(tt(x_row[:, :, W_COL:W_COL + NE], r["wts"][:], wide(r1["rw"]), ALU.mult))
                dve.wait_ge(S["rank_ps"], b + 1)
                link(tt(r["slv"][:], bank_t[0][:, 0:TT * NE].rearrange("p (t e) -> p t e", t=TT), exp_row(C_BASE), ALU.add))
                link(tt(r["slv"][:], r["slv"][:], r["act"][:], ALU.mult))
                link(dve.tensor_copy(cs[:, 0:2, :], cs[:, TT:, :]), True)
                for t in range(TT):
                    link(dve.max(s8[:, t, :], r["slv"][:, t, :]), wait=(t == TT - 1))
                link(ts(t8[:], s8[:], 0.0, const[:, C_TRASH:C_TRASH + 1], ALU.is_equal, ALU.mult))
                link(dve.scalar_tensor_tensor(out=t8[:], in0=t8[:], scalar=-1.0, in1=s8[:], op0=ALU.add, op1=ALU.add))
                dve.tensor_copy(slot[:], t8[:]).then_inc(S["slot_ok"], 1)
                dve.wait_ge(S["slot_ok"], b + 1)
                assert last or at.steps == ROW_STEPS, at.steps

            each_row(dve, row)

            xt_bank, gu_bank, ht_bank = bank_q[0], bank_s[0], bank_s[1]
            steps = [0]

            def step(ins):
                steps[0] += 1
                ins.then_inc(S["cnt_step"], 1)
                dve.wait_ge(S["cnt_step"], steps[0])

            step(dve.memset(pad[:], 0.0))
            step(dve.tensor_copy(pad[:, ID_COL:ID_COL + 1].bitcast(I32), const[:, C_PAD:C_PAD + 1]))
            dve.wait_ge(S["cnt_ps"], 1)
            step(dve.tensor_copy(n_f[:], bank_q[1][:, 0:2 * NE].rearrange("p (i e) -> p i e", i=2)))
            step(dve.tensor_scalar(list_f[:], n_f[:], 1.0, float(P - 1), ALU.max, ALU.add))
            step(dve.tensor_copy(list_i[:], list_f[:]))
            step(dve.tensor_scalar(list_i[:], list_i[:], P.bit_length() - 1, None, ALU.arith_shift_right))
            step(dve.tensor_copy(list_f[:], list_i[:]))
            step(dve.tensor_tensor(nb_f[:], list_f[:, 0, :], list_f[:, 1, :], ALU.add))
            step(dve.tensor_tensor_scan(cum_f[:], ones[:, 0:NE], nb_f[:], 0.0, ALU.mult, ALU.add))
            step(dve.tensor_copy(odd_i[:], cum_f[:, NE - 1:NE]))
            step(dve.tensor_scalar(odd_i[:], odd_i[:], 1, None, ALU.bitwise_and))
            step(dve.tensor_copy(odd_f[:], odd_i[:]))
            step(dve.tensor_tensor(cum_f[:], cum_f[:], nb_f[:], ALU.subtract))
            step(dve.tensor_tensor(nb_f[:, NE - 1:NE], nb_f[:, NE - 1:NE], odd_f[:], ALU.add))
            step(dve.tensor_tensor(list_f[:, 1, NE - 1:NE], list_f[:, 1, NE - 1:NE], odd_f[:], ALU.add))
            step(dve.tensor_tensor(odd_f[:], nb_f[:, NE - 1:NE], cum_f[:, NE - 1:NE], ALU.add))
            step(dve.tensor_scalar(odd_f[:], odd_f[:], 0.5, None, ALU.mult))
            step(dve.tensor_scalar(nb_f[:], nb_f[:], -1.0, None, ALU.add))
            for col, values in ((T_MORE, nb_f[:]), (T_BEFORE, cum_f[:])):
                step(dve.tensor_copy(tab[:, col:col + NE], values))
            for col, values in ((T_TOKENS, n_f[:]), (T_BLOCKS, list_f[:])):
                step(dve.tensor_copy(tab[:, col:col + 2 * NE].rearrange("p (i e) -> p i e", i=2), values))
            step(dve.tensor_copy(tab[:, T_PAIRS:T_PAIRS + 1], odd_f[:]))
            step(dve.tensor_scalar(odd_f[:], odd_f[:], 2.0, -1.0, ALU.mult, ALU.add))
            step(dve.tensor_copy(tab[:, LAST_BEFORE + NE:], odd_f[:]))
            step(dve.tensor_scalar(cum_f[:], cum_f[:], 1.0, -1.0, ALU.max, ALU.add))
            dve.tensor_copy(tab[:, LAST_BEFORE:LAST_BEFORE + NE], cum_f[:]).then_inc(S["tab_ok"], 1)
            dve.wait_ge(S["tab_ok"], 1)

            def split(e, part):
                dve.wait_ge(S["whi_ok"], e * 2 + (part + 1))
                dve.tensor_tensor(part_w(w_lo, e, part, N_SPLIT), part_w(w_raw, e, part, N_RAW), part_w(w_hi, e, part, N_SPLIT).bitcast(F32),
                                  ALU.subtract).then_inc(S["wlo_ok"], 1)

            def xt(blk):
                dve.wait_ge(S["xthi_ok"], blk + 1)
                dve.tensor_tensor(xt_lo[:], xt_bank[:].rearrange("p (k t) -> p k t", k=KT), xt_hi[:].bitcast(F32), ALU.subtract).then_inc(S["xtlo_ok"], 1)

            def hidden(blk):
                half = P // 2
                dve.wait_ge(S["silu_ok"], blk + 1)
                dve.tensor_tensor(h_sb[:, 0:P], silu_g[:, 0:P], gu_bank[:, INTER:INTER + P], ALU.mult).then_inc(S["h_ok"], 1)
                twice = lambda t: t.unsqueeze(1).to_broadcast([P, 2, half])
                dve.tensor_tensor(h_sb[:, P:].rearrange("p (o c) -> p o c", o=2), twice(silu_g[:, P:]), twice(gu_bank[:, INTER + P:2 * INTER]),
                                  ALU.mult).then_inc(S["h_ok"], 1)

            def ht(blk):
                half = P // 2
                dve.wait_ge(S["hthi_ok"], blk + 1)
                dve.tensor_tensor(ht_lo[:], ht_bank[:, 0:P], ht_hi[:, 0:P].bitcast(F32), ALU.subtract).then_inc(S["htlo_ok"], 1)
                dve.tensor_tensor(ht_hi[half:, P:], ht_bank[half:, P:2 * P], ht_hi[half:, P:].bitcast(F32), ALU.subtract).then_inc(S["htlo_ok"], 1)

            for e in range(2):
                for part in range(2):
                    split(e, part)
            xt(0)
            hidden(0)
            xt(1)
            with dve.Fori(0, NE) as e:
                more, c = span(dve, e)
                ht(c)
                split(e + 2, 0)
                with dve.Fori(0, more) as k:
                    blk = c + k
                    hidden(blk + 1)
                    xt(blk + 2)
                    ht(blk + 1)
                split(e + 2, 1)
                hidden(c + more + 1)
                xt(c + more + 2)

        @block.gpsimd
        def _(pool):
            def load_wq(r, group):
                wait_apart(pool, S["qp_ps"], r * H + group * 4)
                for half in range(2):
                    ks = slice(half * KT // 2, (half + 1) * KT // 2)
                    pool.dma_start(wq[:, :, ks], wq_dram[group][:, :, ks]).then_inc(S[f"wq_in{half}"], 16)

            def send(b, half):
                for k in range(TOPK):
                    for i in range(2):
                        if half + k > 0:
                            wait_apart(pool, S[f"sent{i}"], b * SENT + (half * TOPK + k) * 16)
                        t = 2 * half + i
                        pool.indirect_dma_start(out=slots[i], out_offset=bass.IndirectOffsetOnAxis(ap=slot[:, t, k:k + 1].bitcast(U32), axis=0),
                                                in_=x_row[:, t, :], in_offset=None).then_inc(S[f"sent{i}"], 16)

            wq_stored(pool)
            for group in range(1, G):
                load_wq(0, group)
            with pool.Fori(0, NB - 1) as b:
                for group in range(2):
                    load_wq(b + 1, group)
                wait_apart(pool, S["slot_ok"], b + 1)
                send(b, 0)
                load_wq(b + 1, 2)
                send(b, 1)
                load_wq(b + 1, 3)
            wait_apart(pool, S["slot_ok"], NB)
            for half in range(2):
                send(NB - 1, half)

            pool.wait_ge(S["tab_ok"], 1)
            pairs = pool.value_load(tab[0:1, T_PAIRS:T_PAIRS + 1], min_val=NE, max_val=MAX_BLK // 2 + 1)
            pool.dma_start(out[NTOK:, :], pad[:, 0:D]).then_inc(S["added"], 16)
            with pool.Fori(0, pairs) as pair:
                for i in range(2):
                    blk = pair * 2 + i
                    pool.wait_ge(S["yb_ok"], blk + 1)
                    pool.tensor_copy(ids[i][:], meta[:, bass.ds(blk, 1), NE:].rearrange("p o c -> p (o c)").bitcast(I32)).then_inc(S["ids_ok"], 1)
                    pool.wait_ge(S["ids_ok"], blk + 1)
                    wait_apart(pool, S["added"], blk * 16 + 16)
                    pool.indirect_dma_start(out=out, out_offset=bass.IndirectOffsetOnAxis(ap=ids[i][:].bitcast(U32), axis=0),
                                            in_=y_both[:, i, :], in_offset=None, compute_op=ALU.add).then_inc(S["added"], 16)


def expert_weights(gate_up, down):
    gu = gate_up.transpose(0, 2, 1).reshape(NE, KT, P, 2 * INTER).transpose(0, 2, 1, 3).reshape(NE, P, GU_COLS)
    dn = down.transpose(0, 2, 1)
    return np.concatenate([gu, dn[:, 0:P], np.concatenate([dn[:, P:], dn[:, P:]], axis=1)], axis=2)


def kernel(**inputs):
    import concourse.bacc as _bacc
    from concourse.bass_utils import run_bass_kernel_spmd as _run

    i = {k.replace("L0_", ""): np.asarray(v) for k, v in inputs.items()}
    tiles = lambda v: v.reshape(-1, P).T
    arrays = {
        "x": i["x"].reshape(NTOK, D),
        "ctx_t": i["ctx_1024"].transpose(0, 2, 1).reshape(NB * DM, T),
        "g_norm": tiles(i["attn_g_norm"]),
        "wq": i["attn_Wq"], "wkv": i["attn_Wkv"], "wout": i["attn_Wout"], "g_out": i["attn_g_out"],
        "w_in_t": i["xattn_in_proj_w"].T,
        "conv_w": i["xattn_conv_w"], "conv_b": tiles(i["xattn_conv_b"]),
        "w_x_t": i["xattn_x_proj_w"].T, "w_dt_t": i["xattn_dt_proj_w"].T, "dt_b": tiles(i["xattn_dt_proj_b"]),
        "a_log": i["xattn_A_log"].reshape(ET, P, DS).transpose(1, 2, 0), "d_skip": tiles(i["xattn_D"]),
        "w_gate_t": i["ffn_gate_weight"].T,
        "w_exp": expert_weights(i["ffn_gate_up_proj"], i["ffn_down_proj"]),
        "alpha": i["ffn_layer_alpha"].reshape(1),
        "const": constants(),
    }
    arrays = {k: np.ascontiguousarray(v) for k, v in arrays.items()}
    nc = _bacc.Bacc("TRN2", target_bir_lowering=False, num_devices=1)
    a = {k: nc.dram_tensor(f"in_{k}", v.shape, mybir.dt.from_np(v.dtype), kind="ExternalInput").ap() for k, v in arrays.items()}
    a["out"] = nc.dram_tensor("out_0", (NTOK + P, D), F32, kind="ExternalOutput").ap()
    decoder_layer(nc, a)
    res = _run(nc, [{f"in_{k}": v for k, v in arrays.items()}], core_ids=[0])
    return res.results[0]["out_0"][:NTOK].reshape(NB, T, D)
```
